# Optimizing a Trainium2 kernel written in Bass

```python
import numpy as np
import jax
import jax.numpy as jnp

def _softmax(x, axis=-1):
    return jax.nn.softmax(x, axis=axis)

def _gelu(x):
    return jax.nn.gelu(x, approximate=True)

def _silu(x):
    return jax.nn.silu(x)

def _sigmoid(x):
    return jax.nn.sigmoid(x)

def _layernorm(x, axis=-1, eps=1e-05):
    m = jnp.mean(x, axis=axis, keepdims=True)
    v = jnp.var(x, axis=axis, keepdims=True)
    return (x - m) / jnp.sqrt(v + eps)

def _scatter_add(tgt, idx, src, axis=0):
    return tgt.at[idx].add(src)

def _segment_sum(src, seg, n):
    return jax.ops.segment_sum(src, seg, n)
kernel_name = 'mk_gnn_preln_d4_gnn_r32_941f8b'

def setup_inputs(seed: int=0):
    np.random.seed(seed)
    _w = jnp.asarray

    def _rec_inputs():
        import jax
        import jax.numpy as jnp
        _gk = jax.random.key(seed)
        x = -0.0002117 + 1 * jax.random.normal(jax.random.fold_in(_gk, 1), (3125, 256), jnp.float32)
        _s = jax.random.randint(jax.random.fold_in(_gk, 2), (25000,), 0, 3125, jnp.int32)
        _d = jax.random.randint(jax.random.fold_in(_gk, 3), (25000,), 0, 3125, jnp.int32)
        _loop = jnp.arange(3125, dtype=jnp.int32)
        src = jnp.concatenate([_s, _d, _loop])
        dst = jnp.concatenate([_d, _s, _loop])
        _o = jnp.argsort(dst, stable=True)
        src = src[_o]
        dst = dst[_o]
        edge_attr3_1x1 = jax.random.uniform(jax.random.fold_in(_gk, 12), (53125, 1, 1), jnp.float32, 0.0, 0.999998)
        edge_attr_4 = 0.000126197 + 0.999763 * jax.random.normal(jax.random.fold_in(_gk, 13), (53125, 4), jnp.float32)
        edge_attr_8 = jax.random.uniform(jax.random.fold_in(_gk, 14), (53125, 8), jnp.float32, 0.0, 1)
        return (x, src, dst, edge_attr3_1x1, edge_attr_4, edge_attr_8)
    x, src, dst, edge_attr3_1x1, edge_attr_4, edge_attr_8 = _rec_inputs()

    def _L0_gnn_setup():
        import jax, jax.numpy as jnp
        import numpy as np
        N_NODES = 3125
        N_EDGES = 100000
        D = 256
        H = int(D ** 0.5)
        key = jax.random.key(seed)
        ks = jax.random.split(key, 8)
        x = jax.random.normal(ks[0], (N_NODES, D), dtype=jnp.float32)
        edge_index = jax.random.randint(ks[1], (2, N_EDGES), 0, N_NODES, dtype=jnp.int64)
        W1 = jax.random.normal(ks[2], (D, H), dtype=jnp.float32) / np.sqrt(D)
        b1 = jnp.zeros((H,), dtype=jnp.float32)
        W2 = jax.random.normal(ks[3], (H, H), dtype=jnp.float32) / np.sqrt(H)
        b2 = jnp.zeros((H,), dtype=jnp.float32)
        Wout = jax.random.normal(ks[4], (D, H), dtype=jnp.float32) / np.sqrt(H)
        bout = jnp.zeros((D,), dtype=jnp.float32)
        return {'x': x, 'edge_index': edge_index, 'W1': W1, 'b1': b1, 'W2': W2, 'b2': b2, 'Wout': Wout, 'bout': bout}
    _L0_gnn_all = _L0_gnn_setup()
    _L0_gnn_in = {k: v for k, v in _L0_gnn_all.items() if k in ('W1', 'b1', 'W2', 'b2', 'Wout', 'bout')}
    del _L0_gnn_all

    def _L1_gnn_setup():
        import jax, jax.numpy as jnp
        import numpy as np
        N_NODES = 625
        N_EDGES = 10000
        MUL = 64
        NUM_BASIS = 8
        INV_SQRT3 = 0.5773502691896258
        EPS = 1e-05
        key = jax.random.key(seed)
        k = jax.random.split(key, 16)
        return {'node_hiddens': jax.random.normal(k[0], (N_NODES, 4 * MUL), dtype=jnp.float32), 'edge_attr': jax.random.uniform(k[1], (N_EDGES, NUM_BASIS), dtype=jnp.float32), 'edge_sh': jax.random.normal(k[2], (N_EDGES, 4), dtype=jnp.float32), 'w1_s': jax.random.normal(k[3], (MUL, MUL), dtype=jnp.float32), 'w1_v': jax.random.normal(k[4], (MUL, MUL), dtype=jnp.float32), 'wsc_s': jax.random.normal(k[5], (MUL, MUL), dtype=jnp.float32), 'wsc_v': jax.random.normal(k[6], (MUL, MUL), dtype=jnp.float32), 'w2_s': jax.random.normal(k[7], (2 * MUL, MUL), dtype=jnp.float32), 'w2_v': jax.random.normal(k[8], (2 * MUL, MUL), dtype=jnp.float32), 'fc_w1': jax.random.normal(k[9], (NUM_BASIS, 64), dtype=jnp.float32), 'fc_w2': jax.random.normal(k[10], (64, 64), dtype=jnp.float32), 'fc_w3': jax.random.normal(k[11], (64, 4 * MUL), dtype=jnp.float32), 'g_s': jnp.ones((MUL,), dtype=jnp.float32), 'g_v': jnp.ones((MUL,), dtype=jnp.float32), 'edge_index': jax.random.randint(k[12], (2, N_EDGES), 0, N_NODES)}
    _L1_gnn_all = _L1_gnn_setup()
    _L1_gnn_in = {k: v for k, v in _L1_gnn_all.items() if k in ('w1_s', 'w1_v', 'wsc_s', 'wsc_v', 'w2_s', 'w2_v', 'fc_w1', 'fc_w2', 'fc_w3', 'g_s', 'g_v')}
    del _L1_gnn_all

    def _L2_gnn_setup():
        import jax, jax.numpy as jnp
        import numpy as np
        N_NODES = 50000
        N_EDGES = 25000
        IN_DIM = 256
        OUT_DIM = 64
        HEADS = 4
        NEG_SLOPE = 0.2
        LN_EPS = 1e-05
        key = jax.random.key(seed)
        ks = jax.random.split(key, 8)
        features = jax.random.normal(ks[0], (N_NODES, IN_DIM), dtype=jnp.float32)
        src = jax.random.randint(ks[1], (N_EDGES,), 0, N_NODES, dtype=jnp.int32)
        dst = jax.random.randint(ks[2], (N_EDGES,), 0, N_NODES, dtype=jnp.int32)
        W = jax.random.normal(ks[3], (IN_DIM, HEADS * OUT_DIM), dtype=jnp.float32) / np.sqrt(IN_DIM)
        attn_l = jax.random.normal(ks[4], (HEADS, OUT_DIM), dtype=jnp.float32) * 0.1
        attn_r = jax.random.normal(ks[5], (HEADS, OUT_DIM), dtype=jnp.float32) * 0.1
        bias = jnp.zeros((HEADS * OUT_DIM,), dtype=jnp.float32)
        gamma = jnp.ones((HEADS * OUT_DIM,), dtype=jnp.float32)
        beta = jnp.zeros((HEADS * OUT_DIM,), dtype=jnp.float32)
        return {'features': features, 'src': src, 'dst': dst, 'W': W, 'attn_l': attn_l, 'attn_r': attn_r, 'bias': bias, 'gamma': gamma, 'beta': beta}
    _L2_gnn_all = _L2_gnn_setup()
    _L2_gnn_in = {k: v for k, v in _L2_gnn_all.items() if k in ('W', 'attn_l', 'attn_r', 'bias', 'gamma', 'beta')}
    del _L2_gnn_all

    def _L3_gnn_setup():
        import jax, jax.numpy as jnp
        import numpy as np
        N, F_IN, H, OUT, E = (1000, 256, 4, 64, 16000)
        NEG_SLOPE = 0.2
        key = jax.random.key(seed)
        ks = jax.random.split(key, 7)
        return {'feat': jax.random.normal(ks[0], (N, F_IN), dtype=jnp.float32), 'dist': jax.random.uniform(ks[1], (E, 1, 1), dtype=jnp.float32), 'W': jax.random.normal(ks[2], (F_IN, H * OUT), dtype=jnp.float32) * (1.0 / np.sqrt(F_IN)), 'w_att_src': jax.random.normal(ks[3], (1, H, OUT), dtype=jnp.float32) * 0.1, 'w_att_dst': jax.random.normal(ks[4], (1, H, OUT), dtype=jnp.float32) * 0.1, 'src': jax.random.randint(ks[5], (E,), 0, N, dtype=jnp.int32), 'dst': jax.random.randint(ks[6], (E,), 0, N, dtype=jnp.int32)}
    _L3_gnn_all = _L3_gnn_setup()
    _L3_gnn_in = {k: v for k, v in _L3_gnn_all.items() if k in ('W', 'w_att_src', 'w_att_dst')}
    del _L3_gnn_all
    return {'x': x, 'src': src, 'dst': dst, 'edge_attr3_1x1': edge_attr3_1x1, 'edge_attr_4': edge_attr_4, 'edge_attr_8': edge_attr_8, 'L0_gnn_W1': _L0_gnn_in['W1'], 'L0_gnn_b1': _L0_gnn_in['b1'], 'L0_gnn_W2': _L0_gnn_in['W2'], 'L0_gnn_b2': _L0_gnn_in['b2'], 'L0_gnn_Wout': _L0_gnn_in['Wout'], 'L0_gnn_bout': _L0_gnn_in['bout'], 'L1_gnn_w1_s': _L1_gnn_in['w1_s'], 'L1_gnn_w1_v': _L1_gnn_in['w1_v'], 'L1_gnn_wsc_s': _L1_gnn_in['wsc_s'], 'L1_gnn_wsc_v': _L1_gnn_in['wsc_v'], 'L1_gnn_w2_s': _L1_gnn_in['w2_s'], 'L1_gnn_w2_v': _L1_gnn_in['w2_v'], 'L1_gnn_fc_w1': _L1_gnn_in['fc_w1'], 'L1_gnn_fc_w2': _L1_gnn_in['fc_w2'], 'L1_gnn_fc_w3': _L1_gnn_in['fc_w3'], 'L1_gnn_g_s': _L1_gnn_in['g_s'], 'L1_gnn_g_v': _L1_gnn_in['g_v'], 'L2_gnn_W': _L2_gnn_in['W'], 'L2_gnn_attn_l': _L2_gnn_in['attn_l'], 'L2_gnn_attn_r': _L2_gnn_in['attn_r'], 'L2_gnn_bias': _L2_gnn_in['bias'], 'L2_gnn_gamma': _L2_gnn_in['gamma'], 'L2_gnn_beta': _L2_gnn_in['beta'], 'L3_gnn_W': _L3_gnn_in['W'], 'L3_gnn_w_att_src': _L3_gnn_in['w_att_src'], 'L3_gnn_w_att_dst': _L3_gnn_in['w_att_dst']}

def reference(x, src, dst, edge_attr3_1x1, edge_attr_4, edge_attr_8, L0_gnn_W1, L0_gnn_b1, L0_gnn_W2, L0_gnn_b2, L0_gnn_Wout, L0_gnn_bout, L1_gnn_w1_s, L1_gnn_w1_v, L1_gnn_wsc_s, L1_gnn_wsc_v, L1_gnn_w2_s, L1_gnn_w2_v, L1_gnn_fc_w1, L1_gnn_fc_w2, L1_gnn_fc_w3, L1_gnn_g_s, L1_gnn_g_v, L2_gnn_W, L2_gnn_attn_l, L2_gnn_attn_r, L2_gnn_bias, L2_gnn_gamma, L2_gnn_beta, L3_gnn_W, L3_gnn_w_att_src, L3_gnn_w_att_dst):
    import jax
    import jax.numpy as jnp

    def _L0_gnn_ref(x, edge_index, W1, b1, W2, b2, Wout, bout):
        import jax, jax.numpy as jnp
        import numpy as np
        N_NODES = 3125
        N_EDGES = 100000
        D = 256
        H = int(D ** 0.5)
        N = x.shape[0]
        loops = jnp.arange(N, dtype=edge_index.dtype)
        src = jnp.concatenate([edge_index[0], loops])
        dst = jnp.concatenate([edge_index[1], loops])
        deg = jax.ops.segment_sum(jnp.ones_like(src, dtype=x.dtype), dst, num_segments=N)
        dinv = jnp.where(deg > 0, jax.lax.rsqrt(deg), 0.0)
        norm = dinv[src] * dinv[dst]

        def gcn_conv(h, W, b):
            h = h @ W
            msg = h[src] * norm[:, None]
            return jax.ops.segment_sum(msg, dst, num_segments=N) + b
        h = jax.nn.relu(gcn_conv(x, W1, b1))
        h = jax.nn.relu(gcn_conv(h, W2, b2))
        return jax.nn.sigmoid(h @ Wout.T + bout)

    def _L1_gnn_ref(node_hiddens, edge_attr, edge_sh, w1_s, w1_v, wsc_s, wsc_v, w2_s, w2_v, fc_w1, fc_w2, fc_w3, g_s, g_v, edge_index):
        import jax, jax.numpy as jnp
        import numpy as np
        N_NODES = 625
        N_EDGES = 10000
        MUL = 64
        NUM_BASIS = 8
        INV_SQRT3 = 0.5773502691896258
        EPS = 1e-05
        N = node_hiddens.shape[0]
        xs = node_hiddens[:, :MUL]
        xv = node_hiddens[:, MUL:].reshape(N, MUL, 3)
        h = jax.nn.silu(edge_attr @ fc_w1 * (1.0 / np.sqrt(float(NUM_BASIS))))
        h = jax.nn.silu(h @ fc_w2 * (1.0 / np.sqrt(64.0)))
        w = h @ fc_w3 * (1.0 / np.sqrt(64.0))
        wA, wB, wC, wD = jnp.split(w, 4, axis=1)
        inv = 1.0 / np.sqrt(float(MUL))
        sc_s = xs @ wsc_s * inv
        sc_v = jnp.einsum('nud,uv->nvd', xv, wsc_v) * inv
        ys = xs @ w1_s * inv
        yv = jnp.einsum('nud,uv->nvd', xv, w1_v) * inv
        src = edge_index[0]
        dst = edge_index[1]
        es = ys[dst]
        ev = yv[dst]
        sh0 = edge_sh[:, :1]
        sh1 = edge_sh[:, 1:]
        m0a = wA * es * sh0
        m0b = wD * jnp.einsum('eud,ed->eu', ev, sh1) * INV_SQRT3
        m1a = wB[:, :, None] * es[:, :, None] * sh1[:, None, :]
        m1b = wC[:, :, None] * ev * sh0[:, :, None]
        mid_s = jnp.concatenate([m0a, m0b], axis=1)
        mid_v = jnp.concatenate([m1a, m1b], axis=1)
        ns = jax.ops.segment_sum(mid_s, src, num_segments=N)
        nv = jax.ops.segment_sum(mid_v, src, num_segments=N)
        deg = jax.ops.segment_sum(jnp.ones((src.shape[0],), node_hiddens.dtype), src, num_segments=N)
        dn = jax.lax.rsqrt(jnp.maximum(deg, 1.0))
        ns = ns * dn[:, None]
        nv = nv * dn[:, None, None]
        inv2 = 1.0 / np.sqrt(2.0 * MUL)
        os_ = ns @ w2_s * inv2 + sc_s
        ov = jnp.einsum('nud,uv->nvd', nv, w2_v) * inv2 + sc_v
        os_ = os_ * jax.lax.rsqrt(jnp.mean(os_ * os_, axis=1, keepdims=True) + EPS) * g_s
        rms_v = jax.lax.rsqrt(jnp.mean(ov * ov, axis=(1, 2))[:, None, None] + EPS)
        ov = ov * rms_v * g_v[None, :, None]
        return jnp.concatenate([os_, ov.reshape(N, 3 * MUL)], axis=1)

    def _L2_gnn_ref(features, src, dst, W, attn_l, attn_r, bias, gamma, beta):
        import jax, jax.numpy as jnp
        import numpy as np
        N_NODES = 50000
        N_EDGES = 25000
        IN_DIM = 256
        OUT_DIM = 64
        HEADS = 4
        NEG_SLOPE = 0.2
        LN_EPS = 1e-05
        N = features.shape[0]
        H, D = attn_l.shape
        feat = (features @ W).reshape(N, H, D)
        el = jnp.einsum('nhd,hd->nh', feat, attn_l)
        er = jnp.einsum('nhd,hd->nh', feat, attn_r)
        e = jax.nn.leaky_relu(el[src] + er[dst], NEG_SLOPE)
        emax = jax.ops.segment_max(e, dst, num_segments=N)
        emax = jnp.where(jnp.isfinite(emax), emax, 0.0)
        ex = jnp.exp(e - emax[dst])
        denom = jax.ops.segment_sum(ex, dst, num_segments=N)
        alpha = ex / jnp.maximum(denom[dst], 1e-09)
        msg = feat[src] * alpha[:, :, None]
        rst = jax.ops.segment_sum(msg, dst, num_segments=N)
        x = jax.nn.relu(rst.reshape(N, H * D) + bias)
        mu = jnp.mean(x, axis=-1, keepdims=True)
        var = jnp.mean((x - mu) ** 2, axis=-1, keepdims=True)
        return (x - mu) * jax.lax.rsqrt(var + LN_EPS) * gamma + beta

    def _L3_gnn_ref(feat, dist, W, w_att_src, w_att_dst, src, dst):
        import jax, jax.numpy as jnp
        import numpy as np
        N, F_IN, H, OUT, E = (1000, 256, 4, 64, 16000)
        NEG_SLOPE = 0.2
        n = feat.shape[0]
        ft = (feat @ W).reshape(n, H, OUT)
        e_src = jnp.sum(ft * w_att_src, axis=-1, keepdims=True)
        e_dst = jnp.sum(ft * w_att_dst, axis=-1, keepdims=True)
        e = e_src[src] + e_dst[dst]
        e = jnp.where(e >= 0, e, NEG_SLOPE * e)
        emax = jax.ops.segment_max(e, dst, num_segments=n)
        ex = jnp.exp(e - emax[dst])
        denom = jax.ops.segment_sum(ex, dst, num_segments=n)
        a = ex / denom[dst] * dist
        m = ft[src] * a
        out = jax.ops.segment_sum(m, dst, num_segments=n)
        return out.reshape(n, H * OUT)
    edge_index = jnp.stack([src, dst])
    h = jnp.maximum(_layernorm(x, axis=-1), 0.0)
    x = x + _L0_gnn_ref(h, edge_index, L0_gnn_W1, L0_gnn_b1, L0_gnn_W2, L0_gnn_b2, L0_gnn_Wout, L0_gnn_bout)
    h = jnp.maximum(_layernorm(x, axis=-1), 0.0)
    x = x + _L1_gnn_ref(h, edge_attr_8, edge_attr_4, L1_gnn_w1_s, L1_gnn_w1_v, L1_gnn_wsc_s, L1_gnn_wsc_v, L1_gnn_w2_s, L1_gnn_w2_v, L1_gnn_fc_w1, L1_gnn_fc_w2, L1_gnn_fc_w3, L1_gnn_g_s, L1_gnn_g_v, edge_index)
    h = jnp.maximum(_layernorm(x, axis=-1), 0.0)
    x = x + _L2_gnn_ref(h, src, dst, L2_gnn_W, L2_gnn_attn_l, L2_gnn_attn_r, L2_gnn_bias, L2_gnn_gamma, L2_gnn_beta)
    h = jnp.maximum(_layernorm(x, axis=-1), 0.0)
    x = x + _L3_gnn_ref(h, edge_attr3_1x1, L3_gnn_W, L3_gnn_w_att_src, L3_gnn_w_att_dst, src, dst)
    return x

_drawn_inputs = setup_inputs


def setup_inputs(seed=0):
    import zlib

    import numpy as np

    out = dict(_drawn_inputs(seed))
    spreads = {'L0_gnn_b1': (0.0, 0.8),
     'L0_gnn_b2': (0.0, 0.365),
     'L0_gnn_bout': (0.0, 0.302),
     'L1_gnn_g_s': (1.0, 0.2),
     'L1_gnn_g_v': (1.0, 0.2),
     'L2_gnn_bias': (0.0, 0.1),
     'L2_gnn_gamma': (1.0, 0.2),
     'L2_gnn_beta': (0.0, 0.1)}
    factors = {'L0_gnn_W1': 3.26, 'L3_gnn_w_att_src': 4.267, 'L3_gnn_w_att_dst': 8.0}
    for name, (base, spread) in spreads.items():
        noise = np.random.default_rng([zlib.crc32(name.encode()), seed]).standard_normal(out[name].shape)
        drawn = base * np.exp(spread * noise) if base else spread * noise
        out[name] = jnp.asarray(drawn.astype(out[name].dtype))
    for name, factor in factors.items():
        out[name] = (out[name] * factor).astype(out[name].dtype)
    return out
```

```python
from contextlib import ExitStack

import concourse.bass as bass
from concourse import mybir

F32 = mybir.dt.float32
BF16 = mybir.dt.bfloat16
I32 = mybir.dt.int32
U32 = mybir.dt.uint32
ALU = mybir.AluOpType
ACT = mybir.ActivationFunctionType
AX = mybir.AxisListType

P = 128
N = 3125
D = 256
E = 53125
T = -(-N // P)
NP = T * P
C = -(-E // P)
EP = C * P
LASTROW = E - (P - 1) * C
Q = C + T - 1
PAD = NP - 1
QB = 4
QP = Q // QB
CB = 4
CP = C // CB
H = 16
MUL = 64
HEADS = 4
RS = 16
RD = 4
BIG = 1.0e30
FAR = 8192.0
B = 4
EPS = 1e-5


class Steps:

    def __init__(self, sem):
        self.sem, self.n, self.loop = sem, 0, None

    def on(self, eng):
        self.eng = eng
        return self

    def __call__(self, ins):
        ins.then_inc(self.sem, 1)
        self.n += 1
        if self.loop is None:
            self.eng.wait_ge(self.sem, self.n)
        else:
            i, per = self.loop
            self.eng.wait_ge(self.sem, i * per + self.n)

    def run(self, n, body):
        start = self.n
        body(0)
        per = self.n - start
        with self.eng.Fori(1, n, 1) as i:
            self.n, self.loop = start, (i, per)
            body(i)
        self.n, self.loop = start + per * n, None

    def run_ahead(self, n, body):
        start = self.n
        body(0, False)
        per = self.n - start
        with self.eng.Fori(1, n - 1, 1) as i:
            self.n, self.loop = start, (i, per)
            body(i, False)
        self.n, self.loop = start + per * (n - 1), None
        body(n - 1, True)


class Group:

    def __init__(self, i, ng, c):
        self.i, self.ng, self.off, self.slot = i, ng, c // ng, c % ng

    def at(self, per=1, more=0):
        return self.i * (self.ng * per) + ((self.off * self.ng + self.slot) * per + more)

    def lap(self, per=1, more=0):
        return self.i * per + (self.off * per + more)

    def first(self):
        return isinstance(self.i, int) and self.at() == 0


def need(eng, semaphore, value):
    if not isinstance(value, int) or value > 0:
        eng.wait_ge(semaphore, value)


def groups(eng, n, ng, stages, head=None):
    def turn(i, slots):
        for s in slots:
            if head is not None and s == slots[0]:
                head(i, s)
            for lag, step in stages:
                g = Group(i, ng, s - lag)
                if not isinstance(i, int) or 0 <= g.at() < n:
                    step(g)
    for i in range(2):
        turn(i, range(ng))
    with eng.Fori(2, n // ng, 1) as i:
        turn(i, range(ng))
    most = max(lag for lag, _ in stages) + n % ng
    if most:
        turn(n // ng, range(most))


class Links:

    def __init__(self, eng, semaphore, per):
        self.eng, self.sem, self.per = eng, semaphore, per

    def start(self, g):
        self.g, self.k = g, 0
        return self

    def __call__(self, ins):
        self.k += 1
        assert self.k <= self.per
        ins.then_inc(self.sem, 1)
        self.eng.wait_ge(self.sem, self.g.at(self.per, self.k))


def later(i):
    return not (isinstance(i, int) and i == 0)


def gnn(nc, A, out, stop=99):
    with ExitStack() as ctx:
        def sb(name, shape, dt=F32, scope=ctx):
            return scope.enter_context(nc.sbuf_tensor(name, shape, dt))

        def ps(name, shape, dt=F32, scope=ctx):
            return scope.enter_context(nc.psum_tensor(name, shape, dt))

        def bank(name, scope, inner=None, dt=F32):
            b = scope.enter_context(nc.psum_tensor(name, [P, 2048 // (4 if dt == F32 else 2)], dt))
            return b[:] if inner is None else b[:].rearrange("p (n m) -> p n m", m=inner)

        def pair_tiles(k, engine, ng, tiles_of):
            def load(i, s):
                start, n = i * (ng * B) - B, ng * B
                if isinstance(i, int):
                    start, n = max(start, 0), min(n if i else n - B, Q - max(start, 0))
                _, ts = nc.values_load_multi_w_load_instructions(
                    toff[k][0:1, bass.ds(start, n)], engines=(engine,), min_val=0, max_val=T - 1,
                    skip_runtime_bounds_check_because="a pair's tile is one of the T tiles")
                first = 0 if isinstance(i, int) and i == 0 else -B
                for r in range(n):
                    tiles_of[(first + r) % (ng * B)] = ts[r]
            return load

        stage_sems = []

        def sem(name):
            stage_sems.append(nc.alloc_semaphore(name=name))
            return stage_sems[-1]

        def free_sems():
            with nc.Block() as block:
                @block.gpsimd
                def _(pool):
                    nc.clear_and_free_semaphores(stage_sems)
            stage_sems.clear()

        def dram(name, shape, dt=F32):
            return nc.dram_tensor(name, shape, dt, kind="Internal").ap()

        rec_s = dram("rec_s", (EP, RS))
        rec_d = dram("rec_d", (EP, RD))
        tab16 = [dram("tab16a", (NP, H)), dram("tab16b", (NP, H))]
        taby = dram("taby", (NP, D))
        tabf = [dram("tabf2", (NP, D)), dram("tabf3", (NP, D))]
        tabe = [dram("tabe2", (NP, HEADS)), dram("tabe3", (NP, HEADS))]

        dve_step, act_step, pe_step, pool_step = [
            Steps(ctx.enter_context(nc.semaphore(f"{e}_step"))) for e in ("dve", "act", "pe", "pool")]
        parked = ctx.enter_context(nc.semaphore("parked"))

        def hold(eng):
            eng.sem_inc(parked, 1)

        X = sb("X", [P, T, D])
        ident = sb("ident", [P, P])
        identb = sb("identb", [P, P], BF16)
        ones = sb("ones", [P, P])
        icol = sb("icol", [P, Q])
        tri = sb("tri", [P, B, P], BF16)
        lower = sb("lower", [P, P])
        degs = {k: sb(f"deg_{k}", [P, T]) for k in "sd"}
        dinv = sb("dinv", [P, T])
        dn = sb("dn", [P, T])
        toff = {k: sb(f"toff_{k}", [P, Q], I32) for k in "sd"}
        keyl = {k: sb(f"keyl_{k}", [P, Q]) for k in "sd"}
        S_idx = sb("S_idx", [P, Q], U32)
        S_attr = sb("S_attr", [P, Q, 12])
        D_idx = sb("D_idx", [P, Q], U32)
        D_dist = sb("D_dist", [P, Q])
        D_key = sb("D_key", [P, Q])
        src_i = sb("src_i", [P, C], I32)
        dst_i = sb("dst_i", [P, C], I32)
        fl = {k: {n: sb(f"{n}_{k}", [P, C]) for n in ("key", "lo", "hi")} for k in "sd"}

        ld = sem("ld")
        filled = sem("filled")
        made = sem("made")
        with ExitStack() as scope:
            ti = sb("ti", [P, C], I32, scope)
            ii = sb("ii", [P, Q], I32, scope)
            ip = sb("ip", [P, P], I32, scope)
            ipf = sb("ipf", [P, P], F32, scope)
            with nc.Block() as block:
                @block.sync
                def _(sp):
                    sp.wait_ge(filled, 3)
                    for a, b in ((A["src"], src_i), (A["dst"], dst_i)):
                        sp.dma_start(b[0:P - 1, :], a[0:(P - 1) * C].rearrange("(p c) -> p c", c=C)).then_inc(ld, 16)
                        sp.dma_start(b[P - 1:P, 0:LASTROW], a[(P - 1) * C:E].rearrange("(p c) -> p c", p=1)).then_inc(ld, 16)
                    last = N - (T - 1) * P
                    sp.dma_start(X[:, 0:T - 1, :], A["x"][0:(T - 1) * P, :].rearrange("(t p) d -> p t d", p=P)).then_inc(ld, 16)
                    sp.dma_start(X[0:last, T - 1, :], A["x"][(T - 1) * P:N, :]).then_inc(ld, 16)

                @block.gpsimd
                def _(pool):
                    nc.gpsimd.iota(ii[:], pattern=[[1, Q]], base=0, channel_multiplier=0).then_inc(made, 1)
                    nc.gpsimd.iota(ip[:], pattern=[[0, P]], base=0, channel_multiplier=1).then_inc(made, 1)

                @block.vector
                def _(dve):
                    link = dve_step.on(dve)
                    nc.vector.memset(src_i[:], PAD).then_inc(filled, 1)
                    nc.vector.memset(dst_i[:], PAD).then_inc(filled, 1)
                    nc.vector.memset(X[:, T - 1, :], 0.0).then_inc(filled, 1)
                    nc.vector.memset(ones[:], 1.0)
                    dve.wait_ge(made, 2)
                    link(nc.vector.tensor_copy(icol[:], ii[:]))
                    link(nc.vector.tensor_copy(ipf[:], ip[:]))
                    link(nc.vector.tensor_tensor(ident[:], icol[:, 0:P], ipf[:], ALU.is_equal))
                    link(nc.vector.tensor_copy(identb[:], ident[:]))
                    link(nc.vector.tensor_tensor(lower[:], icol[:, 0:P], ipf[:], ALU.is_gt))
                    for b in range(B):
                        link(nc.vector.tensor_tensor(tri[:, b, :], icol[:, 0:P], ipf[:], ALU.is_ge))
                    link(nc.vector.tensor_scalar(tri[:], tri[:], FAR, None, ALU.mult))
                    dve.wait_ge(ld, 96)
                    for k, a in (("s", src_i), ("d", dst_i)):
                        f = fl[k]
                        link(nc.vector.tensor_copy(f["key"][:], a[:]))
                        link(nc.vector.tensor_scalar(ti[:], a[:], 7, None, ALU.logical_shift_right))
                        link(nc.vector.tensor_copy(f["hi"][:], ti[:]))
                        link(nc.vector.scalar_tensor_tensor(out=f["lo"][:], in0=f["hi"][:], scalar=-float(P),
                                                            in1=f["key"][:], op0=ALU.mult, op1=ALU.add))

        def bc(ap, n):
            return ap.unsqueeze(2).to_broadcast([ap.shape[0], ap.shape[1], n])

        def rows(ap, n):
            return ap.unsqueeze(1).to_broadcast([ap.shape[0], n, ap.shape[1]])

        def sort(k, scope):
            f = fl[k]
            W, rec = (RS, rec_s) if k == "s" else (RD, rec_d)
            HH = sb(f"HH{k}", [P, T, C + 1], F32, scope)
            R = sb(f"R{k}", [P, C, W], F32, scope)
            ohlo = sb(f"ohlo{k}", [P, 2, B, P], BF16, scope)
            ohhi = sb(f"ohhi{k}", [P, 2, B, T], F32, scope)
            ohhb = sb(f"ohhb{k}", [P, 2, B, T], BF16, scope)
            base = sb(f"base{k}", [P, 3, T], F32, scope)
            onesc = sb(f"onesc{k}", [P, C + 1], F32, scope)
            raw = sb(f"raw{k}", [P, C, 8], F32, scope) if k == "s" else None
            raw2 = sb(f"raw2{k}", [P, C, 4 if k == "s" else 1], F32, scope)
            banks = ExitStack()
            hp = [bank(f"hp{k}{h}", banks, 32) for h in range(2)]
            oh_ready = [sem(f"oh_ready{k}{h}") for h in range(2)]
            cnt_ready = [sem(f"cnt_ready{k}{h}") for h in range(2)]
            cnt_kept = [sem(f"cnt_kept{k}{h}") for h in range(2)]
            rl, rf = sem(f"rec_loaded{k}"), sem(f"rec_filled{k}")

            with nc.Block() as block:
                @block.sync
                def _(sp):
                    sp.wait_ge(rf, 2 if k == "s" else 1)
                    for a, b in ([(A["edge_attr_8"], raw), (A["edge_attr_4"], raw2)] if k == "s"
                                 else [(A["edge_attr3_1x1"].rearrange("e a b -> e (a b)"), raw2)]):
                        sp.dma_start(b[0:P - 1, :, :], a[0:(P - 1) * C, :].rearrange("(p c) f -> p c f", c=C)).then_inc(rl, 16)
                        sp.dma_start(b[P - 1:P, 0:LASTROW, :], a[(P - 1) * C:E, :].rearrange("(p c) f -> p c f", p=1)).then_inc(rl, 16)

                @block.vector
                def _(dve):
                    link = dve_step.on(dve)
                    nc.vector.memset(raw2[:], 0.0).then_inc(rf, 1)
                    if k == "s":
                        nc.vector.memset(raw[:], 0.0).then_inc(rf, 1)
                    link(nc.vector.memset(onesc[:], 1.0))
                    link(nc.vector.memset(R[:], 0.0))

                    def body(i):
                        for h in range(2):
                            if later(i):
                                dve.wait_ge(cnt_ready[h], i)
                            at = bass.ds(i * (2 * B) + h * B, B)
                            nc.vector.tensor_tensor(ohlo[:, h], rows(icol[:, 0:P], B), bc(f["lo"][:, at], P),
                                                    ALU.is_equal).then_inc(oh_ready[h], 1)
                            nc.vector.tensor_tensor(ohhb[:, h], rows(icol[:, 0:T], B), bc(f["hi"][:, at], T),
                                                    ALU.is_equal).then_inc(oh_ready[h], 1)
                    dve_step.run(C // (2 * B), body)
                    dve.wait_ge(rl, 64 if k == "s" else 32)
                    if k == "s":
                        link(nc.vector.tensor_copy(R[:, :, 0:8], raw[:]))
                        link(nc.vector.tensor_copy(R[:, :, 8:12], raw2[:]))
                        link(nc.vector.tensor_copy(R[:, :, 12], fl["d"]["key"][:]))
                        link(nc.vector.tensor_copy(R[:, :, 13], fl["s"]["key"][:]))
                    else:
                        link(nc.vector.tensor_copy(R[:, :, 0], fl["s"]["key"][:]))
                        link(nc.vector.tensor_copy(R[:, :, 1], fl["d"]["key"][:]))
                        link(nc.vector.tensor_copy(R[:, :, 2], raw2[:, :, 0]))

                @block.tensor
                def _(pe):
                    pe_step.on(pe)

                    def body(i):
                        for h in range(2):
                            pe.wait_ge(oh_ready[h], i * 2 + 2)
                            if later(i):
                                pe.wait_ge(cnt_kept[h], i)
                            for b in range(B):
                                mm = nc.tensor.matmul(hp[h][:, b, 0:T], lhsT=ohlo[:, h, b, :], rhs=ohhb[:, h, b, :],
                                                      start=True, stop=True)
                            mm.then_inc(cnt_ready[h], 1)
                    pe_step.run(C // (2 * B), body)

                @block.scalar
                def _(act):
                    act_step.on(act)

                    def body(i):
                        for h in range(2):
                            act.wait_ge(cnt_ready[h], i + 1)
                            hold(act)
                            nc.scalar.copy(HH[:, :, bass.ds(i * (2 * B) + h * B + 1, B)],
                                           hp[h][:, 0:B, 0:T].rearrange("p b t -> p t b")).then_inc(cnt_kept[h], 1)
                    act_step.run(C // (2 * B), body)

            banks.close()
            tot = [bank(f"tot{k}{n}", scope)[:, 0:T] for n in range(2)]
            totals, summed = sem(f"totals{k}"), sem(f"summed{k}")
            with nc.Block() as block:
                @block.vector
                def _(dve):
                    link = dve_step.on(dve)
                    nc.vector.tensor_reduce(degs[k][:], HH[:, :, 1:C + 1], AX.X, ALU.add).then_inc(totals, 1)
                    dve.wait_ge(summed, 2)
                    link(nc.vector.tensor_copy(base[:, 0, :], tot[1]))
                    link(nc.vector.tensor_tensor_scan(base[:, 1, :], onesc[:, 0:T], base[:, 0, :], 0.0, ALU.mult, ALU.add))
                    link(nc.vector.tensor_tensor(base[:, 2, :], base[:, 1, :], base[:, 0, :], ALU.subtract))
                    link(nc.vector.tensor_tensor(HH[:, :, 0], base[:, 2, :], tot[0], ALU.add))

                    def body(i):
                        row = HH[:, bass.ds(i, 1), :].rearrange("p o c -> p (o c)")
                        link(nc.vector.tensor_tensor_scan(row, onesc[:], row, 0.0, ALU.mult, ALU.add))
                    dve_step.run(T, body)

                @block.tensor
                def _(pe):
                    pe.wait_ge(totals, 1)
                    nc.tensor.matmul(tot[0], lhsT=lower[:], rhs=degs[k][:], start=True, stop=True).then_inc(summed, 1)
                    nc.tensor.matmul(tot[1], lhsT=ones[:], rhs=degs[k][:], start=True, stop=True).then_inc(summed, 1)

            dk = sb(f"dk{k}", [P, 2, B, P], F32, scope)
            eq = sb(f"eq{k}", [P, 2, B, P], F32, scope)
            ohT = sb(f"ohT{k}", [P, 2, B, P], F32, scope)
            pr = sb(f"pr{k}", [P, 2, B, T], F32, scope)
            rk = sb(f"rk{k}", [P, 2, 2, B], F32, scope)
            pos = sb(f"pos{k}", [P, 2, B], U32, scope)
            rst = sb(f"rst{k}", [P, 2, B, W], F32, scope)
            kr = [bank(f"kr{k}{h}", scope, P) for h in range(2)]
            tp = [bank(f"tpb{k}{h}", scope, P, BF16)[:, 0:B] for h in range(2)]
            Rp = [bank(f"Rp{k}{h}", scope, 32) for h in range(2)]
            hot = [sem(f"hot{k}{h}") for h in range(2)]
            keyrow = [sem(f"keyrow{k}{h}") for h in range(2)]
            turned = [sem(f"turned{k}{h}") for h in range(2)]
            hotT = [sem(f"hotT{k}{h}") for h in range(2)]
            found = [sem(f"found{k}{h}") for h in range(2)]
            placed = [sem(f"placed{k}{h}") for h in range(2)]
            staged = [sem(f"staged{k}{h}") for h in range(2)]
            landed = [sem(f"landed{k}{h}") for h in range(2)]
            with nc.Block() as block:
                @block.vector
                def _(dve):
                    link = dve_step.on(dve)

                    def one_hots(i, h):
                        at = bass.ds(i * (2 * B) + h * B, B)
                        nc.vector.tensor_tensor(ohlo[:, h], rows(icol[:, 0:P], B), bc(f["lo"][:, at], P),
                                                ALU.is_equal).then_inc(hot[h], 1)
                        nc.vector.tensor_tensor(dk[:, h], rows(ident[:], B), bc(f["key"][:, at], P),
                                                ALU.mult).then_inc(hot[h], 1)
                        nc.vector.tensor_tensor(ohhi[:, h], rows(icol[:, 0:T], B), bc(f["hi"][:, at], T),
                                                ALU.is_equal).then_inc(hot[h], 1)

                    def places(i, h):
                        at = bass.ds(i * (2 * B) + h * B, B)
                        dve.wait_ge(keyrow[h], i + 1)
                        link(nc.vector.tensor_tensor(eq[:, h], kr[h], bc(f["key"][:, at], P), ALU.is_equal))
                        link(nc.vector.tensor_reduce(rk[:, h, 0], eq[:, h], AX.X, ALU.add))
                        dve.wait_ge(found[h], i + 1)
                        link(nc.vector.tensor_tensor(pr[:, h], Rp[h][:, 0:B, 0:T], ohhi[:, h], ALU.mult))
                        link(nc.vector.tensor_reduce(rk[:, h, 1], pr[:, h], AX.X, ALU.add))
                        if later(i):
                            dve.wait_ge(landed[h], i * (16 * B))
                        nc.vector.tensor_tensor(pos[:, h], rk[:, h, 0], rk[:, h, 1], ALU.add).then_inc(placed[h], 1)

                    def body(i):
                        for h in range(2):
                            if later(i):
                                dve.wait_ge(placed[h], i)
                            one_hots(i, h)
                        for h in range(2):
                            places(i, h)
                    dve_step.run(C // (2 * B), body)

                @block.tensor
                def _(pe):
                    pe_step.on(pe)

                    def body(i):
                        for h in range(2):
                            pe.wait_ge(hot[h], i * 3 + 3)
                            if later(i):
                                pe.wait_ge(placed[h], i)
                            nc.tensor.matmul(kr[h].rearrange("p b m -> p (b m)"), lhsT=ones[:],
                                             rhs=dk[:, h].rearrange("p b m -> p (b m)"), start=True, stop=False)
                            nc.tensor.matmul(kr[h].rearrange("p b m -> p (b m)"), lhsT=identb[:],
                                             rhs=tri[:].rearrange("p b m -> p (b m)"), start=False,
                                             stop=True).then_inc(keyrow[h], 1)
                            for b in range(B):
                                mm = nc.tensor.transpose(tp[h][:, b, :], ohlo[:, h, b, :], identb[:])
                            mm.then_inc(turned[h], 1)
                        for h in range(2):
                            pe.wait_ge(hotT[h], i + 1)
                            hold(pe)
                            for b in range(B):
                                c = i * (2 * B) + (h * B + b)
                                mm = nc.tensor.matmul(Rp[h][:, b, 0:T], lhsT=ohT[:, h, b, :],
                                                      rhs=HH[:, :, bass.ds(c, 1)].rearrange("p t o -> p (t o)"),
                                                      start=True, stop=True)
                            mm.then_inc(found[h], 1)
                    pe_step.run(C // (2 * B), body)

                @block.scalar
                def _(act):
                    act_step.on(act)

                    def body(i):
                        for h in range(2):
                            act.wait_ge(turned[h], i + 1)
                            nc.scalar.copy(ohT[:, h], tp[h]).then_inc(hotT[h], 1)
                            if later(i):
                                act.wait_ge(landed[h], i * (16 * B))
                                hold(act)
                            nc.scalar.copy(rst[:, h], R[:, bass.ds(i * (2 * B) + h * B, B), :]).then_inc(staged[h], 1)
                    act_step.run(C // (2 * B), body)

                @block.gpsimd
                def _(pool):
                    pool_step.on(pool)

                    def body(i):
                        for h in range(2):
                            pool.wait_ge(placed[h], i + 1)
                            pool.wait_ge(staged[h], i + 1)
                            hold(pool)
                            for b in range(B):
                                nc.gpsimd.indirect_dma_start(
                                    rec[:, :], bass.IndirectOffsetOnAxis(ap=pos[:, h, b:b + 1], axis=0),
                                    rst[:, h, b, :], None).then_inc(landed[h], 16)
                    pool_step.run(C // (2 * B), body)
                    for h in range(2):
                        pool.wait_ge(landed[h], 16 * B * (C // (2 * B)))

        for k in "sd":
            if stop >= 1:
                with ExitStack() as scope:
                    sort(k, scope)

        def pairs(k, scope):
            W, rec, kc = (RS, rec_s, 13) if k == "s" else (RD, rec_d, 1)
            lastk = sb(f"lastk{k}", [CP, CB], F32, scope)
            li = sb(f"li{k}", [CP, CB], I32, scope)
            ci = sb(f"ci{k}", [CP, CB], I32, scope)
            v = sb(f"v{k}", [CP, 3, CB], F32, scope)
            cmp = sb(f"cmp{k}", [CP, CB, Q], F32, scope)
            cq = sb(f"cq{k}", [P, Q], F32, scope)
            cidx = sb(f"cidx{k}", [QP, QB], U32, scope)
            TX = sb(f"TX{k}", [QP, QB, P, W], F32, scope)
            cqp = bank(f"cqp{k}", scope)[:, 0:Q]
            cqi = bank(f"cqi{k}", scope)[0:QP, 0:QB]
            tq = [bank(f"tq{k}{n}", scope)[:, 0:Q] for n in range(2)]
            got, iot, cmpd, cnt, ci_ok, rows_in = [sem(f"{n}{k}") for n in ("got", "iot", "cmpd", "cnt", "ci_ok", "rows_in")]
            fields = ([(c, S_attr[:, :, c]) for c in range(12)] + [(12, S_idx[:]), (13, None)]) if k == "s" \
                else [(0, D_idx[:]), (1, None), (2, D_dist[:])]
            turned, taken = sem(f"fturned{k}"), sem(f"ftaken{k}")
            with nc.Block() as block:
                @block.sync
                def _(sp):
                    last = rec.rearrange("(b p e) f -> p b e f", b=CB, p=CP)
                    for b in range(CB):
                        sp.dma_start(lastk[:, b:b + 1], last[:, b, P - 1, kc:kc + 1],
                                     allow_slow_non_contiguous=True).then_inc(got, 16)

                @block.gpsimd
                def _(pool):
                    nc.gpsimd.iota(ci[:], pattern=[[CP, CB]], base=0, channel_multiplier=1).then_inc(iot, 1)
                    pool.wait_ge(ci_ok, 1)
                    for b in range(QB):
                        nc.gpsimd.indirect_dma_start(
                            TX[:, b].rearrange("p e f -> p (e f)"), None,
                            rec.rearrange("(c e) f -> c (e f)", e=P),
                            bass.IndirectOffsetOnAxis(ap=cidx[:, b:b + 1], axis=0)).then_inc(rows_in, 16)
                    pool.wait_ge(rows_in, 16 * QB)

                @block.vector
                def _(dve):
                    link = dve_step.on(dve)
                    dve.wait_ge(got, 16 * CB)
                    dve.wait_ge(iot, 1)
                    link(nc.vector.tensor_copy(li[:], lastk[:]))
                    link(nc.vector.tensor_scalar(li[:], li[:], 7, None, ALU.logical_shift_right))
                    link(nc.vector.tensor_copy(v[:, 0], li[:]))
                    link(nc.vector.tensor_copy(v[:, 1], ci[:]))
                    link(nc.vector.tensor_tensor(v[:, 2], v[:, 0], v[:, 1], ALU.add))
                    for b in range(CB):
                        nc.vector.tensor_scalar(cmp[:, b], icol[0:CP, :], v[:, 2, b:b + 1], None,
                                                ALU.is_gt).then_inc(cmpd, 1)
                    dve.wait_ge(cnt, 2)
                    nc.vector.tensor_copy(cidx[:], cqi).then_inc(ci_ok, 1)
                    link(nc.vector.tensor_copy(cq[:], cqp))
                    link(nc.vector.tensor_tensor(cq[:], icol[:], cq[:], ALU.subtract))
                    link(nc.vector.tensor_copy(toff[k][:], cq[:]))
                    for n, (c, dest) in enumerate(fields):
                        dve.wait_ge(turned, n + 1)
                        if dest is None:
                            if k == "d":
                                link(nc.vector.tensor_copy(D_key[:], tq[n % 2]))
                            nc.vector.scalar_tensor_tensor(out=keyl[k][:], in0=cq[:], scalar=-float(P),
                                                           in1=tq[n % 2], op0=ALU.mult, op1=ALU.add).then_inc(taken, 1)
                        else:
                            nc.vector.tensor_copy(dest, tq[n % 2]).then_inc(taken, 1)

                @block.tensor
                def _(pe):
                    pe.wait_ge(cmpd, CB)
                    for b in range(CB):
                        mm = nc.tensor.matmul(cqp, lhsT=ones[0:CP, :], rhs=cmp[:, b], start=(b == 0), stop=(b == CB - 1))
                    mm.then_inc(cnt, 1)
                    for j in range(QB):
                        for b in range(CB):
                            mm = nc.tensor.matmul(cqi[:, j:j + 1], lhsT=cmp[:, b, j * QP:(j + 1) * QP],
                                                  rhs=ones[0:CP, 0:1], start=(b == 0), stop=(b == CB - 1))
                    mm.then_inc(cnt, 1)
                    pe.wait_ge(rows_in, 16 * QB)
                    for n, (c, dest) in enumerate(fields):
                        if n >= 2:
                            pe.wait_ge(taken, n - 1)
                        for j in range(QB):
                            mm = nc.tensor.transpose(tq[n % 2][:, j * QP:(j + 1) * QP], TX[:, j, :, c],
                                                     ident[0:QP, 0:QP])
                        mm.then_inc(turned, 1)

        for k in "sd":
            if stop >= 2:
                with ExitStack() as scope:
                    pairs(k, scope)

        def layernorm_stats(dve, link, st, m, var_ready, rstd_ready, X=X):
            def body(t):
                link(nc.vector.bn_stats(st[:, bass.ds(t, 1), :].rearrange("p o s -> p (o s)"),
                                        X[:, bass.ds(t, 1), :].rearrange("p o d -> p (o d)")))
            dve_step.run(T, body)
            tt = nc.vector.tensor_tensor
            link(tt(m[:, 2], st[:, :, 1], st[:, :, 4], ALU.subtract))
            link(tt(m[:, 2], m[:, 2], m[:, 2], ALU.mult))
            link(tt(m[:, 3], st[:, :, 2], st[:, :, 5], ALU.add))
            link(nc.vector.tensor_scalar(m[:, 3], m[:, 3], 1.0 / D, None, ALU.mult))
            link(nc.vector.scalar_tensor_tensor(out=m[:, 3], in0=m[:, 2], scalar=0.25, in1=m[:, 3],
                                                op0=ALU.mult, op1=ALU.add))
            nc.vector.tensor_scalar(m[:, 3], m[:, 3], EPS, None, ALU.add).then_inc(var_ready, 1)
            link(tt(m[:, 4], st[:, :, 1], st[:, :, 4], ALU.add))
            dve.wait_ge(rstd_ready, 1)
            link(nc.vector.reciprocal(m[:, 0], m[:, 3]))
            link(nc.vector.scalar_tensor_tensor(out=m[:, 1], in0=m[:, 4], scalar=-0.5, in1=m[:, 0],
                                                op0=ALU.mult, op1=ALU.mult))

        TB = 5

        def tiles(name, fill, K, turns, project, post, before=None, after=None, loads=None, norm=False, w=D, nt=None):
            with ExitStack() as scope:
                nt = nt or (len(turns(X[:, 0, :])) if w == D else 1)
                st = [sb(f"st{name}{k}", [P, w], F32, scope) for k in range(TB)]
                hT = [sb(f"hT{name}{k}", [K, nt, P], F32, scope) for k in range(TB)]
                bst = sb(f"bst{name}", [P, T, 6], F32, scope)
                m = sb(f"m{name}", [P, 5, T], F32, scope)
                tp = [bank(f"tp{name}{k}", scope, P) for k in range(3)]
                op = [bank(f"op{name}{k}", scope) for k in range(3)]
                var_ready, rstd_ready = sem(f"var_ready{name}"), sem(f"rstd_ready{name}")
                loaded, stats, filled, turned, copied, product, taken, stored = [
                    sem(f"{n}{name}") for n in ("loaded", "stats", "filled", "turned", "copied", "product", "taken", "stored")]
                with nc.Block() as block:
                    @block.sync
                    def _(sp):
                        for a, b in loads or []:
                            sp.dma_start(a, b, allow_slow_non_contiguous=True).then_inc(loaded, 16)
                        if after is not None:
                            sp.wait_ge(taken, T)
                            n = after(sp, stored)
                            sp.wait_ge(stored, 16 * n)

                    @block.vector
                    def _(dve):
                        link = dve_step.on(dve)
                        if norm:
                            layernorm_stats(dve, link, bst, m, var_ready, rstd_ready)
                        if loads:
                            dve.wait_ge(loaded, 16 * len(loads))
                        if before is not None:
                            before(dve, link)
                        nc.vector.memset(bst[:, 0, 0:1], 0.0).then_inc(stats, 1)

                        def body(i):
                            for k in range(TB):
                                dve.wait_ge(product, i * TB + (k + 1))
                                post(dve, link, i * TB + k, op[k % 3]).then_inc(taken, 1)
                        dve_step.run(T // TB, body)

                    @block.scalar
                    def _(act):
                        act_step.on(act)
                        if norm:
                            act.wait_ge(var_ready, 1)
                            nc.scalar.sqrt(m[:, 3], m[:, 3]).then_inc(rstd_ready, 1)
                        act.wait_ge(stats, 1)

                        def body(i):
                            for k in range(TB):
                                fill(i * TB + k, st[k], m).then_inc(filled, 1)
                            for k in range(TB):
                                act.wait_ge(turned, i * TB + (k + 1))
                                if later(i):
                                    act.wait_ge(product, i * TB + (k + 1 - TB))
                                nc.scalar.copy(hT[k][:], tp[k % 3][0:K, 0:nt, :]).then_inc(copied, 1)
                        act_step.run(T // TB, body)

                    @block.tensor
                    def _(pe):
                        pe_step.on(pe)
                        if loads:
                            pe.wait_ge(loaded, 16 * len(loads))
                        pe.wait_ge(stats, 1)

                        def turn(i, k):
                            pe.wait_ge(filled, i * TB + (k + 1))
                            if later(i) or k >= 2:
                                pe.wait_ge(copied, i * TB + (k - 1))
                            hold(pe)
                            for j, piece in enumerate(turns(st[k][:])):
                                mm = nc.tensor.transpose(tp[k % 3][0:K, j, :], piece, ident[:])
                            mm.then_inc(turned, 1)

                        def multiply(i, k):
                            pe.wait_ge(copied, i * TB + (k + 1))
                            if later(i) or k >= 2:
                                pe.wait_ge(taken, i * TB + (k - 1))
                            project(hT[k], op[k % 3]).then_inc(product, 1)

                        def body(i):
                            for k in range(TB):
                                turn(i, k)
                                if k:
                                    multiply(i, k - 1)
                            multiply(i, TB - 1)
                        pe_step.run(T // TB, body)

        def tile(a, t):
            return a[:, bass.ds(t, 1), :].rearrange("p o d -> p (o d)")

        def normed(t, st, m):
            return nc.scalar.activation(st[:], tile(X, t), ACT.Relu, bias=m[:, 1, bass.ds(t, 1)],
                                        scale=m[:, 0, bass.ds(t, 1)])

        def two(W):
            def project(hT, o):
                m = W.shape[-1]
                nc.tensor.matmul(o[:, 0:m], lhsT=hT[:, 0, :], rhs=W[:, 0, :], start=True, stop=False)
                return nc.tensor.matmul(o[:, 0:m], lhsT=hT[:, 1, :], rhs=W[:, 1, :], start=False, stop=True)
            return project

        def row(a):
            return a.unsqueeze(0).to_broadcast([P, a.shape[0]])

        def halves(st):
            return [st[:, 0:P], st[:, P:D]]

        def conv(n, g, hout, bias, w):
            with ExitStack() as scope:
                G = sb(f"G{n}", [P, 2, B, H], F32, scope)
                idx = sb(f"idx{n}", [P, 2, B], U32, scope)
                ohlo = sb(f"cohlo{n}", [P, 2, B, P], F32, scope)
                ohhi = sb(f"cohhi{n}", [P, 2, B, T], F32, scope)
                V = sb(f"V{n}", [P, 2, B, T, H], F32, scope)
                acc = bank(f"acc{n}", scope)[:, 0:T * H]
                gathered = [sem(f"gathered{n}{h}") for h in range(2)]
                spread = [sem(f"spread{n}{h}") for h in range(2)]
                summed = [sem(f"csummed{n}{h}") for h in range(2)]
                with nc.Block() as block:
                    @block.gpsimd
                    def _(pool):
                        link = pool_step.on(pool)

                        def body(i):
                            for h in range(2):
                                if later(i):
                                    pool.wait_ge(spread[h], i * 2)
                                    hold(pool)
                                link(nc.gpsimd.tensor_copy(idx[:, h], src_i[:, bass.ds(i * (2 * B) + h * B, B)]))
                                hold(pool)
                                for b in range(B):
                                    nc.gpsimd.indirect_dma_start(
                                        G[:, h, b, :], None, tab16[n][:, :],
                                        bass.IndirectOffsetOnAxis(ap=idx[:, h, b:b + 1], axis=0)).then_inc(gathered[h], 16)
                        pool_step.run(C // (2 * B), body)
                        for h in range(2):
                            pool.wait_ge(gathered[h], 16 * B * (C // (2 * B)))

                    @block.vector
                    def _(dve):
                        link = dve_step.on(dve)

                        def body(i):
                            for h in range(2):
                                at = bass.ds(i * (2 * B) + h * B, B)
                                if later(i):
                                    dve.wait_ge(summed[h], i)
                                nc.vector.tensor_tensor(ohlo[:, h], rows(icol[:, 0:P], B), bc(fl["d"]["lo"][:, at], P),
                                                        ALU.is_equal).then_inc(spread[h], 1)
                                link(nc.vector.tensor_tensor(ohhi[:, h], rows(icol[:, 0:T], B),
                                                             bc(fl["d"]["hi"][:, at], T), ALU.is_equal))
                                dve.wait_ge(gathered[h], i * (16 * B) + 16 * B)
                                nc.vector.tensor_tensor(
                                    V[:, h], G[:, h].unsqueeze(2).to_broadcast([P, B, T, H]),
                                    ohhi[:, h].unsqueeze(3).to_broadcast([P, B, T, H]), ALU.mult).then_inc(spread[h], 1)
                        dve_step.run(C // (2 * B), body)
                        for h in range(2):
                            dve.wait_ge(summed[h], C // (2 * B))
                        hv = hout[:].rearrange("p t f -> p (t f)")
                        link(nc.vector.tensor_tensor(hv, acc, g[:].rearrange("p t f -> p (t f)"), ALU.add))
                        link(nc.vector.tensor_tensor(hout[:], hout[:], bc(dinv[:], H), ALU.mult))
                        link(nc.vector.tensor_tensor(hout[:], hout[:], rows(bias[:], T), ALU.add))
                        link(nc.vector.tensor_scalar(hout[:], hout[:], 0.0, None, ALU.max))

                    @block.tensor
                    def _(pe):
                        pe_step.on(pe)

                        def body(i):
                            for h in range(2):
                                pe.wait_ge(spread[h], i * 2 + 2)
                                for b in range(B):
                                    mm = nc.tensor.matmul(acc, lhsT=ohlo[:, h, b, :],
                                                          rhs=V[:, h, b].rearrange("p t f -> p (t f)"),
                                                          start=not later(i) and h == 0 and b == 0, stop=False,
                                                          skip_group_check=True)
                                mm.then_inc(summed[h], 1)
                        pe_step.run(C // (2 * B), body)

        if stop >= 3:
            free_sems()
            with ExitStack() as scope:
                W1 = sb("W1", [P, 2, H], F32, scope)
                W2 = sb("W2", [H, H], F32, scope)
                WoT = sb("WoT", [H, D], F32, scope)
                b1 = sb("b1", [P, H], F32, scope)
                b2 = sb("b2", [P, H], F32, scope)
                bo = sb("bo", [P, D], F32, scope)
                g = [sb(f"g{n}", [P, T, H], F32, scope) for n in range(2)]
                h16 = [sb(f"h16{n}", [P, T, H], F32, scope) for n in range(2)]
                pre = sb("pre", [P, T, D], F32, scope)

                rooted = sem("rooted")

                with nc.Block() as block:
                    @block.vector
                    def _(dve):
                        link = dve_step.on(dve)
                        link(nc.vector.tensor_scalar(dinv[:], degs["d"][:], 1.0, None, ALU.add))
                        nc.vector.tensor_scalar(dn[:], degs["s"][:], 1.0, None, ALU.max).then_inc(rooted, 1)
                        dve.wait_ge(rooted, 3)
                        link(nc.vector.reciprocal(dinv[:], dinv[:]))
                        link(nc.vector.reciprocal(dn[:], dn[:]))

                    @block.scalar
                    def _(act):
                        act.wait_ge(rooted, 1)
                        nc.scalar.sqrt(dinv[:], dinv[:]).then_inc(rooted, 1)
                        nc.scalar.sqrt(dn[:], dn[:]).then_inc(rooted, 1)

                def scaled(n):
                    def post(dve, link, t, o):
                        return nc.vector.tensor_scalar(tile(g[n], t), o[:, 0:H], dinv[:, bass.ds(t, 1)], None, ALU.mult)
                    return post

                def store16(n):
                    def after(sp, s):
                        sp.dma_start(tab16[n].rearrange("(t p) f -> p t f", p=P), g[n][:]).then_inc(s, 16)
                        return 1
                    return after

                tiles("a", normed, P, halves, two(W1), scaled(0), after=store16(0), norm=True,
                      loads=[(W1[:], A["L0_gnn_W1"].rearrange("(k p) m -> p k m", p=P)), (W2[:], A["L0_gnn_W2"]),
                             (WoT[:], A["L0_gnn_Wout"].rearrange("d h -> h d")), (b1[:], row(A["L0_gnn_b1"])),
                             (b2[:], row(A["L0_gnn_b2"])), (bo[:], row(A["L0_gnn_bout"]))])
                conv(0, g[0], h16[0], b1, H)
                tiles("b", lambda t, st, m: nc.scalar.copy(st[:], tile(h16[0], t)), H, lambda st: [st],
                      lambda hT, o: nc.tensor.matmul(o[:, 0:H], lhsT=hT[:, 0, :], rhs=W2[:], start=True, stop=True),
                      scaled(1), after=store16(1), w=H)
                conv(1, g[1], h16[1], b2, H)
                tiles("c", lambda t, st, m: nc.scalar.copy(st[:], tile(h16[1], t)), H, lambda st: [st],
                      lambda hT, o: nc.tensor.matmul(o[:, 0:D], lhsT=hT[:, 0, :], rhs=WoT[:], start=True, stop=True),
                      lambda dve, link, t, o: nc.vector.tensor_tensor(tile(pre, t), o[:, 0:D], bo[:], ALU.add), w=H)
                gate = sem("gate")
                with nc.Block() as block:
                    @block.scalar
                    def _(act):
                        nc.scalar.activation(pre[:], pre[:], ACT.Sigmoid).then_inc(gate, 1)

                    @block.vector
                    def _(dve):
                        dve.wait_ge(gate, 1)
                        dve_step.on(dve)(nc.vector.tensor_tensor(X[:], X[:], pre[:], ALU.add))

        def rsqrt_block(v, name, pre=None):
            made, rooted = sem(f"made{name}"), sem(f"rooted{name}")
            with nc.Block() as block:
                @block.vector
                def _(dve):
                    link = dve_step.on(dve)
                    pre(link)
                    dve.sem_inc(made, 1)
                    dve.wait_ge(rooted, 1)
                    link(nc.vector.reciprocal(v, v))

                @block.scalar
                def _(act):
                    act.wait_ge(made, 1)
                    nc.scalar.sqrt(v, v).then_inc(rooted, 1)

        def messages(SUM, fc1, fc2, fc3):
            with ExitStack() as scope:
                NG = 4
                G = sb("Gy", [P, 2, B, D], F32, scope)
                idx = sb("idxy", [P, NG, B], U32, scope)
                at = sb("at", [P, NG, B * 8], F32, scope)
                aT = sb("aT", [B * 8, 2, P], F32, scope)
                s1 = sb("s1", [P, 2, 2 * P], F32, scope)
                s2 = sb("s2", [P, 2, 2 * P], F32, scope)
                oh = sb("oh1", [P, 2, B, P], F32, scope)
                M = sb("M1", [P, 2, B, 8, MUL], F32, scope)
                w = sb("w", [P, 2, B, 4, MUL], F32, scope)
                te = sb("te", [P, B, MUL], F32, scope)
                tb = sb("tb", [P, 2, B, MUL], F32, scope)
                evs = sb("evs", [P, B, 3, MUL], F32, scope)
                wb = [[bank(f"w{h}{n}", scope) for n in range(2)] for h in range(2)]
                sm = [bank(f"sm{n}", scope) for n in range(2)]
                a0, a1 = bank("a0", scope), bank("a1", scope)
                gathered = [sem(f"gathered_y{h}") for h in range(NG)]
                pool_idx = sem("pool_idx")
                attr_st, attr_tp, attr_T, h1_done, s1_done, h2_done, s2_done, w_done, w_kept, parts, msg, summed, added = [
                    sem(f"{x}_y") for x in ("attr_st", "attr_tp", "attr_T", "h1_done", "s1_done", "h2_done", "s2_done",
                                            "w_done", "w_kept", "parts", "msg", "summed", "added")]
                n_g = Q // B
                with nc.Block() as block:
                    @block.gpsimd
                    def _(pool):
                        link = Links(pool, pool_idx, 1)

                        def gather(g):
                            need(pool, gathered[g.slot], g.lap(16 * B))
                            link.start(g)(nc.gpsimd.tensor_copy(idx[:, g.slot], S_idx[:, bass.ds(g.at(B), B)]))
                            need(pool, msg, g.at(5, 5 - 2 * 5))
                            hold(pool)
                            for b in range(B):
                                nc.gpsimd.indirect_dma_start(
                                    G[:, g.slot % 2, b, :], None, taby[:, :],
                                    bass.IndirectOffsetOnAxis(ap=idx[:, g.slot, b:b + 1], axis=0)
                                ).then_inc(gathered[g.slot], 16)
                        groups(pool, n_g, NG, [(0, gather)])

                    @block.scalar
                    def _(act):
                        copy = nc.scalar.copy

                        def stage(g):
                            need(act, attr_tp, g.at(1, 1 - NG))
                            hold(act)
                            copy(at[:, g.slot].rearrange("p (b f) -> p b f", b=B),
                                 S_attr[:, bass.ds(g.at(B), B), 0:8]).then_inc(attr_st, 1)

                        def keep_turned(g):
                            act.wait_ge(attr_tp, g.at(1, 1))
                            need(act, h1_done, g.at(1, -1))
                            copy(aT[:, g.slot % 2], a0[0:B * 8, 0:P]).then_inc(attr_T, 1)

                        def keep_weights(g):
                            need(act, msg, g.at(5, 5 - 2 * 5))
                            for n in range(2):
                                act.wait_ge(w_done, g.at(2, n + 1))
                                w4 = wb[g.slot % 2][n].rearrange("p (b k u) -> p b k u", k=4, u=MUL)
                                copy(w[:, g.slot % 2, 2 * n:2 * n + 2, 1:4:2, :], w4[:, :, 1:4:2, :]).then_inc(w_kept, 1)
                                hold(act)
                                for b in range(2):
                                    nc.scalar.activation(w[:, g.slot % 2, 2 * n + b, 0:4:2, :], w4[:, b, 0:4:2, :], ACT.Copy,
                                                         scale=S_attr[:, bass.ds(g.at(B, 2 * n + b), 1), 8]).then_inc(w_kept, 1)

                        def silu1(g):
                            act.wait_ge(h1_done, g.at(1, 1))
                            need(act, h2_done, g.at(1, -1))
                            nc.scalar.activation(s1[:, g.slot % 2], a0[:, 0:2 * P], ACT.Silu, scale=8.0 ** -0.5).then_inc(s1_done, 1)

                        def silu2(g):
                            act.wait_ge(h2_done, g.at(1, 1))
                            need(act, w_done, g.at(2, -2))
                            nc.scalar.activation(s2[:, g.slot % 2], a1[:, 0:2 * P], ACT.Silu, scale=0.125).then_inc(s2_done, 1)
                        groups(act, n_g, NG, [(0, stage), (1, keep_turned), (4, keep_weights), (1, silu1), (2, silu2)])

                    @block.tensor
                    def _(pe):
                        def turn(g):
                            pe.wait_ge(attr_st, g.at(1, 1))
                            need(pe, s1_done, g.at(1))
                            hold(pe)
                            nc.tensor.transpose(a0[0:B * 8, 0:P], at[:, g.slot], ident[:]).then_inc(attr_tp, 1)

                        def layer1(g):
                            pe.wait_ge(attr_T, g.at(1, 1))
                            hold(pe)
                            for j in range(2):
                                mm = nc.tensor.matmul(a0[:, j * P:(j + 1) * P], lhsT=fc1[:, j], rhs=aT[:, g.slot % 2],
                                                      start=True, stop=True)
                            mm.then_inc(h1_done, 1)

                        def layer2(g):
                            pe.wait_ge(s1_done, g.at(1, 1))
                            need(pe, s2_done, g.at(1))
                            hold(pe)
                            nc.tensor.matmul(a1[:, 0:2 * P], lhsT=fc2[:], rhs=s1[:, g.slot % 2], start=True,
                                             stop=True).then_inc(h2_done, 1)

                        def weights(g):
                            pe.wait_ge(s2_done, g.at(1, 1))
                            need(pe, w_kept, g.at(6, 6 - 2 * 6))
                            for n in range(2):
                                nc.tensor.matmul(wb[g.slot % 2][n], lhsT=s2[:, g.slot % 2, n * P:(n + 1) * P],
                                                 rhs=fc3[:], start=True, stop=True).then_inc(w_done, 1)

                        def sums(bs):
                            def step(g):
                                need(pe, msg, g.at(5, 5))
                                for b in bs:
                                    need(pe, added, g.at(B, b - 1))
                                    nc.tensor.matmul(sm[b % 2], lhsT=oh[:, g.slot % 2, b, :],
                                                     rhs=M[:, g.slot % 2, b].rearrange("p k u -> p (k u)"), start=True,
                                                     stop=True).then_inc(summed, 1)
                            return step
                        groups(pe, n_g, NG, [(0, turn), (4, sums((0, 1))), (0, layer1), (4, sums((2, 3))), (1, layer2), (2, weights)])

                    @block.vector
                    def _(dve):
                        mul = ALU.mult
                        tt = nc.vector.tensor_tensor
                        tiles_of = {}
                        dve_step.on(dve)(nc.vector.memset(SUM[:], 0.0))

                        def add(g, b):
                            r = g.slot * B + b
                            acc = SUM[:, bass.ds(tiles_of[r], 1), :].rearrange("p o f -> p (o f)")
                            need(dve, added, g.at(B, b))
                            dve.wait_ge(summed, g.at(B, b + 1))
                            tt(acc, acc, sm[b % 2], ALU.add).then_inc(added, 1)

                        def messages_of(g):
                            h = g.slot % 2
                            at_q = bass.ds(g.at(B), B)
                            sh1 = S_attr[:, at_q, 9:12].unsqueeze(3).to_broadcast([P, B, 3, MUL])
                            es = G[:, h, :, 0:MUL]
                            ev = G[:, h, :, MUL:D].rearrange("p b (d u) -> p b d u", u=MUL)
                            old = None if g.first() else Group(g.i, NG, g.off * NG + g.slot - 1)

                            def add_old(b):
                                if old is not None:
                                    add(old, b)
                            need(dve, summed, g.at(B, B - 2 * B))
                            tt(oh[:, h], rows(icol[:, 0:P], B), bc(keyl["s"][:, at_q], P), ALU.is_equal).then_inc(msg, 1)
                            dve.wait_ge(gathered[g.slot], g.lap(16 * B, 16 * B))
                            tt(evs[:], ev, sh1, mul).then_inc(parts, 1)
                            add_old(0)
                            dve.wait_ge(parts, g.at(4, 1))
                            tt(te[:], evs[:, :, 0], evs[:, :, 1], ALU.add).then_inc(parts, 1)
                            dve.wait_ge(w_kept, g.at(6, 6))
                            tt(tb[:, 0], w[:, h, :, 1, :], es, mul).then_inc(parts, 1)
                            dve.wait_ge(parts, g.at(4, 2))
                            tt(tb[:, 1], te[:], evs[:, :, 2], ALU.add).then_inc(parts, 1)
                            add_old(1)
                            tt(M[:, h, :, 0, :], w[:, h, :, 0, :], es, mul).then_inc(msg, 1)
                            dve.wait_ge(parts, g.at(4, 3))
                            tt(M[:, h, :, 2:8:2, :], tb[:, 0].unsqueeze(2).to_broadcast([P, B, 3, MUL]), sh1, mul).then_inc(msg, 1)
                            add_old(2)
                            tt(M[:, h, :, 3:8:2, :], w[:, h, :, 2:3, :].to_broadcast([P, B, 3, MUL]), ev, mul).then_inc(msg, 1)
                            dve.wait_ge(parts, g.at(4, 4))
                            tt(M[:, h, :, 1, :], w[:, h, :, 3, :], tb[:, 1], mul).then_inc(msg, 1)
                            add_old(3)
                        groups(dve, n_g, NG, [(0, messages_of)], pair_tiles("s", mybir.EngineType.DVE, NG, tiles_of))
                        for b in range(B):
                            add(Group(n_g // NG, NG, n_g % NG - 1), b)
                        dve.wait_ge(added, Q)

        if stop >= 4:
            free_sems()
            with ExitStack() as scope:
                w1 = [sb(f"w1{n}", [MUL, 2 * MUL], F32, scope) for n in "sv"]
                w2 = [sb(f"w2{n}", [2 * MUL, MUL], F32, scope) for n in "sv"]
                fc1 = sb("fc1", [B * 8, 2, P], F32, scope)
                fc2 = sb("fc2", [P, P], F32, scope)
                fc3 = sb("fc3", [P, 2 * 4 * MUL], F32, scope)
                cleared = sem("fc_cleared")
                with nc.Block() as block:
                    @block.vector
                    def _(dve):
                        for a in (fc1, fc2, fc3):
                            nc.vector.memset(a[:], 0.0).then_inc(cleared, 1)
                        dve.wait_ge(cleared, 3)
                gsv = sb("gsv", [P, 2, MUL], F32, scope)
                SC = sb("SC", [P, T, D], F32, scope)
                SUM = sb("SUM", [P, T, 8 * MUL], F32, scope)
                with ExitStack() as inner:
                    Y = sb("Y", [P, T, D], F32, inner)

                    def y_project(hT, o):
                        for j in range(4):
                            mm = nc.tensor.matmul(o[:, j * 2 * MUL:(j + 1) * 2 * MUL], lhsT=hT[:, j, :],
                                                  rhs=w1[min(j, 1)][:], start=True, stop=True)
                        return mm

                    def y_post(dve, link, t, o):
                        o4 = o.rearrange("p (j k u) -> p j k u", k=2, u=MUL)
                        link(nc.vector.tensor_copy(tile(Y, t).rearrange("p (j u) -> p j u", u=MUL), o4[:, :, 0, :]))
                        return nc.vector.tensor_scalar(tile(SC, t).rearrange("p (j u) -> p j u", u=MUL), o4[:, :, 1, :],
                                                       MUL ** -0.5, None, ALU.mult)

                    def y_store(sp, s):
                        sp.dma_start(taby.rearrange("(t p) f -> p t f", p=P), Y[:]).then_inc(s, 16)
                        return 1

                    pre = "L1_gnn_"
                    tiles("d", normed, MUL, lambda st: [st[:, 0:MUL]] + [st[:, MUL + d:D:3] for d in range(3)],
                          y_project, y_post, after=y_store, norm=True,
                          loads=[(w1[0][:, 0:MUL], A[pre + "w1_s"]), (w1[0][:, MUL:], A[pre + "wsc_s"]),
                                 (w1[1][:, 0:MUL], A[pre + "w1_v"]), (w1[1][:, MUL:], A[pre + "wsc_v"]),
                                 (w2[0][:], A[pre + "w2_s"]), (w2[1][:], A[pre + "w2_v"]),
                                 *[(fc1[b * 8:(b + 1) * 8, b // 2, b % 2 * MUL:(b % 2 + 1) * MUL], A[pre + "fc_w1"])
                                   for b in range(B)],
                                 *[(fc2[h * MUL:(h + 1) * MUL, h * MUL:(h + 1) * MUL], A[pre + "fc_w2"]) for h in range(2)],
                                 *[(fc3[h * MUL:(h + 1) * MUL, h * 4 * MUL:(h + 1) * 4 * MUL], A[pre + "fc_w3"]) for h in range(2)],
                                 (gsv[:, 0], row(A[pre + "g_s"])), (gsv[:, 1], row(A[pre + "g_v"]))])
                messages(SUM, fc1, fc2, fc3)
                O = sb("O", [P, T, D], F32, scope)
                ms = sb("ms", [P, 2, T], F32, scope)
                dns = sb("dns", [P, T], F32, scope)

                def before(dve, link):
                    link(nc.vector.tensor_scalar(dns[:], dn[:], MUL ** -0.5 * MUL ** -0.5 * (2 * MUL) ** -0.5, None, ALU.mult))
                    link(nc.vector.tensor_scalar(w2[0][MUL:, :], w2[0][MUL:, :], 0.5773502691896258, None, ALU.mult))

                def o_project(hT, o):
                    for j in range(4):
                        mm = nc.tensor.matmul(o[:, j * MUL:(j + 1) * MUL], lhsT=hT[:, j, :], rhs=w2[min(j, 1)][:],
                                              start=True, stop=True)
                    return mm

                tiles("e", lambda t, st, m: nc.scalar.copy(st[:], tile(SUM, t)), P,
                      lambda st: [st[:, j * P:(j + 1) * P] for j in range(4)], o_project,
                      lambda dve, link, t, o: nc.vector.scalar_tensor_tensor(
                          out=tile(O, t), in0=o[:, 0:D], scalar=dns[:, bass.ds(t, 1)], in1=tile(SC, t),
                          op0=ALU.mult, op1=ALU.add), before=before, w=8 * MUL, nt=4)

                def mean_squares(link):
                    sq = SUM[:, :, 0:D]
                    link(nc.vector.tensor_tensor(sq, O[:], O[:], ALU.mult))
                    for n, (a, b) in enumerate(((0, MUL), (MUL, D))):
                        link(nc.vector.tensor_reduce(ms[:, n], sq[:, :, a:b], AX.X, ALU.add))
                        link(nc.vector.tensor_scalar(ms[:, n], ms[:, n], 1.0 / (b - a), EPS, ALU.mult, ALU.add))

                rsqrt_block(ms[:], "rms", mean_squares)
                with nc.Block() as block:
                    @block.vector
                    def _(dve):
                        link = dve_step.on(dve)
                        for n, (a, b) in enumerate(((0, MUL), (MUL, D))):
                            link(nc.vector.tensor_tensor(O[:, :, a:b], O[:, :, a:b], bc(ms[:, n], b - a), ALU.mult))
                            for j in range(a // MUL, b // MUL):
                                o = O[:, :, j * MUL:(j + 1) * MUL]
                                x = X[:, :, 0:MUL] if j == 0 else X[:, :, MUL + j - 1:D:3]
                                link(nc.vector.tensor_tensor(o, o, rows(gsv[:, n], T), ALU.mult))
                                link(nc.vector.tensor_tensor(x, x, o, ALU.add))

        def attend(l, W, al, ar, dist):
            n_it = Q // (2 * B)
            outer = ExitStack()
            with outer:
                EX = sb(f"EX{l}", [P, Q, HEADS], F32, outer)
                EA = sb(f"EA{l}", [P, Q, HEADS], F32, outer) if dist else EX
                with ExitStack() as scope:
                    wt = sb(f"wt{l}", [P, 2, D], F32, scope)
                    attn = sb(f"attn{l}", [P, 2, D], F32, scope)
                    el = sb(f"el{l}", [P, T, 2, HEADS], F32, scope)
                    elt = sb(f"elt{l}", [P, T, HEADS], F32, scope)
                    ert = sb(f"ert{l}", [P, T, HEADS], F32, scope)
                    EL = sb(f"EL{l}", [P, Q, HEADS], F32, scope)
                    ER = sb(f"ER{l}", [P, Q, HEADS], F32, scope)
                    with ExitStack() as inner:
                        F = sb(f"F{l}", [P, T, D], F32, inner)
                        fa = sb(f"fa{l}", [P, 2, D], F32, inner)

                        def post(dve, link, t, o):
                            link(nc.vector.tensor_copy(tile(F, t), o[:, 0:D]))
                            link(nc.vector.tensor_tensor(fa[:], tile(F, t).unsqueeze(1).to_broadcast([P, 2, D]), attn[:], ALU.mult))
                            return nc.vector.tensor_reduce(
                                el[:, bass.ds(t, 1)].rearrange("p o k h -> p (o k h)"),
                                fa[:].rearrange("p k (h d) -> p (k h) d", h=HEADS), AX.X, ALU.add)

                        def store(sp, s):
                            sp.dma_start(tabf[l - 2].rearrange("(t p) f -> p t f", p=P), F[:]).then_inc(s, 16)
                            return 1

                        tiles(f"f{l}", normed, P, halves, two(wt), post, after=store, norm=True,
                              loads=[(wt[:], W.rearrange("(k p) m -> p k m", p=P)), (attn[:, 0], row(al)), (attn[:, 1], row(ar))])
                    logits(l, el, elt, ert, EL, ER)
                    weights_of_edges(l, EL, ER, EX, EA, dist)
                SUM = sb(f"SUM{l}", [P, T, D + HEADS], F32, outer)
                with ExitStack() as scope:
                    NG = 5
                    SUM2 = sb(f"SUM2{l}", [P, T, D + HEADS], F32, scope)
                    G = sb(f"G{l}", [P, NG, B, D], F32, scope)
                    idx = sb(f"idx{l}", [P, NG, B], U32, scope)
                    oh = sb(f"oh{l}", [P, NG, B, P], F32, scope)
                    M = sb(f"M{l}", [P, NG, B, D + HEADS], F32, scope)
                    sm = [bank(f"sm{l}{n}", scope)[:, 0:D + HEADS] for n in range(NG)]
                    gathered = [sem(f"gathered{l}{h}") for h in range(NG)]
                    staged, msg, summed, added, cleared = [
                        sem(f"{x}{l}") for x in ("staged", "msg", "summed", "added", "cleared")]
                    with nc.Block() as block:
                        @block.scalar
                        def _(act):
                            def stage(g):
                                need(act, msg, g.at(3, 3 - 3 * NG))
                                hold(act)
                                nc.scalar.copy(idx[:, g.slot], D_idx[:, bass.ds(g.at(B), B)]).then_inc(staged, 1)
                            groups(act, Q // B, NG, [(0, stage)])

                        @block.gpsimd
                        def _(pool):
                            def gather(g):
                                need(pool, staged, g.at(1, 1))
                                hold(pool)
                                for b in range(B):
                                    nc.gpsimd.indirect_dma_start(
                                        G[:, g.slot, b, :], None, tabf[l - 2][:, :],
                                        bass.IndirectOffsetOnAxis(ap=idx[:, g.slot, b:b + 1], axis=0)
                                    ).then_inc(gathered[g.slot], 16)
                            groups(pool, Q // B, NG, [(0, gather)])

                        @block.tensor
                        def _(pe):
                            def sums(g):
                                need(pe, msg, g.at(3, 3))
                                for b in range(B):
                                    need(pe, added, g.at(B, b + 1 - NG))
                                    nc.tensor.matmul(sm[(g.slot * B + b) % NG], lhsT=oh[:, g.slot, b, :], rhs=M[:, g.slot, b],
                                                     start=True, stop=True).then_inc(summed, 1)
                            groups(pe, Q // B, NG, [(0, sums)])

                        @block.vector
                        def _(dve):
                            tt = nc.vector.tensor_tensor
                            nc.vector.memset(SUM[:], 0.0).then_inc(cleared, 1)
                            nc.vector.memset(SUM2[:], 0.0).then_inc(cleared, 1)
                            dve.wait_ge(cleared, 2)
                            tiles_of = {}

                            def message(g):
                                at_q = bass.ds(g.at(B), B)
                                need(dve, summed, g.at(B, B - B * NG))
                                tt(oh[:, g.slot], rows(icol[:, 0:P], B), bc(keyl["d"][:, at_q], P),
                                   ALU.is_equal).then_inc(msg, 1)
                                nc.vector.tensor_copy(M[:, g.slot, :, D:], EX[:, at_q, :]).then_inc(msg, 1)
                                dve.wait_ge(gathered[g.slot], g.lap(16 * B, 16 * B))
                                tt(M[:, g.slot, :, 0:D].rearrange("p b (k d) -> p b k d", k=HEADS),
                                   G[:, g.slot].rearrange("p b (k d) -> p b k d", k=HEADS),
                                   EA[:, at_q, :].unsqueeze(3).to_broadcast([P, B, HEADS, D // HEADS]),
                                   ALU.mult).then_inc(msg, 1)

                            def add(g):
                                for b in range(B):
                                    r = g.slot * B + b
                                    acc = (SUM, SUM2)[b % 2][:, bass.ds(tiles_of[r], 1), :].rearrange("p o f -> p (o f)")
                                    need(dve, added, g.at(B, b - 1))
                                    dve.wait_ge(summed, g.at(B, b + 1))
                                    tt(acc, acc, sm[r % NG], ALU.add).then_inc(added, 1)
                            groups(dve, Q // B, NG, [(0, message), (1, add)],
                                   pair_tiles("d", mybir.EngineType.DVE, NG, tiles_of))
                            dve.wait_ge(added, Q)
                            dve_step.on(dve)(tt(SUM[:], SUM[:], SUM2[:], ALU.add))
                gat_end(l, SUM)

        def logits(l, el, elt, ert, EL, ER):
            with ExitStack() as scope:
                lo = sb(f"llo{l}", [P, Q], F32, scope)
                hi = sb(f"lhi{l}", [P, Q], F32, scope)
                hii = sb(f"lhii{l}", [P, Q], U32, scope)
                NG, ahead = 4, 2
                el3 = sb(f"el3{l}", [P, 3, T, HEADS], BF16, scope)
                er3 = sb(f"er3{l}", [P, T, 3, HEADS], BF16, scope)
                hot_s = sb(f"hot_s{l}", [P, NG, B, P], BF16, scope)
                hot_d = sb(f"hot_d{l}", [P, NG, B, P], BF16, scope)
                ohhi = sb(f"lohhi{l}", [P, NG, B, T], F32, scope)
                hotT = sb(f"hotT{l}", [P, NG, 2 * B, P], BF16, scope)
                pr = sb(f"lpr{l}", [P, NG, B, T * HEADS], F32, scope)
                tp = [bank(f"ltp{l}{h}", scope, P, BF16) for h in range(NG)]
                lp = [bank(f"llp{l}{h}", scope) for h in range(NG)]
                made_s, made_d, turned, copied, looked, picked, taken, split = [
                    sem(f"{x}{l}") for x in ("made_s", "made_d", "lturned", "lcopied", "looked", "picked", "ltaken", "lsplit")]
                NL = B * T * HEADS
                with nc.Block() as block:
                    @block.vector
                    def _(dve):
                        link = dve_step.on(dve)
                        tt = nc.vector.tensor_tensor
                        link(nc.vector.tensor_scalar(hii[:], D_idx[:], 7, None, ALU.logical_shift_right))
                        link(nc.vector.tensor_copy(hi[:], hii[:]))
                        link(nc.vector.tensor_copy(lo[:], D_idx[:]))
                        link(nc.vector.scalar_tensor_tensor(out=lo[:], in0=hi[:], scalar=-float(P), in1=lo[:],
                                                            op0=ALU.mult, op1=ALU.add))
                        link(nc.vector.tensor_copy(elt[:], el[:, :, 0, :]))
                        link(nc.vector.tensor_copy(ert[:], el[:, :, 1, :]))
                        for n in range(3):
                            link(nc.vector.tensor_copy(el3[:, n], elt[:]))
                            link(nc.vector.tensor_copy(er3[:, :, n, :], ert[:]))
                            link(tt(elt[:], elt[:], el3[:, n], ALU.subtract))
                            link(tt(ert[:], ert[:], er3[:, :, n, :], ALU.subtract))
                        dve.sem_inc(split, 1)

                        def hots(g):
                            at_q = bass.ds(g.at(B), B)
                            need(dve, turned, g.at(1, 1 - NG))
                            tt(hot_s[:, g.slot], rows(icol[:, 0:P], B), bc(lo[:, at_q], P), ALU.is_equal).then_inc(made_s, 1)
                            tt(hot_d[:, g.slot], rows(icol[:, 0:P], B), bc(keyl["d"][:, at_q], P), ALU.is_equal).then_inc(made_d, 1)
                            need(dve, taken, g.at(2, 2 - 2 * NG))
                            tt(ohhi[:, g.slot], rows(icol[:, 0:T], B), bc(hi[:, at_q], T), ALU.is_equal).then_inc(made_s, 1)

                        def take(g):
                            at_q = bass.ds(g.at(B), B)
                            dve.wait_ge(looked, g.at(1, 1))
                            dve.wait_ge(made_s, g.at(2, 2))
                            tt(pr[:, g.slot].rearrange("p b (t k) -> p b t k", k=HEADS),
                               lp[g.slot][:, 0:NL].rearrange("p (b t k) -> p b t k", b=B, k=HEADS),
                               ohhi[:, g.slot].unsqueeze(3).to_broadcast([P, B, T, HEADS]), ALU.mult).then_inc(picked, 1)
                            nc.vector.tensor_reduce(
                                ER[:, at_q, :], lp[g.slot][:, NL:NL + 3 * B * HEADS].rearrange("p (b n k) -> p b k n", b=B, k=HEADS),
                                AX.X, ALU.add).then_inc(taken, 1)
                            dve.wait_ge(picked, g.at(1, 1))
                            nc.vector.tensor_reduce(EL[:, at_q, :], pr[:, g.slot].rearrange("p b (t k) -> p b k t", k=HEADS),
                                                    AX.X, ALU.add).then_inc(taken, 1)
                        groups(dve, Q // B, NG, [(0, hots), (ahead, take)])

                    @block.scalar
                    def _(act):
                        def copy(g):
                            act.wait_ge(turned, g.at(1, 1))
                            need(act, looked, g.at(1, 1 - NG))
                            nc.scalar.copy(hotT[:, g.slot], tp[g.slot]).then_inc(copied, 1)
                        groups(act, Q // B, NG, [(0, copy)])

                    @block.tensor
                    def _(pe):
                        pe.wait_ge(split, 1)
                        tiles_of = {}

                        def turn(g):
                            pe.wait_ge(made_s, g.at(2, 1))
                            pe.wait_ge(made_d, g.at(1, 1))
                            need(pe, copied, g.at(1, 1 - NG))
                            for b in range(B):
                                nc.tensor.transpose(tp[g.slot][:, b, :], hot_s[:, g.slot, b, :], identb[:])
                            for b in range(B):
                                mm = nc.tensor.transpose(tp[g.slot][:, B + b, :], hot_d[:, g.slot, b, :], identb[:])
                            mm.then_inc(turned, 1)

                        def look(g):
                            need(pe, taken, g.at(2, 2 - 2 * NG))
                            pe.wait_ge(copied, g.at(1, 1))
                            hold(pe)
                            o = lp[g.slot]
                            for b in range(B):
                                for n in range(3):
                                    nc.tensor.matmul(o[:, b * T * HEADS:(b + 1) * T * HEADS], lhsT=hotT[:, g.slot, b, :],
                                                     rhs=el3[:, n].rearrange("p t k -> p (t k)"), start=(n == 0), stop=(n == 2))
                            for b in range(B):
                                at = NL + b * 3 * HEADS
                                mm = nc.tensor.matmul(o[:, at:at + 3 * HEADS], lhsT=hotT[:, g.slot, B + b, :],
                                                      rhs=er3[:, bass.ds(tiles_of[g.slot * B + b], 1)]
                                                      .rearrange("p o n k -> p (o n k)"), start=True, stop=True)
                            mm.then_inc(looked, 1)
                        groups(pe, Q // B, NG, [(0, turn), (1, look)], pair_tiles("d", mybir.EngineType.PE, NG, tiles_of))

        def weights_of_edges(l, EL, ER, EX, EA, dist):
            with ExitStack() as scope:
                TE = sb(f"TE{l}", [QP, QB, HEADS, P], F32, scope)
                TK = sb(f"TK{l}", [QP, QB, P], F32, scope)
                pen = sb(f"pen{l}", [QP, QB, P + 1], F32, scope)
                S = sb(f"S{l}", [QP, QB, HEADS, P], F32, scope)
                ends = sb(f"ends{l}", [QP, QB, HEADS], F32, scope)
                LR = sb(f"LR{l}", [HEADS, Q], F32, scope)
                KF = sb(f"KF{l}", [HEADS, Q], F32, scope)
                KL = sb(f"KL{l}", [HEADS, Q], F32, scope)
                pl = sb(f"pl{l}", [HEADS, Q + 1], F32, scope)
                pls = sb(f"pls{l}", [HEADS, Q], F32, scope)
                plb = sb(f"plb{l}", [HEADS, Q], F32, scope)
                GR = sb(f"GR{l}", [HEADS, Q + 2], F32, scope)
                CR = sb(f"CR{l}", [HEADS, Q], F32, scope)
                cin = sb(f"cin{l}", [QP, QB, HEADS], F32, scope)
                MX = sb(f"MX{l}", [P, HEADS, Q], F32, scope)
                ts = sb(f"ts{l}", [P, HEADS, Q], F32, scope)
                z = sb(f"z{l}", [P, Q, HEADS], F32, scope)
                bk = [bank(f"wb{l}{n}", scope) for n in range(2)]
                r_up, r_down = sem(f"r_up{l}"), sem(f"r_down{l}")

                plan = []
                for b in range(QB):
                    plan.append([("T", (b, h), EL) for h in range(HEADS)])
                plan.append([("K", b, None) for b in range(QB)])
                plan.append([("F", b, None) for b in range(QB)])
                plan.append([("L", b, None) for b in range(QB)])
                for way in range(2):
                    plan.append([("E", b, None) for b in range(QB)])
                    plan.append([("C", b, None) for b in range(QB)])
                for h in range(HEADS):
                    plan.append([("M", (b, h), None) for b in range(QB)])

                with nc.Block() as block:
                    @block.tensor
                    def _(pe):
                        for n, work in enumerate(plan):
                            pe.wait_ge(r_down, n + 1)
                            o = bk[n % 2]
                            for what, k, _ in work:
                                if what == "T":
                                    mm = nc.tensor.transpose(o[0:QP, k[1] * P:(k[1] + 1) * P],
                                                             EL[:, k[0] * QP:(k[0] + 1) * QP, k[1]], ident[:])
                                elif what == "K":
                                    mm = nc.tensor.transpose(o[0:QP, k * P:(k + 1) * P], D_key[:, k * QP:(k + 1) * QP], ident[:])
                                elif what in "FL":
                                    e = 0 if what == "F" else P - 1
                                    mm = nc.tensor.matmul(o[0:HEADS, k * QP:(k + 1) * QP],
                                                          lhsT=TK[:, k, e:e + 1].to_broadcast([QP, HEADS]),
                                                          rhs=ident[0:QP, 0:QP], start=True, stop=True)
                                elif what == "E":
                                    mm = nc.tensor.transpose(o[0:HEADS, k * QP:(k + 1) * QP], ends[:, k, :], ident[0:QP, 0:QP])
                                elif what == "C":
                                    mm = nc.tensor.transpose(o[0:QP, k * HEADS:(k + 1) * HEADS], CR[:, k * QP:(k + 1) * QP],
                                                             ident[0:HEADS, 0:HEADS])
                                else:
                                    mm = nc.tensor.transpose(o[:, k[0] * QP:(k[0] + 1) * QP], TE[:, k[0], k[1], :],
                                                             ident[0:QP, 0:QP])
                            mm.then_inc(r_up, 1)

                    @block.vector
                    def _(dve):
                        link = dve_step.on(dve)
                        v = nc.vector
                        tt = v.tensor_tensor
                        done = [0]

                        def go():
                            dve.sem_inc(r_down, 1)

                        def got():
                            done[0] += 1
                            dve.wait_ge(r_up, done[0])
                            return bk[(done[0] - 1) % 2]

                        go()
                        for b in range(QB):
                            o = got()
                            link(v.tensor_copy(TE[:, b].rearrange("p h e -> p (h e)"), o[0:QP, :]))
                            go()
                        link(v.tensor_copy(TK[:].rearrange("p b e -> p (b e)"), got()[0:QP, :]))
                        go()
                        link(v.tensor_copy(KF[:], got()[0:HEADS, 0:Q]))
                        go()
                        link(v.tensor_copy(KL[:], got()[0:HEADS, 0:Q]))
                        link(v.memset(pen[:], 0.0))
                        link(tt(pen[:, :, 1:P], TK[:, :, 1:P], TK[:, :, 0:P - 1], ALU.not_equal))
                        link(v.tensor_scalar(pen[:], pen[:], -BIG, None, ALU.mult))
                        link(v.memset(pl[:], 1.0))
                        link(tt(pl[:, 1:Q], KF[:, 1:Q], KL[:, 0:Q - 1], ALU.not_equal))
                        link(v.tensor_scalar(pl[:], pl[:], -BIG, None, ALU.mult))
                        link(tt(CR[:], KF[:], KL[:], ALU.not_equal))
                        link(v.tensor_scalar(CR[:], CR[:], -BIG, None, ALU.mult))
                        link(tt(pls[:], pl[:, 0:Q], CR[:], ALU.add))
                        link(tt(plb[:], pl[:, 1:Q + 1], CR[:], ALU.add))
                        link(v.memset(GR[:], -BIG))
                        for way in range(2):
                            for b in range(QB):
                                for h in range(HEADS):
                                    if way == 0:
                                        link(v.tensor_tensor_scan(S[:, b, h], pen[:, b, 0:P], TE[:, b, h], -BIG, ALU.add, ALU.max))
                                    else:
                                        link(v.tensor_tensor_scan(S[:, b, h, ::-1], pen[:, b, P:0:-1], TE[:, b, h, ::-1], -BIG,
                                                                  ALU.add, ALU.max))
                            link(v.tensor_copy(ends[:], S[:, :, :, P - 1 if way == 0 else 0]))
                            go()
                            link(v.tensor_copy(LR[:], got()[0:HEADS, 0:Q]))
                            if way == 0:
                                link(v.tensor_tensor_scan(GR[:, 1:Q + 1], pls[:], LR[:], -BIG, ALU.add, ALU.max))
                                link(tt(CR[:], GR[:, 0:Q], pl[:, 0:Q], ALU.add))
                            else:
                                link(v.tensor_tensor_scan(GR[:, Q:0:-1], plb[:, ::-1], LR[:, ::-1], -BIG, ALU.add, ALU.max))
                                link(tt(CR[:], GR[:, 2:Q + 2], pl[:, 1:Q + 1], ALU.add))
                            go()
                            link(v.tensor_copy(cin[:], got()[0:QP, 0:QB * HEADS].rearrange("p (b h) -> p b h", h=HEADS)))
                            for b in range(QB):
                                for h in range(HEADS):
                                    c = cin[:, b, h:h + 1]
                                    if way == 0:
                                        link(v.tensor_tensor_scan(TE[:, b, h], pen[:, b, 0:P], TE[:, b, h], c, ALU.add, ALU.max))
                                    else:
                                        link(v.tensor_tensor_scan(TE[:, b, h, ::-1], pen[:, b, P:0:-1], TE[:, b, h, ::-1], c,
                                                                  ALU.add, ALU.max))
                        go()
                        for h in range(HEADS):
                            link(v.tensor_copy(MX[:, h], got()[:, 0:Q]))
                            if h < HEADS - 1:
                                go()
                        er = ER[:].rearrange("p q h -> p h q")
                        link(tt(MX[:], MX[:], er, ALU.add))
                        link(v.scalar_tensor_tensor(out=ts[:], in0=MX[:], scalar=0.2, in1=MX[:], op0=ALU.mult, op1=ALU.max))
                        link(tt(z[:], EL[:], ER[:], ALU.add))
                        link(v.scalar_tensor_tensor(out=z[:], in0=z[:], scalar=0.2, in1=z[:], op0=ALU.mult, op1=ALU.max))
                        link(tt(z[:], z[:], ts[:].rearrange("p h q -> p q h"), ALU.subtract))
                        dve.sem_inc(r_down, 1)
                        if dist:
                            dve.wait_ge(r_up, len(plan) + 1)
                            link(tt(EA[:], EX[:], bc(D_dist[:], HEADS), ALU.mult))

                    @block.scalar
                    def _(act):
                        act.wait_ge(r_down, len(plan) + 1)
                        nc.scalar.activation(EX[:], z[:], ACT.Exp).then_inc(r_up, 1)

        def gat_end(l, SUM):
            with ExitStack() as scope:
                den = sb(f"den{l}", [P, T, HEADS], F32, scope)
                st = sb(f"gst{l}", [P, T, 6], F32, scope)
                m = sb(f"gm{l}", [P, 5, T], F32, scope)
                R = sb(f"GR2{l}", [P, T, D], F32, scope)
                vec = sb(f"vec{l}", [P, 3, D], F32, scope)
                var_ready, rstd_ready, loaded = sem(f"gvar{l}"), sem(f"grstd{l}"), sem(f"gld{l}")
                with nc.Block() as block:
                    @block.sync
                    def _(sp):
                        if l == 2:
                            for n, a in enumerate(("bias", "gamma", "beta")):
                                sp.dma_start(vec[:, n], row(A["L2_gnn_" + a])).then_inc(loaded, 16)

                    @block.scalar
                    def _(act):
                        if l == 2:
                            act.wait_ge(var_ready, 1)
                            nc.scalar.sqrt(m[:, 3], m[:, 3]).then_inc(rstd_ready, 1)

                    @block.vector
                    def _(dve):
                        link = dve_step.on(dve)
                        tt = nc.vector.tensor_tensor
                        link(nc.vector.tensor_scalar(den[:], SUM[:, :, D:], 1e-9, None, ALU.max))
                        link(nc.vector.reciprocal(den[:], den[:]))
                        link(tt(R[:].rearrange("p t (h d) -> p t h d", h=HEADS),
                                SUM[:, :, 0:D].rearrange("p t (h d) -> p t h d", h=HEADS),
                                den[:].unsqueeze(3).to_broadcast([P, T, HEADS, D // HEADS]), ALU.mult))
                        if l == 2:
                            dve.wait_ge(loaded, 48)
                            link(tt(R[:], R[:], rows(vec[:, 0], T), ALU.add))
                            link(nc.vector.tensor_scalar(R[:], R[:], 0.0, None, ALU.max))
                            layernorm_stats(dve, link, st, m, var_ready, rstd_ready, R)
                            link(tt(R[:], R[:], bc(m[:, 0], D), ALU.mult))
                            link(tt(R[:], R[:], bc(m[:, 1], D), ALU.add))
                            link(tt(R[:], R[:], rows(vec[:, 1], T), ALU.mult))
                            link(tt(R[:], R[:], rows(vec[:, 2], T), ALU.add))
                        link(tt(X[:], X[:], R[:], ALU.add))

        if stop >= 5:
            free_sems()
            attend(2, A["L2_gnn_W"], A["L2_gnn_attn_l"].rearrange("h d -> (h d)"),
                   A["L2_gnn_attn_r"].rearrange("h d -> (h d)"), False)
        if stop >= 6:
            free_sems()
            attend(3, A["L3_gnn_W"], A["L3_gnn_w_att_src"].rearrange("o h d -> (o h d)"),
                   A["L3_gnn_w_att_dst"].rearrange("o h d -> (o h d)"), True)

        written = sem("written")
        with nc.Block() as block:
            @block.sync
            def _(sp):
                last = N - (T - 1) * P
                sp.dma_start(out[0:(T - 1) * P, :].rearrange("(t p) d -> p t d", p=P), X[:, 0:T - 1, :]).then_inc(written, 16)
                sp.dma_start(out[(T - 1) * P:N, :], X[0:last, T - 1, :]).then_inc(written, 16)
                sp.wait_ge(written, 32)


_INS = ['x', 'src', 'dst', 'edge_attr3_1x1', 'edge_attr_4', 'edge_attr_8', 'L0_gnn_W1', 'L0_gnn_b1', 'L0_gnn_W2',
        'L0_gnn_b2', 'L0_gnn_Wout', 'L0_gnn_bout', 'L1_gnn_w1_s', 'L1_gnn_w1_v', 'L1_gnn_wsc_s', 'L1_gnn_wsc_v',
        'L1_gnn_w2_s', 'L1_gnn_w2_v', 'L1_gnn_fc_w1', 'L1_gnn_fc_w2', 'L1_gnn_fc_w3', 'L1_gnn_g_s', 'L1_gnn_g_v',
        'L2_gnn_W', 'L2_gnn_attn_l', 'L2_gnn_attn_r', 'L2_gnn_bias', 'L2_gnn_gamma', 'L2_gnn_beta', 'L3_gnn_W',
        'L3_gnn_w_att_src', 'L3_gnn_w_att_dst']


def kernel(**inputs):
    import numpy as _np
    import concourse.bacc as _bacc
    from concourse import mybir as _mybir
    from concourse.bass_utils import run_bass_kernel_spmd as _run

    nc = _bacc.Bacc("TRN2", target_bir_lowering=False, num_devices=1)
    arrays, args = {}, {}
    for name in _INS:
        a = _np.ascontiguousarray(inputs[name])
        arrays[f"in_{name}_dram"] = a
        args[name] = nc.dram_tensor(f"in_{name}_dram", a.shape, _mybir.dt.from_np(a.dtype), kind="ExternalInput").ap()
    out = nc.dram_tensor("out_0_dram", (N, D), _mybir.dt.float32, kind="ExternalOutput").ap()
    gnn(nc, args, out)
    r = _run(nc, [arrays], core_ids=[0])
    return r.results[0]["out_0_dram"]
```

```python
from contextlib import ExitStack, contextmanager

import concourse.bass as bass
from concourse import mybir

F32 = mybir.dt.float32
BF16 = mybir.dt.bfloat16
I32 = mybir.dt.int32
U32 = mybir.dt.uint32
ALU = mybir.AluOpType
ACT = mybir.ActivationFunctionType
AX = mybir.AxisListType

P = 128
N = 3125
D = 256
E = 53125
T = -(-N // P)
NP = T * P
C = -(-E // P)
EP = C * P
LASTROW = E - (P - 1) * C
Q = C + T - 1
PAD = NP - 1
QB = 4
QP = Q // QB
CB = 4
CP = C // CB
H = 16
MUL = 64
HEADS = 4
RS = 16
RD = 4
BIG = 1.0e30
FAR = 8192.0
B = 4
EPS = 1e-5


class Steps:

    def __init__(self, sem):
        self.sem, self.n, self.loop = sem, 0, None

    def on(self, eng):
        self.eng = eng
        return self

    def __call__(self, ins):
        ins.then_inc(self.sem, 1)
        self.n += 1
        if self.loop is None:
            self.eng.wait_ge(self.sem, self.n)
        else:
            i, per = self.loop
            self.eng.wait_ge(self.sem, i * per + self.n)

    def run(self, n, body):
        start = self.n
        body(0)
        per = self.n - start
        with self.eng.Fori(1, n, 1) as i:
            self.n, self.loop = start, (i, per)
            body(i)
        self.n, self.loop = start + per * n, None

    def run_ahead(self, n, body):
        start = self.n
        body(0, False)
        per = self.n - start
        with self.eng.Fori(1, n - 1, 1) as i:
            self.n, self.loop = start, (i, per)
            body(i, False)
        self.n, self.loop = start + per * (n - 1), None
        body(n - 1, True)


class Group:

    def __init__(self, i, ng, c):
        self.i, self.ng, self.off, self.slot = i, ng, c // ng, c % ng

    def at(self, per=1, more=0):
        return self.i * (self.ng * per) + ((self.off * self.ng + self.slot) * per + more)

    def lap(self, per=1, more=0):
        return self.i * per + (self.off * per + more)

    def first(self):
        return isinstance(self.i, int) and self.at() == 0


def need(eng, semaphore, value):
    if not isinstance(value, int) or value > 0:
        eng.wait_ge(semaphore, value)


def groups(eng, n, ng, stages, head=None):
    def turn(i, slots):
        for s in slots:
            if head is not None and s == slots[0]:
                head(i, s)
            for lag, step in stages:
                g = Group(i, ng, s - lag)
                if not isinstance(i, int) or 0 <= g.at() < n:
                    step(g)
    for i in range(2):
        turn(i, range(ng))
    with eng.Fori(2, n // ng, 1) as i:
        turn(i, range(ng))
    most = max(lag for lag, _ in stages) + n % ng
    if most:
        turn(n // ng, range(most))


class Links:

    def __init__(self, eng, semaphore, per):
        self.eng, self.sem, self.per = eng, semaphore, per

    def start(self, g):
        self.g, self.k = g, 0
        return self

    def __call__(self, ins):
        self.k += 1
        assert self.k <= self.per
        ins.then_inc(self.sem, 1)
        self.eng.wait_ge(self.sem, self.g.at(self.per, self.k))


def later(i):
    return not (isinstance(i, int) and i == 0)


def gnn(nc, A, out, stop=99):
    with ExitStack() as ctx:
        def sb(name, shape, dt=F32, scope=ctx):
            return scope.enter_context(nc.sbuf_tensor(name, shape, dt))

        def ps(name, shape, dt=F32, scope=ctx):
            return scope.enter_context(nc.psum_tensor(name, shape, dt))

        def bank(name, scope, inner=None, dt=F32):
            b = scope.enter_context(nc.psum_tensor(name, [P, 2048 // (4 if dt == F32 else 2)], dt))
            return b[:] if inner is None else b[:].rearrange("p (n m) -> p n m", m=inner)

        def pair_tiles(k, engine, ng, tiles_of):
            def load(i, s):
                start, n = i * (ng * B) - B, ng * B
                if isinstance(i, int):
                    start, n = max(start, 0), min(n if i else n - B, Q - max(start, 0))
                _, ts = nc.values_load_multi_w_load_instructions(
                    toff[k][0:1, bass.ds(start, n)], engines=(engine,), min_val=0, max_val=T - 1,
                    skip_runtime_bounds_check_because="a pair's tile is one of the T tiles")
                first = 0 if isinstance(i, int) and i == 0 else -B
                for r in range(n):
                    tiles_of[(first + r) % (ng * B)] = ts[r]
            return load

        stage_sems = []

        def sem(name):
            stage_sems.append(nc.alloc_semaphore(name=name))
            return stage_sems[-1]

        def free_sems():
            with nc.Block() as block:
                @block.gpsimd
                def _(pool):
                    nc.clear_and_free_semaphores(stage_sems)
            stage_sems.clear()

        def dram(name, shape, dt=F32):
            return nc.dram_tensor(name, shape, dt, kind="Internal").ap()

        rec_s = dram("rec_s", (EP, RS))
        rec_d = dram("rec_d", (EP, RD))
        taby = dram("taby", (NP, D))
        tabf = [dram("tabf2", (NP, D)), dram("tabf3", (NP, D))]
        tabe = [dram("tabe2", (NP, HEADS)), dram("tabe3", (NP, HEADS))]

        dve_step, act_step, pe_step, pool_step = [
            Steps(ctx.enter_context(nc.semaphore(f"{e}_step"))) for e in ("dve", "act", "pe", "pool")]
        parked = ctx.enter_context(nc.semaphore("parked"))

        def hold(eng):
            eng.sem_inc(parked, 1)

        X = sb("X", [P, T, D])
        ident = sb("ident", [P, P])
        identb = sb("identb", [P, P], BF16)
        ones = sb("ones", [P, P])
        icol = sb("icol", [P, Q])
        unsorted = sb("unsorted", [P, 1], I32)
        tri = sb("tri", [P, B, P], BF16)
        lower = sb("lower", [P, P])
        degs = {k: sb(f"deg_{k}", [P, T]) for k in "sd"}
        dinv = sb("dinv", [P, T])
        dn = sb("dn", [P, T])
        toff = {k: sb(f"toff_{k}", [P, Q], I32) for k in "sd"}
        keyl = {k: sb(f"keyl_{k}", [P, Q]) for k in "sd"}
        S_idx = sb("S_idx", [P, Q], U32)
        S_attr = sb("S_attr", [P, Q, 12])
        D_idx = sb("D_idx", [P, Q], U32)
        D_dist = sb("D_dist", [P, Q])
        D_key = sb("D_key", [P, Q])
        src_i = sb("src_i", [P, C], I32)
        dst_i = sb("dst_i", [P, C], I32)
        fl = {k: {n: sb(f"{n}_{k}", [P, C]) for n in ("key", "lo", "hi")} for k in "sd"}

        ld = sem("ld")
        filled = sem("filled")
        made = sem("made")
        with ExitStack() as scope:
            ti = sb("ti", [P, C], I32, scope)
            ii = sb("ii", [P, Q], I32, scope)
            ip = sb("ip", [P, P], I32, scope)
            ipf = sb("ipf", [P, P], F32, scope)
            with nc.Block() as block:
                @block.sync
                def _(sp):
                    sp.wait_ge(filled, 3)
                    for a, b in ((A["src"], src_i), (A["dst"], dst_i)):
                        sp.dma_start(b[0:P - 1, :], a[0:(P - 1) * C].rearrange("(p c) -> p c", c=C)).then_inc(ld, 16)
                        sp.dma_start(b[P - 1:P, 0:LASTROW], a[(P - 1) * C:E].rearrange("(p c) -> p c", p=1)).then_inc(ld, 16)
                    last = N - (T - 1) * P
                    sp.dma_start(X[:, 0:T - 1, :], A["x"][0:(T - 1) * P, :].rearrange("(t p) d -> p t d", p=P)).then_inc(ld, 16)
                    sp.dma_start(X[0:last, T - 1, :], A["x"][(T - 1) * P:N, :]).then_inc(ld, 16)

                @block.gpsimd
                def _(pool):
                    nc.gpsimd.iota(ii[:], pattern=[[1, Q]], base=0, channel_multiplier=0).then_inc(made, 1)
                    nc.gpsimd.iota(ip[:], pattern=[[0, P]], base=0, channel_multiplier=1).then_inc(made, 1)

                @block.vector
                def _(dve):
                    link = dve_step.on(dve)
                    nc.vector.memset(src_i[:], PAD).then_inc(filled, 1)
                    nc.vector.memset(dst_i[:], PAD).then_inc(filled, 1)
                    nc.vector.memset(X[:, T - 1, :], 0.0).then_inc(filled, 1)
                    nc.vector.memset(ones[:], 1.0)
                    dve.wait_ge(made, 2)
                    link(nc.vector.tensor_copy(icol[:], ii[:]))
                    link(nc.vector.tensor_copy(ipf[:], ip[:]))
                    link(nc.vector.tensor_tensor(ident[:], icol[:, 0:P], ipf[:], ALU.is_equal))
                    link(nc.vector.tensor_copy(identb[:], ident[:]))
                    link(nc.vector.tensor_tensor(lower[:], icol[:, 0:P], ipf[:], ALU.is_gt))
                    for b in range(B):
                        link(nc.vector.tensor_tensor(tri[:, b, :], icol[:, 0:P], ipf[:], ALU.is_ge))
                    link(nc.vector.tensor_scalar(tri[:], tri[:], FAR, None, ALU.mult))
                    dve.wait_ge(ld, 96)
                    for k, a in (("s", src_i), ("d", dst_i)):
                        f = fl[k]
                        link(nc.vector.tensor_copy(f["key"][:], a[:]))
                        link(nc.vector.tensor_scalar(ti[:], a[:], 7, None, ALU.logical_shift_right))
                        link(nc.vector.tensor_copy(f["hi"][:], ti[:]))
                        link(nc.vector.scalar_tensor_tensor(out=f["lo"][:], in0=f["hi"][:], scalar=-float(P),
                                                            in1=f["key"][:], op0=ALU.mult, op1=ALU.add))

        def bc(ap, n):
            return ap.unsqueeze(2).to_broadcast([ap.shape[0], ap.shape[1], n])

        def rows(ap, n):
            return ap.unsqueeze(1).to_broadcast([ap.shape[0], n, ap.shape[1]])

        def one_hots(out, key, q):
            return nc.vector.tensor_tensor(out, rows(icol[:, 0:out.shape[-1]], B), bc(key[:, bass.ds(q, B)], out.shape[-1]),
                                           ALU.is_equal)

        with ExitStack() as scope:
            less = sb("less", [P, C], F32, scope)
            count = sb("count", [P, 2], F32, scope)
            nxt = sb("nxt", [P, 1], F32, scope)
            first, total = bank("first", scope), bank("total", scope)
            shifted, counted, summed = sem("shifted"), sem("counted"), sem("unsorted_summed")
            with nc.Block() as block:
                @block.tensor
                def _(pe):
                    nc.tensor.matmul(first[0:P - 1, 0:1], lhsT=ident[:, 1:P], rhs=fl["d"]["key"][:, 0:1], start=True,
                                     stop=True).then_inc(shifted, 1)
                    pe.wait_ge(counted, 1)
                    nc.tensor.matmul(total[:, 0:2], lhsT=ones[:], rhs=count[:], start=True, stop=True).then_inc(summed, 1)

                @block.vector
                def _(dve):
                    link = dve_step.on(dve)
                    tt = nc.vector.tensor_tensor
                    key = fl["d"]["key"]
                    link(nc.vector.memset(count[:], 0.0))
                    link(nc.vector.memset(less[:], 0.0))
                    link(tt(less[:, 1:C], key[:, 1:C], key[:, 0:C - 1], ALU.is_lt))
                    link(nc.vector.tensor_reduce(count[:, 0:1], less[:], AX.X, ALU.add))
                    dve.wait_ge(shifted, 1)
                    link(tt(count[0:P - 1, 1:2], first[0:P - 1, 0:1], key[0:P - 1, C - 1:C], ALU.is_lt))
                    dve.sem_inc(counted, 1)
                    dve.wait_ge(summed, 1)
                    link(nc.vector.tensor_reduce(nxt[:], total[:, 0:2], AX.X, ALU.add))
                    link(nc.vector.tensor_copy(unsorted[:], nxt[:]))

        def sort(k, scope):
            f = fl[k]
            W, rec = (RS, rec_s) if k == "s" else (RD, rec_d)
            HH = sb(f"HH{k}", [P, T, C + 1], F32, scope)
            R = sb(f"R{k}", [P, C, W], F32, scope)
            NG = 4
            ohlo = sb(f"ohlo{k}", [P, NG, B, P], BF16, scope)
            ohhi = sb(f"ohhi{k}", [P, NG, B, T], F32, scope)
            ohhb = sb(f"ohhb{k}", [P, 2, B, T], BF16, scope)
            base = sb(f"base{k}", [P, 3, T], F32, scope)
            onesc = sb(f"onesc{k}", [P, C + 1], F32, scope)
            raw = sb(f"raw{k}", [P, C, 8], F32, scope) if k == "s" else None
            raw2 = sb(f"raw2{k}", [P, C, 4 if k == "s" else 1], F32, scope)
            banks = ExitStack()
            hp = [bank(f"hp{k}{h}", banks, 32) for h in range(2)]
            oh_ready = [sem(f"oh_ready{k}{h}") for h in range(2)]
            cnt_ready = [sem(f"cnt_ready{k}{h}") for h in range(2)]
            cnt_kept = [sem(f"cnt_kept{k}{h}") for h in range(2)]
            rl, rf = sem(f"rec_loaded{k}"), sem(f"rec_filled{k}")

            with nc.Block() as block:
                @block.sync
                def _(sp):
                    sp.wait_ge(rf, 2 if k == "s" else 1)
                    for a, b in ([(A["edge_attr_8"], raw), (A["edge_attr_4"], raw2)] if k == "s"
                                 else [(A["edge_attr3_1x1"].rearrange("e a b -> e (a b)"), raw2)]):
                        sp.dma_start(b[0:P - 1, :, :], a[0:(P - 1) * C, :].rearrange("(p c) f -> p c f", c=C)).then_inc(rl, 16)
                        sp.dma_start(b[P - 1:P, 0:LASTROW, :], a[(P - 1) * C:E, :].rearrange("(p c) f -> p c f", p=1)).then_inc(rl, 16)

                @block.vector
                def _(dve):
                    link = dve_step.on(dve)
                    nc.vector.memset(raw2[:], 0.0).then_inc(rf, 1)
                    if k == "s":
                        nc.vector.memset(raw[:], 0.0).then_inc(rf, 1)
                    link(nc.vector.memset(onesc[:], 1.0))
                    link(nc.vector.memset(R[:], 0.0))

                    def body(i):
                        for h in range(2):
                            if later(i):
                                dve.wait_ge(cnt_ready[h], i)
                            at = bass.ds(i * (2 * B) + h * B, B)
                            one_hots(ohlo[:, h], f["lo"], i * (2 * B) + h * B).then_inc(oh_ready[h], 1)
                            nc.vector.tensor_tensor(ohhb[:, h], rows(icol[:, 0:T], B), bc(f["hi"][:, at], T),
                                                    ALU.is_equal).then_inc(oh_ready[h], 1)
                    dve_step.run(C // (2 * B), body)
                    dve.wait_ge(rl, 64 if k == "s" else 32)
                    if k == "s":
                        link(nc.vector.tensor_copy(R[:, :, 0:8], raw[:]))
                        link(nc.vector.tensor_copy(R[:, :, 8:12], raw2[:]))
                        link(nc.vector.tensor_copy(R[:, :, 12], fl["d"]["key"][:]))
                        link(nc.vector.tensor_copy(R[:, :, 13], fl["s"]["key"][:]))
                    else:
                        link(nc.vector.tensor_copy(R[:, :, 0], fl["s"]["key"][:]))
                        link(nc.vector.tensor_copy(R[:, :, 1], fl["d"]["key"][:]))
                        link(nc.vector.tensor_copy(R[:, :, 2], raw2[:, :, 0]))

                @block.tensor
                def _(pe):
                    pe_step.on(pe)

                    def body(i):
                        for h in range(2):
                            pe.wait_ge(oh_ready[h], i * 2 + 2)
                            if later(i):
                                pe.wait_ge(cnt_kept[h], i)
                            for b in range(B):
                                mm = nc.tensor.matmul(hp[h][:, b, 0:T], lhsT=ohlo[:, h, b, :], rhs=ohhb[:, h, b, :],
                                                      start=True, stop=True)
                            mm.then_inc(cnt_ready[h], 1)
                    pe_step.run(C // (2 * B), body)

                @block.scalar
                def _(act):
                    act_step.on(act)

                    def body(i):
                        for h in range(2):
                            act.wait_ge(cnt_ready[h], i + 1)
                            hold(act)
                            nc.scalar.copy(HH[:, :, bass.ds(i * (2 * B) + h * B + 1, B)],
                                           hp[h][:, 0:B, 0:T].rearrange("p b t -> p t b")).then_inc(cnt_kept[h], 1)
                    act_step.run(C // (2 * B), body)

            banks.close()
            tot = [bank(f"tot{k}{n}", banks)[:, 0:T] for n in range(2)]
            totals, summed = sem(f"totals{k}"), sem(f"summed{k}")
            with nc.Block() as block:
                @block.vector
                def _(dve):
                    link = dve_step.on(dve)
                    nc.vector.tensor_reduce(degs[k][:], HH[:, :, 1:C + 1], AX.X, ALU.add).then_inc(totals, 1)
                    dve.wait_ge(summed, 2)
                    link(nc.vector.tensor_copy(base[:, 0, :], tot[1]))
                    link(nc.vector.tensor_tensor_scan(base[:, 1, :], onesc[:, 0:T], base[:, 0, :], 0.0, ALU.mult, ALU.add))
                    link(nc.vector.tensor_tensor(base[:, 2, :], base[:, 1, :], base[:, 0, :], ALU.subtract))
                    link(nc.vector.tensor_tensor(HH[:, :, 0], base[:, 2, :], tot[0], ALU.add))

                    def body(i):
                        row = HH[:, bass.ds(i, 1), :].rearrange("p o c -> p (o c)")
                        link(nc.vector.tensor_tensor_scan(row, onesc[:], row, 0.0, ALU.mult, ALU.add))
                    dve_step.run(T, body)

                @block.tensor
                def _(pe):
                    pe.wait_ge(totals, 1)
                    nc.tensor.matmul(tot[0], lhsT=lower[:], rhs=degs[k][:], start=True, stop=True).then_inc(summed, 1)
                    nc.tensor.matmul(tot[1], lhsT=ones[:], rhs=degs[k][:], start=True, stop=True).then_inc(summed, 1)

            banks.close()
            dk = sb(f"dk{k}", [P, NG, B, P], F32, scope)
            eq = sb(f"eq{k}", [P, 2, B, P], F32, scope)
            ohT = sb(f"ohT{k}", [P, NG, B, P], F32, scope)
            pr = sb(f"pr{k}", [P, 2, B, T], F32, scope)
            rk = sb(f"rk{k}", [P, 2, 2, B], F32, scope)
            pos = sb(f"pos{k}", [P, NG, B], U32, scope)
            rst = sb(f"rst{k}", [P, NG, B, W], F32, scope)
            kr = [bank(f"kr{k}{h}", scope, P) for h in range(NG)]
            tp = [bank(f"tpb{k}{h}", scope, P, BF16)[:, 0:B] for h in range(2)]
            Rp = [bank(f"Rp{k}{h}", scope, 32) for h in range(2)]
            hot, keyed, keyrow, turned, hotT, found, parts, placed, staged, copied = [
                sem(f"rank_{n}_{k}") for n in ("hot", "keyed", "keyrow", "turned", "hotT", "found", "parts", "placed", "staged", "copied")]
            landed = [sem(f"landed{k}{h}") for h in range(NG)]
            n_g = C // B

            @contextmanager
            def branch(eng, kind):
                if k == "s":
                    yield
                else:
                    n = nc.values_load(unsorted[0:1, 0:1], engines=(kind,), min_val=0, max_val=EP)
                    with eng.If(n != 0):
                        yield

            with nc.Block() as block:
                @block.sync
                def _(sp):
                    if k == "d":
                        n = nc.values_load(unsorted[0:1, 0:1], engines=(mybir.EngineType.SP,), min_val=0, max_val=EP)
                        with sp.If(n == 0):
                            sp.dma_start(rec.rearrange("(p c) f -> p c f", c=C), R[:]).then_inc(copied, 16)
                            sp.wait_ge(copied, 16)

                @block.vector
                def _(dve):
                    with branch(dve, mybir.EngineType.DVE):
                        tt = nc.vector.tensor_tensor

                        def hots(g):
                            at = bass.ds(g.at(B), B)
                            need(dve, turned, g.at(1, 1 - NG))
                            one_hots(ohlo[:, g.slot], f["lo"], g.at(B)).then_inc(hot, 1)
                            need(dve, keyrow, g.at(1, 1 - NG))
                            tt(dk[:, g.slot], rows(ident[:], B), bc(f["key"][:, at], P), ALU.mult).then_inc(keyed, 1)
                            need(dve, placed, g.at(1, 1 - NG))
                            one_hots(ohhi[:, g.slot], f["hi"], g.at(B)).then_inc(hot, 1)

                        def places(g):
                            at, h = bass.ds(g.at(B), B), g.slot % 2
                            dve.wait_ge(keyrow, g.at(1, 1))
                            tt(eq[:, h], kr[g.slot], bc(f["key"][:, at], P), ALU.is_equal).then_inc(parts, 1)
                            dve.wait_ge(found, g.at(1, 1))
                            dve.wait_ge(hot, g.at(2, 2))
                            tt(pr[:, h], Rp[h][:, 0:B, 0:T], ohhi[:, g.slot], ALU.mult).then_inc(parts, 1)
                            dve.wait_ge(parts, g.at(4, 1))
                            nc.vector.tensor_reduce(rk[:, h, 0], eq[:, h], AX.X, ALU.add).then_inc(parts, 1)
                            dve.wait_ge(parts, g.at(4, 2))
                            nc.vector.tensor_reduce(rk[:, h, 1], pr[:, h], AX.X, ALU.add).then_inc(parts, 1)
                            need(dve, landed[g.slot], g.lap(16 * B))
                            dve.wait_ge(parts, g.at(4, 4))
                            tt(pos[:, g.slot], rk[:, h, 0], rk[:, h, 1], ALU.add).then_inc(placed, 1)
                        groups(dve, n_g, NG, [(0, hots), (2, places)])

                @block.tensor
                def _(pe):
                    with branch(pe, mybir.EngineType.PE):
                        def keys(g):
                            pe.wait_ge(keyed, g.at(1, 1))
                            need(pe, placed, g.at(1, 1 - NG))
                            out = kr[g.slot].rearrange("p b m -> p (b m)")
                            nc.tensor.matmul(out, lhsT=ones[:], rhs=dk[:, g.slot].rearrange("p b m -> p (b m)"),
                                             start=True, stop=False)
                            nc.tensor.matmul(out, lhsT=identb[:], rhs=tri[:].rearrange("p b m -> p (b m)"), start=False,
                                             stop=True).then_inc(keyrow, 1)

                        def turn(g):
                            pe.wait_ge(hot, g.at(2, 1))
                            need(pe, hotT, g.at(1, -1))
                            for b in range(B):
                                mm = nc.tensor.transpose(tp[g.slot % 2][:, b, :], ohlo[:, g.slot, b, :], identb[:])
                            mm.then_inc(turned, 1)

                        def look(g):
                            pe.wait_ge(hotT, g.at(1, 1))
                            need(pe, placed, g.at(1, -1))
                            hold(pe)
                            for b in range(B):
                                mm = nc.tensor.matmul(Rp[g.slot % 2][:, b, 0:T], lhsT=ohT[:, g.slot, b, :],
                                                      rhs=HH[:, :, bass.ds(g.at(B, b), 1)].rearrange("p t o -> p (t o)"),
                                                      start=True, stop=True)
                            mm.then_inc(found, 1)
                        groups(pe, n_g, NG, [(0, turn), (0, keys), (1, look)])

                @block.scalar
                def _(act):
                    with branch(act, mybir.EngineType.Activation):
                        def keep(g):
                            act.wait_ge(turned, g.at(1, 1))
                            need(act, found, g.at(1, 1 - NG))
                            nc.scalar.copy(ohT[:, g.slot], tp[g.slot % 2]).then_inc(hotT, 1)

                        def stage(g):
                            need(act, landed[g.slot], g.lap(16 * B))
                            hold(act)
                            nc.scalar.copy(rst[:, g.slot], R[:, bass.ds(g.at(B), B), :]).then_inc(staged, 1)
                        groups(act, n_g, NG, [(0, keep), (1, stage)])

                @block.gpsimd
                def _(pool):
                    with branch(pool, mybir.EngineType.Pool):
                        def scatter(g):
                            pool.wait_ge(placed, g.at(1, 1))
                            pool.wait_ge(staged, g.at(1, 1))
                            hold(pool)
                            for b in range(B):
                                nc.gpsimd.indirect_dma_start(
                                    rec[:, :], bass.IndirectOffsetOnAxis(ap=pos[:, g.slot, b:b + 1], axis=0),
                                    rst[:, g.slot, b, :], None).then_inc(landed[g.slot], 16)
                        groups(pool, n_g, NG, [(0, scatter)])
                        for h in range(NG):
                            pool.wait_ge(landed[h], 16 * B * (n_g // NG))

        for k in "sd":
            if stop >= 1:
                with ExitStack() as scope:
                    sort(k, scope)

        def pairs(k, scope):
            W, rec, kc = (RS, rec_s, 13) if k == "s" else (RD, rec_d, 1)
            lastk = sb(f"lastk{k}", [CP, CB], F32, scope)
            li = sb(f"li{k}", [CP, CB], I32, scope)
            ci = sb(f"ci{k}", [CP, CB], I32, scope)
            v = sb(f"v{k}", [CP, 3, CB], F32, scope)
            cmp = sb(f"cmp{k}", [CP, CB, Q], F32, scope)
            cq = sb(f"cq{k}", [P, Q], F32, scope)
            cidx = sb(f"cidx{k}", [QP, QB], U32, scope)
            TX = sb(f"TX{k}", [QP, QB, P, W], F32, scope)
            cqp = bank(f"cqp{k}", scope)[:, 0:Q]
            cqi = bank(f"cqi{k}", scope)[0:QP, 0:QB]
            tq = [bank(f"tq{k}{n}", scope)[:, 0:Q] for n in range(2)]
            got, iot, cmpd, cnt, ci_ok, rows_in = [sem(f"{n}{k}") for n in ("got", "iot", "cmpd", "cnt", "ci_ok", "rows_in")]
            fields = ([(c, S_attr[:, :, c]) for c in range(12)] + [(12, S_idx[:]), (13, None)]) if k == "s" \
                else [(0, D_idx[:]), (1, None), (2, D_dist[:])]
            turned, taken = sem(f"fturned{k}"), sem(f"ftaken{k}")
            with nc.Block() as block:
                @block.sync
                def _(sp):
                    last = rec.rearrange("(b p e) f -> p b e f", b=CB, p=CP)
                    for b in range(CB):
                        sp.dma_start(lastk[:, b:b + 1], last[:, b, P - 1, kc:kc + 1],
                                     allow_slow_non_contiguous=True).then_inc(got, 16)

                @block.gpsimd
                def _(pool):
                    nc.gpsimd.iota(ci[:], pattern=[[CP, CB]], base=0, channel_multiplier=1).then_inc(iot, 1)
                    pool.wait_ge(ci_ok, 1)
                    for b in range(QB):
                        nc.gpsimd.indirect_dma_start(
                            TX[:, b].rearrange("p e f -> p (e f)"), None,
                            rec.rearrange("(c e) f -> c (e f)", e=P),
                            bass.IndirectOffsetOnAxis(ap=cidx[:, b:b + 1], axis=0)).then_inc(rows_in, 16)
                    pool.wait_ge(rows_in, 16 * QB)

                @block.vector
                def _(dve):
                    link = dve_step.on(dve)
                    dve.wait_ge(got, 16 * CB)
                    dve.wait_ge(iot, 1)
                    link(nc.vector.tensor_copy(li[:], lastk[:]))
                    link(nc.vector.tensor_scalar(li[:], li[:], 7, None, ALU.logical_shift_right))
                    link(nc.vector.tensor_copy(v[:, 0], li[:]))
                    link(nc.vector.tensor_copy(v[:, 1], ci[:]))
                    link(nc.vector.tensor_tensor(v[:, 2], v[:, 0], v[:, 1], ALU.add))
                    for b in range(CB):
                        nc.vector.tensor_scalar(cmp[:, b], icol[0:CP, :], v[:, 2, b:b + 1], None,
                                                ALU.is_gt).then_inc(cmpd, 1)
                    dve.wait_ge(cnt, 2)
                    nc.vector.tensor_copy(cidx[:], cqi).then_inc(ci_ok, 1)
                    link(nc.vector.tensor_copy(cq[:], cqp))
                    link(nc.vector.tensor_tensor(cq[:], icol[:], cq[:], ALU.subtract))
                    link(nc.vector.tensor_copy(toff[k][:], cq[:]))
                    for n, (c, dest) in enumerate(fields):
                        dve.wait_ge(turned, n + 1)
                        if dest is None:
                            if k == "d":
                                link(nc.vector.tensor_copy(D_key[:], tq[n % 2]))
                            nc.vector.scalar_tensor_tensor(out=keyl[k][:], in0=cq[:], scalar=-float(P),
                                                           in1=tq[n % 2], op0=ALU.mult, op1=ALU.add).then_inc(taken, 1)
                        else:
                            nc.vector.tensor_copy(dest, tq[n % 2]).then_inc(taken, 1)

                @block.tensor
                def _(pe):
                    pe.wait_ge(cmpd, CB)
                    for b in range(CB):
                        mm = nc.tensor.matmul(cqp, lhsT=ones[0:CP, :], rhs=cmp[:, b], start=(b == 0), stop=(b == CB - 1))
                    mm.then_inc(cnt, 1)
                    for j in range(QB):
                        for b in range(CB):
                            mm = nc.tensor.matmul(cqi[:, j:j + 1], lhsT=cmp[:, b, j * QP:(j + 1) * QP],
                                                  rhs=ones[0:CP, 0:1], start=(b == 0), stop=(b == CB - 1))
                    mm.then_inc(cnt, 1)
                    pe.wait_ge(rows_in, 16 * QB)
                    for n, (c, dest) in enumerate(fields):
                        if n >= 2:
                            pe.wait_ge(taken, n - 1)
                        for j in range(QB):
                            mm = nc.tensor.transpose(tq[n % 2][:, j * QP:(j + 1) * QP], TX[:, j, :, c],
                                                     ident[0:QP, 0:QP])
                        mm.then_inc(turned, 1)

        for k in "sd":
            if stop >= 2:
                with ExitStack() as scope:
                    pairs(k, scope)

        def layernorm_stats(dve, link, st, m, var_ready, rstd_ready, X=X):
            def body(t):
                link(nc.vector.bn_stats(st[:, bass.ds(t, 1), :].rearrange("p o s -> p (o s)"),
                                        X[:, bass.ds(t, 1), :].rearrange("p o d -> p (o d)")))
            dve_step.run(T, body)
            tt = nc.vector.tensor_tensor
            link(tt(m[:, 2], st[:, :, 1], st[:, :, 4], ALU.subtract))
            link(tt(m[:, 2], m[:, 2], m[:, 2], ALU.mult))
            link(tt(m[:, 3], st[:, :, 2], st[:, :, 5], ALU.add))
            link(nc.vector.tensor_scalar(m[:, 3], m[:, 3], 1.0 / D, None, ALU.mult))
            link(nc.vector.scalar_tensor_tensor(out=m[:, 3], in0=m[:, 2], scalar=0.25, in1=m[:, 3],
                                                op0=ALU.mult, op1=ALU.add))
            nc.vector.tensor_scalar(m[:, 3], m[:, 3], EPS, None, ALU.add).then_inc(var_ready, 1)
            link(tt(m[:, 4], st[:, :, 1], st[:, :, 4], ALU.add))
            dve.wait_ge(rstd_ready, 1)
            link(nc.vector.reciprocal(m[:, 0], m[:, 3]))
            link(nc.vector.scalar_tensor_tensor(out=m[:, 1], in0=m[:, 4], scalar=-0.5, in1=m[:, 0],
                                                op0=ALU.mult, op1=ALU.mult))

        TB = 5

        def tiles(name, fill, K, turns, project, post, before=None, after=None, loads=None, norm=False, w=D, nt=None):
            with ExitStack() as scope:
                nt = nt or (len(turns(X[:, 0, :])) if w == D else 1)
                st = [sb(f"st{name}{k}", [P, w], F32, scope) for k in range(TB)]
                hT = [sb(f"hT{name}{k}", [K, nt, P], F32, scope) for k in range(TB)]
                bst = sb(f"bst{name}", [P, T, 6], F32, scope)
                m = sb(f"m{name}", [P, 5, T], F32, scope)
                tp = [bank(f"tp{name}{k}", scope, P) for k in range(3)]
                op = [bank(f"op{name}{k}", scope) for k in range(3)]
                var_ready, rstd_ready = sem(f"var_ready{name}"), sem(f"rstd_ready{name}")
                loaded, stats, filled, turned, copied, product, taken, stored = [
                    sem(f"{n}{name}") for n in ("loaded", "stats", "filled", "turned", "copied", "product", "taken", "stored")]
                with nc.Block() as block:
                    @block.sync
                    def _(sp):
                        for a, b in loads or []:
                            sp.dma_start(a, b, allow_slow_non_contiguous=True).then_inc(loaded, 16)
                        if after is not None:
                            sp.wait_ge(taken, T)
                            n = after(sp, stored)
                            sp.wait_ge(stored, 16 * n)

                    @block.vector
                    def _(dve):
                        link = dve_step.on(dve)
                        if norm:
                            layernorm_stats(dve, link, bst, m, var_ready, rstd_ready)
                        if loads:
                            dve.wait_ge(loaded, 16 * len(loads))
                        if before is not None:
                            before(dve, link)
                        nc.vector.memset(bst[:, 0, 0:1], 0.0).then_inc(stats, 1)

                        def body(i):
                            for k in range(TB):
                                dve.wait_ge(product, i * TB + (k + 1))
                                post(dve, link, i * TB + k, op[k % 3]).then_inc(taken, 1)
                        dve_step.run(T // TB, body)

                    @block.scalar
                    def _(act):
                        act_step.on(act)
                        if norm:
                            act.wait_ge(var_ready, 1)
                            nc.scalar.sqrt(m[:, 3], m[:, 3]).then_inc(rstd_ready, 1)
                        act.wait_ge(stats, 1)

                        def body(i):
                            for k in range(TB):
                                fill(i * TB + k, st[k], m).then_inc(filled, 1)
                            for k in range(TB):
                                act.wait_ge(turned, i * TB + (k + 1))
                                if later(i):
                                    act.wait_ge(product, i * TB + (k + 1 - TB))
                                nc.scalar.copy(hT[k][:], tp[k % 3][0:K, 0:nt, :]).then_inc(copied, 1)
                        act_step.run(T // TB, body)

                    @block.tensor
                    def _(pe):
                        pe_step.on(pe)
                        if loads:
                            pe.wait_ge(loaded, 16 * len(loads))
                        pe.wait_ge(stats, 1)

                        def turn(i, k):
                            pe.wait_ge(filled, i * TB + (k + 1))
                            if later(i) or k >= 2:
                                pe.wait_ge(copied, i * TB + (k - 1))
                            hold(pe)
                            for j, piece in enumerate(turns(st[k][:])):
                                mm = nc.tensor.transpose(tp[k % 3][0:K, j, :], piece, ident[:])
                            mm.then_inc(turned, 1)

                        def multiply(i, k):
                            pe.wait_ge(copied, i * TB + (k + 1))
                            if later(i) or k >= 2:
                                pe.wait_ge(taken, i * TB + (k - 1))
                            project(hT[k], op[k % 3]).then_inc(product, 1)

                        def body(i):
                            for k in range(TB):
                                turn(i, k)
                                if k:
                                    multiply(i, k - 1)
                            multiply(i, TB - 1)
                        pe_step.run(T // TB, body)

        def tile(a, t):
            return a[:, bass.ds(t, 1), :].rearrange("p o d -> p (o d)")

        def normed(t, st, m):
            return nc.scalar.activation(st[:], tile(X, t), ACT.Relu, bias=m[:, 1, bass.ds(t, 1)],
                                        scale=m[:, 0, bass.ds(t, 1)])

        def two(W):
            def project(hT, o):
                m = W.shape[-1]
                nc.tensor.matmul(o[:, 0:m], lhsT=hT[:, 0, :], rhs=W[:, 0, :], start=True, stop=False)
                return nc.tensor.matmul(o[:, 0:m], lhsT=hT[:, 1, :], rhs=W[:, 1, :], start=False, stop=True)
            return project

        def row(a):
            return a.unsqueeze(0).to_broadcast([P, a.shape[0]])

        def halves(st):
            return [st[:, 0:P], st[:, P:D]]

        def conv(n, g, hout, bias, lo, hi):
            with ExitStack() as scope:
                NG = 4
                hot = sb(f"chot{n}", [P, NG, B, P], BF16, scope)
                hotT = sb(f"chotT{n}", [P, NG, B, P], F32, scope)
                G = sb(f"G{n}", [P, NG, B, H], F32, scope)
                ohlo = sb(f"cohlo{n}", [P, NG, B, P], F32, scope)
                ohhi = sb(f"cohhi{n}", [P, NG, B, T], F32, scope)
                V = sb(f"V{n}", [P, NG, B, T, H], F32, scope)
                acc = bank(f"acc{n}", scope)[:, 0:T * H]
                tp = [bank(f"ctp{n}{h}", scope, P, BF16)[:, 0:B] for h in range(2)]
                gp = [bank(f"cgp{n}{h}", scope, H) for h in range(4)]
                made, turned, kept, fetched, got, mades, spread, summed = [
                    sem(f"c{x}{n}") for x in ("made", "turned", "kept", "fetched", "got", "mades", "spread", "summed")]
                table = g
                with nc.Block() as block:
                    @block.vector
                    def _(dve):
                        link = dve_step.on(dve)
                        tt = nc.vector.tensor_tensor

                        def hots(g):
                            need(dve, turned, g.at(1, 1 - NG))
                            one_hots(hot[:, g.slot], keyl["s"], g.at(B)).then_inc(made, 1)
                            need(dve, summed, g.at(1, 1 - NG))
                            one_hots(ohhi[:, g.slot], hi, g.at(B)).then_inc(mades, 1)
                            one_hots(ohlo[:, g.slot], lo, g.at(B)).then_inc(mades, 1)

                        def spreads(g):
                            dve.wait_ge(got, g.at(1, 1))
                            dve.wait_ge(mades, g.at(2, 1))
                            tt(V[:, g.slot], G[:, g.slot].unsqueeze(2).to_broadcast([P, B, T, H]),
                               ohhi[:, g.slot].unsqueeze(3).to_broadcast([P, B, T, H]), ALU.mult).then_inc(spread, 1)
                        groups(dve, Q // B, NG, [(0, hots), (2, spreads)])
                        dve.wait_ge(summed, Q // B)
                        hv = hout[:].rearrange("p t f -> p (t f)")
                        link(tt(hv, acc, g[:].rearrange("p t f -> p (t f)"), ALU.add))
                        link(tt(hout[:], hout[:], bc(dinv[:], H), ALU.mult))
                        link(tt(hout[:], hout[:], rows(bias[:], T), ALU.add))
                        link(nc.vector.tensor_scalar(hout[:], hout[:], 0.0, None, ALU.max))

                    @block.scalar
                    def _(act):
                        def keep(g):
                            act.wait_ge(turned, g.at(1, 1))
                            need(act, fetched, g.at(1, 1 - NG))
                            nc.scalar.copy(hotT[:, g.slot], tp[g.slot % 2]).then_inc(kept, 1)

                        def take(g):
                            act.wait_ge(fetched, g.at(1, 1))
                            need(act, spread, g.at(1, 1 - NG))
                            nc.scalar.copy(G[:, g.slot], gp[g.slot][:, 0:B, :]).then_inc(got, 1)
                        groups(act, Q // B, NG, [(0, keep), (1, take)])

                    @block.tensor
                    def _(pe):
                        tiles_of = {}

                        def turn(g):
                            pe.wait_ge(made, g.at(1, 1))
                            need(pe, kept, g.at(1, -1))
                            for b in range(B):
                                mm = nc.tensor.transpose(tp[g.slot % 2][:, b, :], hot[:, g.slot, b, :], identb[:])
                            mm.then_inc(turned, 1)

                        def fetch(g):
                            pe.wait_ge(kept, g.at(1, 1))
                            need(pe, got, g.at(1, 1 - NG))
                            hold(pe)
                            for b in range(B):
                                mm = nc.tensor.matmul(gp[g.slot][:, b, :], lhsT=hotT[:, g.slot, b, :],
                                                      rhs=table[:, bass.ds(tiles_of[g.slot * B + b], 1), :]
                                                      .rearrange("p o f -> p (o f)"), start=True, stop=True)
                            mm.then_inc(fetched, 1)

                        def sums(g):
                            pe.wait_ge(spread, g.at(1, 1))
                            pe.wait_ge(mades, g.at(2, 2))
                            for b in range(B):
                                mm = nc.tensor.matmul(acc, lhsT=ohlo[:, g.slot, b, :],
                                                      rhs=V[:, g.slot, b].rearrange("p t f -> p (t f)"),
                                                      start=g.first() and b == 0, stop=False, skip_group_check=True)
                            mm.then_inc(summed, 1)
                        groups(pe, Q // B, NG, [(3, sums), (0, turn), (1, fetch)], pair_tiles("s", mybir.EngineType.PE, NG, tiles_of))

        if stop >= 3:
            free_sems()
            with ExitStack() as scope:
                W1 = sb("W1", [P, 2, H], F32, scope)
                W2 = sb("W2", [H, H], F32, scope)
                WoT = sb("WoT", [H, D], F32, scope)
                b1 = sb("b1", [P, H], F32, scope)
                b2 = sb("b2", [P, H], F32, scope)
                bo = sb("bo", [P, D], F32, scope)
                g = [sb(f"g{n}", [P, T, H], F32, scope) for n in range(2)]
                h16 = [sb(f"h16{n}", [P, T, H], F32, scope) for n in range(2)]
                pre = sb("pre", [P, T, D], F32, scope)

                rooted = sem("rooted")
                dst_lo, dst_hi = sb("dst_lo", [P, Q], F32, scope), sb("dst_hi", [P, Q], F32, scope)
                tile_of_dst = sb("tile_of_dst", [P, Q], U32, scope)

                with nc.Block() as block:
                    @block.vector
                    def _(dve):
                        link = dve_step.on(dve)
                        link(nc.vector.tensor_scalar(tile_of_dst[:], S_idx[:], 7, None, ALU.logical_shift_right))
                        link(nc.vector.tensor_copy(dst_hi[:], tile_of_dst[:]))
                        link(nc.vector.tensor_copy(dst_lo[:], S_idx[:]))
                        link(nc.vector.scalar_tensor_tensor(out=dst_lo[:], in0=dst_hi[:], scalar=-float(P), in1=dst_lo[:],
                                                            op0=ALU.mult, op1=ALU.add))
                        link(nc.vector.tensor_scalar(dinv[:], degs["d"][:], 1.0, None, ALU.add))
                        nc.vector.tensor_scalar(dn[:], degs["s"][:], 1.0, None, ALU.max).then_inc(rooted, 1)
                        dve.wait_ge(rooted, 3)
                        link(nc.vector.reciprocal(dinv[:], dinv[:]))
                        link(nc.vector.reciprocal(dn[:], dn[:]))

                    @block.scalar
                    def _(act):
                        act.wait_ge(rooted, 1)
                        nc.scalar.sqrt(dinv[:], dinv[:]).then_inc(rooted, 1)
                        nc.scalar.sqrt(dn[:], dn[:]).then_inc(rooted, 1)

                def scaled(n):
                    def post(dve, link, t, o):
                        return nc.vector.tensor_scalar(tile(g[n], t), o[:, 0:H], dinv[:, bass.ds(t, 1)], None, ALU.mult)
                    return post

                tiles("a", normed, P, halves, two(W1), scaled(0), norm=True,
                      loads=[(W1[:], A["L0_gnn_W1"].rearrange("(k p) m -> p k m", p=P)), (W2[:], A["L0_gnn_W2"]),
                             (WoT[:], A["L0_gnn_Wout"].rearrange("d h -> h d")), (b1[:], row(A["L0_gnn_b1"])),
                             (b2[:], row(A["L0_gnn_b2"])), (bo[:], row(A["L0_gnn_bout"]))])
                conv(0, g[0], h16[0], b1, dst_lo, dst_hi)
                tiles("b", lambda t, st, m: nc.scalar.copy(st[:], tile(h16[0], t)), H, lambda st: [st],
                      lambda hT, o: nc.tensor.matmul(o[:, 0:H], lhsT=hT[:, 0, :], rhs=W2[:], start=True, stop=True),
                      scaled(1), w=H)
                conv(1, g[1], h16[1], b2, dst_lo, dst_hi)
                tiles("c", lambda t, st, m: nc.scalar.copy(st[:], tile(h16[1], t)), H, lambda st: [st],
                      lambda hT, o: nc.tensor.matmul(o[:, 0:D], lhsT=hT[:, 0, :], rhs=WoT[:], start=True, stop=True),
                      lambda dve, link, t, o: nc.vector.tensor_tensor(tile(pre, t), o[:, 0:D], bo[:], ALU.add), w=H)
                gate = sem("gate")
                with nc.Block() as block:
                    @block.scalar
                    def _(act):
                        nc.scalar.activation(pre[:], pre[:], ACT.Sigmoid).then_inc(gate, 1)

                    @block.vector
                    def _(dve):
                        dve.wait_ge(gate, 1)
                        dve_step.on(dve)(nc.vector.tensor_tensor(X[:], X[:], pre[:], ALU.add))

        def rsqrt_block(v, name, pre=None):
            made, rooted = sem(f"made{name}"), sem(f"rooted{name}")
            with nc.Block() as block:
                @block.vector
                def _(dve):
                    link = dve_step.on(dve)
                    pre(link)
                    dve.sem_inc(made, 1)
                    dve.wait_ge(rooted, 1)
                    link(nc.vector.reciprocal(v, v))

                @block.scalar
                def _(act):
                    act.wait_ge(made, 1)
                    nc.scalar.sqrt(v, v).then_inc(rooted, 1)

        def messages(SUM, fc1, fc2, fc3):
            with ExitStack() as scope:
                NG = 4
                G = sb("Gy", [P, 2, B, D], F32, scope)
                idx = sb("idxy", [P, NG, B], U32, scope)
                at = sb("at", [P, NG, B * 8], F32, scope)
                aT = sb("aT", [B * 8, 2, P], F32, scope)
                s1 = sb("s1", [P, 2, 2 * P], F32, scope)
                s2 = sb("s2", [P, 2, 2 * P], F32, scope)
                oh = sb("oh1", [P, 2, B, P], F32, scope)
                M = sb("M1", [P, 2, B, 8, MUL], F32, scope)
                w = sb("w", [P, 2, B, 4, MUL], F32, scope)
                te = sb("te", [P, B, MUL], F32, scope)
                tb = sb("tb", [P, 2, B, MUL], F32, scope)
                evs = sb("evs", [P, B, 3, MUL], F32, scope)
                wb = [[bank(f"w{h}{n}", scope) for n in range(2)] for h in range(2)]
                sm = [bank(f"sm{n}", scope) for n in range(2)]
                a0, a1 = bank("a0", scope), bank("a1", scope)
                gathered = [sem(f"gathered_y{h}") for h in range(NG)]
                pool_idx = sem("pool_idx")
                attr_st, attr_tp, attr_T, h1_done, s1_done, h2_done, s2_done, w_done, w_kept, parts, msg, summed, added = [
                    sem(f"{x}_y") for x in ("attr_st", "attr_tp", "attr_T", "h1_done", "s1_done", "h2_done", "s2_done",
                                            "w_done", "w_kept", "parts", "msg", "summed", "added")]
                n_g = Q // B
                with nc.Block() as block:
                    @block.gpsimd
                    def _(pool):
                        link = Links(pool, pool_idx, 1)

                        def gather(g):
                            need(pool, gathered[g.slot], g.lap(16 * B))
                            link.start(g)(nc.gpsimd.tensor_copy(idx[:, g.slot], S_idx[:, bass.ds(g.at(B), B)]))
                            need(pool, msg, g.at(5, 5 - 2 * 5))
                            hold(pool)
                            for b in range(B):
                                nc.gpsimd.indirect_dma_start(
                                    G[:, g.slot % 2, b, :], None, taby[:, :],
                                    bass.IndirectOffsetOnAxis(ap=idx[:, g.slot, b:b + 1], axis=0)
                                ).then_inc(gathered[g.slot], 16)
                        groups(pool, n_g, NG, [(0, gather)])

                    @block.scalar
                    def _(act):
                        copy = nc.scalar.copy

                        def stage(g):
                            need(act, attr_tp, g.at(1, 1 - NG))
                            hold(act)
                            copy(at[:, g.slot].rearrange("p (b f) -> p b f", b=B),
                                 S_attr[:, bass.ds(g.at(B), B), 0:8]).then_inc(attr_st, 1)

                        def keep_turned(g):
                            act.wait_ge(attr_tp, g.at(1, 1))
                            need(act, h1_done, g.at(1, -1))
                            copy(aT[:, g.slot % 2], a0[0:B * 8, 0:P]).then_inc(attr_T, 1)

                        def keep_weights(g):
                            need(act, msg, g.at(5, 5 - 2 * 5))
                            for n in range(2):
                                act.wait_ge(w_done, g.at(2, n + 1))
                                w4 = wb[g.slot % 2][n].rearrange("p (b k u) -> p b k u", k=4, u=MUL)
                                copy(w[:, g.slot % 2, 2 * n:2 * n + 2, 1:4:2, :], w4[:, :, 1:4:2, :]).then_inc(w_kept, 1)
                                hold(act)
                                for b in range(2):
                                    nc.scalar.activation(w[:, g.slot % 2, 2 * n + b, 0:4:2, :], w4[:, b, 0:4:2, :], ACT.Copy,
                                                         scale=S_attr[:, bass.ds(g.at(B, 2 * n + b), 1), 8]).then_inc(w_kept, 1)

                        def silu1(g):
                            act.wait_ge(h1_done, g.at(1, 1))
                            need(act, h2_done, g.at(1, -1))
                            nc.scalar.activation(s1[:, g.slot % 2], a0[:, 0:2 * P], ACT.Silu, scale=8.0 ** -0.5).then_inc(s1_done, 1)

                        def silu2(g):
                            act.wait_ge(h2_done, g.at(1, 1))
                            need(act, w_done, g.at(2, -2))
                            nc.scalar.activation(s2[:, g.slot % 2], a1[:, 0:2 * P], ACT.Silu, scale=0.125).then_inc(s2_done, 1)
                        groups(act, n_g, NG, [(0, stage), (1, keep_turned), (4, keep_weights), (1, silu1), (2, silu2)])

                    @block.tensor
                    def _(pe):
                        def turn(g):
                            pe.wait_ge(attr_st, g.at(1, 1))
                            need(pe, s1_done, g.at(1))
                            hold(pe)
                            nc.tensor.transpose(a0[0:B * 8, 0:P], at[:, g.slot], ident[:]).then_inc(attr_tp, 1)

                        def layer1(g):
                            pe.wait_ge(attr_T, g.at(1, 1))
                            hold(pe)
                            for j in range(2):
                                mm = nc.tensor.matmul(a0[:, j * P:(j + 1) * P], lhsT=fc1[:, j], rhs=aT[:, g.slot % 2],
                                                      start=True, stop=True)
                            mm.then_inc(h1_done, 1)

                        def layer2(g):
                            pe.wait_ge(s1_done, g.at(1, 1))
                            need(pe, s2_done, g.at(1))
                            hold(pe)
                            nc.tensor.matmul(a1[:, 0:2 * P], lhsT=fc2[:], rhs=s1[:, g.slot % 2], start=True,
                                             stop=True).then_inc(h2_done, 1)

                        def weights(g):
                            pe.wait_ge(s2_done, g.at(1, 1))
                            need(pe, w_kept, g.at(6, 6 - 2 * 6))
                            for n in range(2):
                                nc.tensor.matmul(wb[g.slot % 2][n], lhsT=s2[:, g.slot % 2, n * P:(n + 1) * P],
                                                 rhs=fc3[:], start=True, stop=True).then_inc(w_done, 1)

                        def sums(bs):
                            def step(g):
                                need(pe, msg, g.at(5, 5))
                                for b in bs:
                                    need(pe, added, g.at(B, b - 1))
                                    nc.tensor.matmul(sm[b % 2], lhsT=oh[:, g.slot % 2, b, :],
                                                     rhs=M[:, g.slot % 2, b].rearrange("p k u -> p (k u)"), start=True,
                                                     stop=True).then_inc(summed, 1)
                            return step
                        groups(pe, n_g, NG, [(0, turn), (4, sums((0, 1))), (0, layer1), (4, sums((2, 3))), (1, layer2), (2, weights)])

                    @block.vector
                    def _(dve):
                        mul = ALU.mult
                        tt = nc.vector.tensor_tensor
                        tiles_of = {}
                        dve_step.on(dve)(nc.vector.memset(SUM[:], 0.0))

                        def add(g, b):
                            r = g.slot * B + b
                            acc = SUM[:, bass.ds(tiles_of[r], 1), :].rearrange("p o f -> p (o f)")
                            need(dve, added, g.at(B, b))
                            dve.wait_ge(summed, g.at(B, b + 1))
                            tt(acc, acc, sm[b % 2], ALU.add).then_inc(added, 1)

                        def messages_of(g):
                            h = g.slot % 2
                            at_q = bass.ds(g.at(B), B)
                            sh1 = S_attr[:, at_q, 9:12].unsqueeze(3).to_broadcast([P, B, 3, MUL])
                            es = G[:, h, :, 0:MUL]
                            ev = G[:, h, :, MUL:D].rearrange("p b (d u) -> p b d u", u=MUL)
                            old = None if g.first() else Group(g.i, NG, g.off * NG + g.slot - 1)

                            def add_old(b):
                                if old is not None:
                                    add(old, b)
                            need(dve, summed, g.at(B, B - 2 * B))
                            one_hots(oh[:, h], keyl["s"], g.at(B)).then_inc(msg, 1)
                            dve.wait_ge(gathered[g.slot], g.lap(16 * B, 16 * B))
                            tt(evs[:], ev, sh1, mul).then_inc(parts, 1)
                            add_old(0)
                            dve.wait_ge(parts, g.at(4, 1))
                            tt(te[:], evs[:, :, 0], evs[:, :, 1], ALU.add).then_inc(parts, 1)
                            dve.wait_ge(w_kept, g.at(6, 6))
                            tt(tb[:, 0], w[:, h, :, 1, :], es, mul).then_inc(parts, 1)
                            dve.wait_ge(parts, g.at(4, 2))
                            tt(tb[:, 1], te[:], evs[:, :, 2], ALU.add).then_inc(parts, 1)
                            add_old(1)
                            tt(M[:, h, :, 0, :], w[:, h, :, 0, :], es, mul).then_inc(msg, 1)
                            dve.wait_ge(parts, g.at(4, 3))
                            tt(M[:, h, :, 2:8:2, :], tb[:, 0].unsqueeze(2).to_broadcast([P, B, 3, MUL]), sh1, mul).then_inc(msg, 1)
                            add_old(2)
                            tt(M[:, h, :, 3:8:2, :], w[:, h, :, 2:3, :].to_broadcast([P, B, 3, MUL]), ev, mul).then_inc(msg, 1)
                            dve.wait_ge(parts, g.at(4, 4))
                            tt(M[:, h, :, 1, :], w[:, h, :, 3, :], tb[:, 1], mul).then_inc(msg, 1)
                            add_old(3)
                        groups(dve, n_g, NG, [(0, messages_of)], pair_tiles("s", mybir.EngineType.DVE, NG, tiles_of))
                        for b in range(B):
                            add(Group(n_g // NG, NG, n_g % NG - 1), b)
                        dve.wait_ge(added, Q)

        if stop >= 4:
            free_sems()
            with ExitStack() as scope:
                w1 = [sb(f"w1{n}", [MUL, 2 * MUL], F32, scope) for n in "sv"]
                w2 = [sb(f"w2{n}", [2 * MUL, MUL], F32, scope) for n in "sv"]
                fc1 = sb("fc1", [B * 8, 2, P], F32, scope)
                fc2 = sb("fc2", [P, P], F32, scope)
                fc3 = sb("fc3", [P, 2 * 4 * MUL], F32, scope)
                cleared = sem("fc_cleared")
                with nc.Block() as block:
                    @block.vector
                    def _(dve):
                        for a in (fc1, fc2, fc3):
                            nc.vector.memset(a[:], 0.0).then_inc(cleared, 1)
                        dve.wait_ge(cleared, 3)
                gsv = sb("gsv", [P, 2, MUL], F32, scope)
                SC = sb("SC", [P, T, D], F32, scope)
                SUM = sb("SUM", [P, T, 8 * MUL], F32, scope)
                with ExitStack() as inner:
                    Y = sb("Y", [P, T, D], F32, inner)

                    def y_project(hT, o):
                        for j in range(4):
                            mm = nc.tensor.matmul(o[:, j * 2 * MUL:(j + 1) * 2 * MUL], lhsT=hT[:, j, :],
                                                  rhs=w1[min(j, 1)][:], start=True, stop=True)
                        return mm

                    def y_post(dve, link, t, o):
                        o4 = o.rearrange("p (j k u) -> p j k u", k=2, u=MUL)
                        link(nc.vector.tensor_copy(tile(Y, t).rearrange("p (j u) -> p j u", u=MUL), o4[:, :, 0, :]))
                        return nc.vector.tensor_scalar(tile(SC, t).rearrange("p (j u) -> p j u", u=MUL), o4[:, :, 1, :],
                                                       MUL ** -0.5, None, ALU.mult)

                    def y_store(sp, s):
                        sp.dma_start(taby.rearrange("(t p) f -> p t f", p=P), Y[:]).then_inc(s, 16)
                        return 1

                    pre = "L1_gnn_"
                    tiles("d", normed, MUL, lambda st: [st[:, 0:MUL]] + [st[:, MUL + d:D:3] for d in range(3)],
                          y_project, y_post, after=y_store, norm=True,
                          loads=[(w1[0][:, 0:MUL], A[pre + "w1_s"]), (w1[0][:, MUL:], A[pre + "wsc_s"]),
                                 (w1[1][:, 0:MUL], A[pre + "w1_v"]), (w1[1][:, MUL:], A[pre + "wsc_v"]),
                                 (w2[0][:], A[pre + "w2_s"]), (w2[1][:], A[pre + "w2_v"]),
                                 *[(fc1[b * 8:(b + 1) * 8, b // 2, b % 2 * MUL:(b % 2 + 1) * MUL], A[pre + "fc_w1"])
                                   for b in range(B)],
                                 *[(fc2[h * MUL:(h + 1) * MUL, h * MUL:(h + 1) * MUL], A[pre + "fc_w2"]) for h in range(2)],
                                 *[(fc3[h * MUL:(h + 1) * MUL, h * 4 * MUL:(h + 1) * 4 * MUL], A[pre + "fc_w3"]) for h in range(2)],
                                 (gsv[:, 0], row(A[pre + "g_s"])), (gsv[:, 1], row(A[pre + "g_v"]))])
                messages(SUM, fc1, fc2, fc3)
                O = sb("O", [P, T, D], F32, scope)
                ms = sb("ms", [P, 2, T], F32, scope)
                dns = sb("dns", [P, T], F32, scope)

                def before(dve, link):
                    link(nc.vector.tensor_scalar(dns[:], dn[:], MUL ** -0.5 * MUL ** -0.5 * (2 * MUL) ** -0.5, None, ALU.mult))
                    link(nc.vector.tensor_scalar(w2[0][MUL:, :], w2[0][MUL:, :], 0.5773502691896258, None, ALU.mult))

                def o_project(hT, o):
                    for j in range(4):
                        mm = nc.tensor.matmul(o[:, j * MUL:(j + 1) * MUL], lhsT=hT[:, j, :], rhs=w2[min(j, 1)][:],
                                              start=True, stop=True)
                    return mm

                tiles("e", lambda t, st, m: nc.scalar.copy(st[:], tile(SUM, t)), P,
                      lambda st: [st[:, j * P:(j + 1) * P] for j in range(4)], o_project,
                      lambda dve, link, t, o: nc.vector.scalar_tensor_tensor(
                          out=tile(O, t), in0=o[:, 0:D], scalar=dns[:, bass.ds(t, 1)], in1=tile(SC, t),
                          op0=ALU.mult, op1=ALU.add), before=before, w=8 * MUL, nt=4)

                def mean_squares(link):
                    sq = SUM[:, :, 0:D]
                    link(nc.vector.tensor_tensor(sq, O[:], O[:], ALU.mult))
                    for n, (a, b) in enumerate(((0, MUL), (MUL, D))):
                        link(nc.vector.tensor_reduce(ms[:, n], sq[:, :, a:b], AX.X, ALU.add))
                        link(nc.vector.tensor_scalar(ms[:, n], ms[:, n], 1.0 / (b - a), EPS, ALU.mult, ALU.add))

                rsqrt_block(ms[:], "rms", mean_squares)
                with nc.Block() as block:
                    @block.vector
                    def _(dve):
                        link = dve_step.on(dve)
                        for n, (a, b) in enumerate(((0, MUL), (MUL, D))):
                            link(nc.vector.tensor_tensor(O[:, :, a:b], O[:, :, a:b], bc(ms[:, n], b - a), ALU.mult))
                            for j in range(a // MUL, b // MUL):
                                o = O[:, :, j * MUL:(j + 1) * MUL]
                                x = X[:, :, 0:MUL] if j == 0 else X[:, :, MUL + j - 1:D:3]
                                link(nc.vector.tensor_tensor(o, o, rows(gsv[:, n], T), ALU.mult))
                                link(nc.vector.tensor_tensor(x, x, o, ALU.add))

        def attend(l, W, al, ar, dist):
            n_it = Q // (2 * B)
            outer = ExitStack()
            with outer:
                EX = sb(f"EX{l}", [P, Q, HEADS], F32, outer)
                EA = sb(f"EA{l}", [P, Q, HEADS], F32, outer) if dist else EX
                with ExitStack() as scope:
                    wt = sb(f"wt{l}", [P, 2, D], F32, scope)
                    attn = sb(f"attn{l}", [P, 2, D], F32, scope)
                    el = sb(f"el{l}", [P, T, 2, HEADS], F32, scope)
                    elt = sb(f"elt{l}", [P, T, HEADS], F32, scope)
                    ert = sb(f"ert{l}", [P, T, HEADS], F32, scope)
                    EL = sb(f"EL{l}", [P, Q, HEADS], F32, scope)
                    ER = sb(f"ER{l}", [P, Q, HEADS], F32, scope)
                    with ExitStack() as inner:
                        F = sb(f"F{l}", [P, T, D], F32, inner)
                        fa = sb(f"fa{l}", [P, 2, D], F32, inner)

                        def post(dve, link, t, o):
                            link(nc.vector.tensor_copy(tile(F, t), o[:, 0:D]))
                            link(nc.vector.tensor_tensor(fa[:], tile(F, t).unsqueeze(1).to_broadcast([P, 2, D]), attn[:], ALU.mult))
                            return nc.vector.tensor_reduce(
                                el[:, bass.ds(t, 1)].rearrange("p o k h -> p (o k h)"),
                                fa[:].rearrange("p k (h d) -> p (k h) d", h=HEADS), AX.X, ALU.add)

                        def store(sp, s):
                            sp.dma_start(tabf[l - 2].rearrange("(t p) f -> p t f", p=P), F[:]).then_inc(s, 16)
                            return 1

                        tiles(f"f{l}", normed, P, halves, two(wt), post, after=store, norm=True,
                              loads=[(wt[:], W.rearrange("(k p) m -> p k m", p=P)), (attn[:, 0], row(al)), (attn[:, 1], row(ar))])
                    logits(l, el, elt, ert, EL, ER)
                    weights_of_edges(l, EL, ER, EX, EA, dist)
                SUM = sb(f"SUM{l}", [P, T, D + HEADS], F32, outer)
                with ExitStack() as scope:
                    NG = 5
                    SUM2 = sb(f"SUM2{l}", [P, T, D + HEADS], F32, scope)
                    G = sb(f"G{l}", [P, NG, B, D], F32, scope)
                    idx = sb(f"idx{l}", [P, NG, B], U32, scope)
                    oh = sb(f"oh{l}", [P, NG, B, P], F32, scope)
                    M = sb(f"M{l}", [P, NG, B, D + HEADS], F32, scope)
                    sm = [bank(f"sm{l}{n}", scope)[:, 0:D + HEADS] for n in range(NG)]
                    gathered = [sem(f"gathered{l}{h}") for h in range(NG)]
                    staged, msg, summed, added, cleared = [
                        sem(f"{x}{l}") for x in ("staged", "msg", "summed", "added", "cleared")]
                    with nc.Block() as block:
                        @block.scalar
                        def _(act):
                            def stage(g):
                                need(act, msg, g.at(3, 3 - 3 * NG))
                                hold(act)
                                nc.scalar.copy(idx[:, g.slot], D_idx[:, bass.ds(g.at(B), B)]).then_inc(staged, 1)
                            groups(act, Q // B, NG, [(0, stage)])

                        @block.gpsimd
                        def _(pool):
                            def gather(g):
                                need(pool, staged, g.at(1, 1))
                                hold(pool)
                                for b in range(B):
                                    nc.gpsimd.indirect_dma_start(
                                        G[:, g.slot, b, :], None, tabf[l - 2][:, :],
                                        bass.IndirectOffsetOnAxis(ap=idx[:, g.slot, b:b + 1], axis=0)
                                    ).then_inc(gathered[g.slot], 16)
                            groups(pool, Q // B, NG, [(0, gather)])

                        @block.tensor
                        def _(pe):
                            def sums(g):
                                need(pe, msg, g.at(3, 3))
                                for b in range(B):
                                    need(pe, added, g.at(B, b + 1 - NG))
                                    nc.tensor.matmul(sm[(g.slot * B + b) % NG], lhsT=oh[:, g.slot, b, :], rhs=M[:, g.slot, b],
                                                     start=True, stop=True).then_inc(summed, 1)
                            groups(pe, Q // B, NG, [(0, sums)])

                        @block.vector
                        def _(dve):
                            tt = nc.vector.tensor_tensor
                            nc.vector.memset(SUM[:], 0.0).then_inc(cleared, 1)
                            nc.vector.memset(SUM2[:], 0.0).then_inc(cleared, 1)
                            dve.wait_ge(cleared, 2)
                            tiles_of = {}

                            def message(g):
                                at_q = bass.ds(g.at(B), B)
                                need(dve, summed, g.at(B, B - B * NG))
                                one_hots(oh[:, g.slot], keyl["d"], g.at(B)).then_inc(msg, 1)
                                nc.vector.tensor_copy(M[:, g.slot, :, D:], EX[:, at_q, :]).then_inc(msg, 1)
                                dve.wait_ge(gathered[g.slot], g.lap(16 * B, 16 * B))
                                tt(M[:, g.slot, :, 0:D].rearrange("p b (k d) -> p b k d", k=HEADS),
                                   G[:, g.slot].rearrange("p b (k d) -> p b k d", k=HEADS),
                                   EA[:, at_q, :].unsqueeze(3).to_broadcast([P, B, HEADS, D // HEADS]),
                                   ALU.mult).then_inc(msg, 1)

                            def add(g):
                                for b in range(B):
                                    r = g.slot * B + b
                                    acc = (SUM, SUM2)[b % 2][:, bass.ds(tiles_of[r], 1), :].rearrange("p o f -> p (o f)")
                                    need(dve, added, g.at(B, b - 1))
                                    dve.wait_ge(summed, g.at(B, b + 1))
                                    tt(acc, acc, sm[r % NG], ALU.add).then_inc(added, 1)
                            groups(dve, Q // B, NG, [(0, message), (1, add)],
                                   pair_tiles("d", mybir.EngineType.DVE, NG, tiles_of))
                            dve.wait_ge(added, Q)
                            dve_step.on(dve)(tt(SUM[:], SUM[:], SUM2[:], ALU.add))
                gat_end(l, SUM)

        def logits(l, el, elt, ert, EL, ER):
            with ExitStack() as scope:
                lo = sb(f"llo{l}", [P, Q], F32, scope)
                hi = sb(f"lhi{l}", [P, Q], F32, scope)
                hii = sb(f"lhii{l}", [P, Q], U32, scope)
                NG, ahead = 4, 3
                el3 = sb(f"el3{l}", [P, 3, T, HEADS], BF16, scope)
                er3 = sb(f"er3{l}", [P, T, 3, HEADS], BF16, scope)
                hot_s = sb(f"hot_s{l}", [P, NG, B, P], BF16, scope)
                hot_d = sb(f"hot_d{l}", [P, NG, B, P], BF16, scope)
                ohhi = sb(f"lohhi{l}", [P, NG, B, T], F32, scope)
                hotT = sb(f"hotT{l}", [P, NG, 2 * B, P], BF16, scope)
                pr = sb(f"lpr{l}", [P, NG, B, T * HEADS], F32, scope)
                tp = [bank(f"ltp{l}{h}", scope, P, BF16) for h in range(NG)]
                lp = [bank(f"llp{l}{h}", scope) for h in range(NG)]
                made_s, made_d, turned, copied, looked, picked, taken, split = [
                    sem(f"{x}{l}") for x in ("made_s", "made_d", "lturned", "lcopied", "looked", "picked", "ltaken", "lsplit")]
                NL = B * T * HEADS
                with nc.Block() as block:
                    @block.vector
                    def _(dve):
                        link = dve_step.on(dve)
                        tt = nc.vector.tensor_tensor
                        link(nc.vector.tensor_scalar(hii[:], D_idx[:], 7, None, ALU.logical_shift_right))
                        link(nc.vector.tensor_copy(hi[:], hii[:]))
                        link(nc.vector.tensor_copy(lo[:], D_idx[:]))
                        link(nc.vector.scalar_tensor_tensor(out=lo[:], in0=hi[:], scalar=-float(P), in1=lo[:],
                                                            op0=ALU.mult, op1=ALU.add))
                        link(nc.vector.tensor_copy(elt[:], el[:, :, 0, :]))
                        link(nc.vector.tensor_copy(ert[:], el[:, :, 1, :]))
                        for n in range(3):
                            link(nc.vector.tensor_copy(el3[:, n], elt[:]))
                            link(nc.vector.tensor_copy(er3[:, :, n, :], ert[:]))
                            link(tt(elt[:], elt[:], el3[:, n], ALU.subtract))
                            link(tt(ert[:], ert[:], er3[:, :, n, :], ALU.subtract))
                        dve.sem_inc(split, 1)

                        def pick(g):
                            dve.wait_ge(looked, g.at(1, 1))
                            dve.wait_ge(made_s, g.at(2, 2))
                            tt(pr[:, g.slot].rearrange("p b (t k) -> p b t k", k=HEADS),
                               lp[g.slot][:, 0:NL].rearrange("p (b t k) -> p b t k", b=B, k=HEADS),
                               ohhi[:, g.slot].unsqueeze(3).to_broadcast([P, B, T, HEADS]), ALU.mult).then_inc(picked, 1)

                        def hots(g):
                            need(dve, turned, g.at(1, 1 - NG))
                            one_hots(hot_s[:, g.slot], lo, g.at(B)).then_inc(made_s, 1)
                            one_hots(hot_d[:, g.slot], keyl["d"], g.at(B)).then_inc(made_d, 1)
                            need(dve, picked, g.at(1, 1 - NG))
                            one_hots(ohhi[:, g.slot], hi, g.at(B)).then_inc(made_s, 1)

                        def take(g):
                            at_q = bass.ds(g.at(B), B)
                            nc.vector.tensor_reduce(
                                ER[:, at_q, :], lp[g.slot][:, NL:NL + 3 * B * HEADS].rearrange("p (b n k) -> p b k n", b=B, k=HEADS),
                                AX.X, ALU.add).then_inc(taken, 1)
                            dve.wait_ge(picked, g.at(1, 1))
                            nc.vector.tensor_reduce(EL[:, at_q, :], pr[:, g.slot].rearrange("p b (t k) -> p b k t", k=HEADS),
                                                    AX.X, ALU.add).then_inc(taken, 1)
                        groups(dve, Q // B, NG, [(ahead, pick), (0, hots), (ahead, take)])

                    @block.scalar
                    def _(act):
                        def copy(g):
                            act.wait_ge(turned, g.at(1, 1))
                            need(act, looked, g.at(1, 1 - NG))
                            nc.scalar.copy(hotT[:, g.slot], tp[g.slot]).then_inc(copied, 1)
                        groups(act, Q // B, NG, [(0, copy)])

                    @block.tensor
                    def _(pe):
                        pe.wait_ge(split, 1)
                        tiles_of = {}

                        def turn(g):
                            pe.wait_ge(made_s, g.at(2, 1))
                            pe.wait_ge(made_d, g.at(1, 1))
                            need(pe, copied, g.at(1, 1 - NG))
                            for b in range(B):
                                nc.tensor.transpose(tp[g.slot][:, b, :], hot_s[:, g.slot, b, :], identb[:])
                            for b in range(B):
                                mm = nc.tensor.transpose(tp[g.slot][:, B + b, :], hot_d[:, g.slot, b, :], identb[:])
                            mm.then_inc(turned, 1)

                        def look(g):
                            need(pe, taken, g.at(2, 2 - 2 * NG))
                            pe.wait_ge(copied, g.at(1, 1))
                            hold(pe)
                            o = lp[g.slot]
                            for b in range(B):
                                for n in range(3):
                                    nc.tensor.matmul(o[:, b * T * HEADS:(b + 1) * T * HEADS], lhsT=hotT[:, g.slot, b, :],
                                                     rhs=el3[:, n].rearrange("p t k -> p (t k)"), start=(n == 0), stop=(n == 2))
                            for b in range(B):
                                at = NL + b * 3 * HEADS
                                mm = nc.tensor.matmul(o[:, at:at + 3 * HEADS], lhsT=hotT[:, g.slot, B + b, :],
                                                      rhs=er3[:, bass.ds(tiles_of[g.slot * B + b], 1)]
                                                      .rearrange("p o n k -> p (o n k)"), start=True, stop=True)
                            mm.then_inc(looked, 1)
                        groups(pe, Q // B, NG, [(0, turn), (1, look)], pair_tiles("d", mybir.EngineType.PE, NG, tiles_of))

        def weights_of_edges(l, EL, ER, EX, EA, dist):
            with ExitStack() as scope:
                TE = sb(f"TE{l}", [QP, QB, HEADS, P], F32, scope)
                TK = sb(f"TK{l}", [QP, QB, P], F32, scope)
                pen = sb(f"pen{l}", [QP, QB, P + 1], F32, scope)
                S = sb(f"S{l}", [QP, QB, HEADS, P], F32, scope)
                ends = sb(f"ends{l}", [QP, QB, HEADS], F32, scope)
                LR = sb(f"LR{l}", [HEADS, Q], F32, scope)
                KF = sb(f"KF{l}", [HEADS, Q], F32, scope)
                KL = sb(f"KL{l}", [HEADS, Q], F32, scope)
                pl = sb(f"pl{l}", [HEADS, Q + 1], F32, scope)
                pls = sb(f"pls{l}", [HEADS, Q], F32, scope)
                plb = sb(f"plb{l}", [HEADS, Q], F32, scope)
                GR = sb(f"GR{l}", [HEADS, Q + 2], F32, scope)
                CR = sb(f"CR{l}", [HEADS, Q], F32, scope)
                cin = sb(f"cin{l}", [QP, QB, HEADS], F32, scope)
                MX = sb(f"MX{l}", [P, HEADS, Q], F32, scope)
                ts = sb(f"ts{l}", [P, HEADS, Q], F32, scope)
                z = sb(f"z{l}", [P, Q, HEADS], F32, scope)
                bk = [bank(f"wb{l}{n}", scope) for n in range(2)]
                r_up, r_down = sem(f"r_up{l}"), sem(f"r_down{l}")

                plan = []
                for b in range(QB):
                    plan.append([("T", (b, h), EL) for h in range(HEADS)])
                plan.append([("K", b, None) for b in range(QB)])
                plan.append([("F", b, None) for b in range(QB)])
                plan.append([("L", b, None) for b in range(QB)])
                for way in range(2):
                    plan.append([("E", b, None) for b in range(QB)])
                    plan.append([("C", b, None) for b in range(QB)])
                for h in range(HEADS):
                    plan.append([("M", (b, h), None) for b in range(QB)])

                with nc.Block() as block:
                    @block.tensor
                    def _(pe):
                        for n, work in enumerate(plan):
                            pe.wait_ge(r_down, n + 1)
                            o = bk[n % 2]
                            for what, k, _ in work:
                                if what == "T":
                                    mm = nc.tensor.transpose(o[0:QP, k[1] * P:(k[1] + 1) * P],
                                                             EL[:, k[0] * QP:(k[0] + 1) * QP, k[1]], ident[:])
                                elif what == "K":
                                    mm = nc.tensor.transpose(o[0:QP, k * P:(k + 1) * P], D_key[:, k * QP:(k + 1) * QP], ident[:])
                                elif what in "FL":
                                    e = 0 if what == "F" else P - 1
                                    mm = nc.tensor.matmul(o[0:HEADS, k * QP:(k + 1) * QP],
                                                          lhsT=TK[:, k, e:e + 1].to_broadcast([QP, HEADS]),
                                                          rhs=ident[0:QP, 0:QP], start=True, stop=True)
                                elif what == "E":
                                    mm = nc.tensor.transpose(o[0:HEADS, k * QP:(k + 1) * QP], ends[:, k, :], ident[0:QP, 0:QP])
                                elif what == "C":
                                    mm = nc.tensor.transpose(o[0:QP, k * HEADS:(k + 1) * HEADS], CR[:, k * QP:(k + 1) * QP],
                                                             ident[0:HEADS, 0:HEADS])
                                else:
                                    mm = nc.tensor.transpose(o[:, k[0] * QP:(k[0] + 1) * QP], TE[:, k[0], k[1], :],
                                                             ident[0:QP, 0:QP])
                            mm.then_inc(r_up, 1)

                    @block.vector
                    def _(dve):
                        link = dve_step.on(dve)
                        v = nc.vector
                        tt = v.tensor_tensor
                        done = [0]

                        def go():
                            dve.sem_inc(r_down, 1)

                        def got():
                            done[0] += 1
                            dve.wait_ge(r_up, done[0])
                            return bk[(done[0] - 1) % 2]

                        go()
                        for b in range(QB):
                            o = got()
                            link(v.tensor_copy(TE[:, b].rearrange("p h e -> p (h e)"), o[0:QP, :]))
                            go()
                        link(v.tensor_copy(TK[:].rearrange("p b e -> p (b e)"), got()[0:QP, :]))
                        go()
                        link(v.tensor_copy(KF[:], got()[0:HEADS, 0:Q]))
                        go()
                        link(v.tensor_copy(KL[:], got()[0:HEADS, 0:Q]))
                        link(v.memset(pen[:], 0.0))
                        link(tt(pen[:, :, 1:P], TK[:, :, 1:P], TK[:, :, 0:P - 1], ALU.not_equal))
                        link(v.tensor_scalar(pen[:], pen[:], -BIG, None, ALU.mult))
                        link(v.memset(pl[:], 1.0))
                        link(tt(pl[:, 1:Q], KF[:, 1:Q], KL[:, 0:Q - 1], ALU.not_equal))
                        link(v.tensor_scalar(pl[:], pl[:], -BIG, None, ALU.mult))
                        link(tt(CR[:], KF[:], KL[:], ALU.not_equal))
                        link(v.tensor_scalar(CR[:], CR[:], -BIG, None, ALU.mult))
                        link(tt(pls[:], pl[:, 0:Q], CR[:], ALU.add))
                        link(tt(plb[:], pl[:, 1:Q + 1], CR[:], ALU.add))
                        link(v.memset(GR[:], -BIG))
                        for way in range(2):
                            for b in range(QB):
                                for h in range(HEADS):
                                    if way == 0:
                                        link(v.tensor_tensor_scan(S[:, b, h], pen[:, b, 0:P], TE[:, b, h], -BIG, ALU.add, ALU.max))
                                    else:
                                        link(v.tensor_tensor_scan(S[:, b, h, ::-1], pen[:, b, P:0:-1], TE[:, b, h, ::-1], -BIG,
                                                                  ALU.add, ALU.max))
                            link(v.tensor_copy(ends[:], S[:, :, :, P - 1 if way == 0 else 0]))
                            go()
                            link(v.tensor_copy(LR[:], got()[0:HEADS, 0:Q]))
                            if way == 0:
                                link(v.tensor_tensor_scan(GR[:, 1:Q + 1], pls[:], LR[:], -BIG, ALU.add, ALU.max))
                                link(tt(CR[:], GR[:, 0:Q], pl[:, 0:Q], ALU.add))
                            else:
                                link(v.tensor_tensor_scan(GR[:, Q:0:-1], plb[:, ::-1], LR[:, ::-1], -BIG, ALU.add, ALU.max))
                                link(tt(CR[:], GR[:, 2:Q + 2], pl[:, 1:Q + 1], ALU.add))
                            go()
                            link(v.tensor_copy(cin[:], got()[0:QP, 0:QB * HEADS].rearrange("p (b h) -> p b h", h=HEADS)))
                            for b in range(QB):
                                for h in range(HEADS):
                                    c = cin[:, b, h:h + 1]
                                    if way == 0:
                                        link(v.tensor_tensor_scan(TE[:, b, h], pen[:, b, 0:P], TE[:, b, h], c, ALU.add, ALU.max))
                                    else:
                                        link(v.tensor_tensor_scan(TE[:, b, h, ::-1], pen[:, b, P:0:-1], TE[:, b, h, ::-1], c,
                                                                  ALU.add, ALU.max))
                        go()
                        for h in range(HEADS):
                            link(v.tensor_copy(MX[:, h], got()[:, 0:Q]))
                            if h < HEADS - 1:
                                go()
                        er = ER[:].rearrange("p q h -> p h q")
                        link(tt(MX[:], MX[:], er, ALU.add))
                        link(v.scalar_tensor_tensor(out=ts[:], in0=MX[:], scalar=0.2, in1=MX[:], op0=ALU.mult, op1=ALU.max))
                        link(tt(z[:], EL[:], ER[:], ALU.add))
                        link(v.scalar_tensor_tensor(out=z[:], in0=z[:], scalar=0.2, in1=z[:], op0=ALU.mult, op1=ALU.max))
                        link(tt(z[:], z[:], ts[:].rearrange("p h q -> p q h"), ALU.subtract))
                        dve.sem_inc(r_down, 1)
                        if dist:
                            dve.wait_ge(r_up, len(plan) + 1)
                            link(tt(EA[:], EX[:], bc(D_dist[:], HEADS), ALU.mult))

                    @block.scalar
                    def _(act):
                        act.wait_ge(r_down, len(plan) + 1)
                        nc.scalar.activation(EX[:], z[:], ACT.Exp).then_inc(r_up, 1)

        def gat_end(l, SUM):
            with ExitStack() as scope:
                den = sb(f"den{l}", [P, T, HEADS], F32, scope)
                st = sb(f"gst{l}", [P, T, 6], F32, scope)
                m = sb(f"gm{l}", [P, 5, T], F32, scope)
                R = sb(f"GR2{l}", [P, T, D], F32, scope)
                vec = sb(f"vec{l}", [P, 3, D], F32, scope)
                var_ready, rstd_ready, loaded = sem(f"gvar{l}"), sem(f"grstd{l}"), sem(f"gld{l}")
                with nc.Block() as block:
                    @block.sync
                    def _(sp):
                        if l == 2:
                            for n, a in enumerate(("bias", "gamma", "beta")):
                                sp.dma_start(vec[:, n], row(A["L2_gnn_" + a])).then_inc(loaded, 16)

                    @block.scalar
                    def _(act):
                        if l == 2:
                            act.wait_ge(var_ready, 1)
                            nc.scalar.sqrt(m[:, 3], m[:, 3]).then_inc(rstd_ready, 1)

                    @block.vector
                    def _(dve):
                        link = dve_step.on(dve)
                        tt = nc.vector.tensor_tensor
                        link(nc.vector.tensor_scalar(den[:], SUM[:, :, D:], 1e-9, None, ALU.max))
                        link(nc.vector.reciprocal(den[:], den[:]))
                        link(tt(R[:].rearrange("p t (h d) -> p t h d", h=HEADS),
                                SUM[:, :, 0:D].rearrange("p t (h d) -> p t h d", h=HEADS),
                                den[:].unsqueeze(3).to_broadcast([P, T, HEADS, D // HEADS]), ALU.mult))
                        if l == 2:
                            dve.wait_ge(loaded, 48)
                            link(tt(R[:], R[:], rows(vec[:, 0], T), ALU.add))
                            link(nc.vector.tensor_scalar(R[:], R[:], 0.0, None, ALU.max))
                            layernorm_stats(dve, link, st, m, var_ready, rstd_ready, R)
                            link(tt(R[:], R[:], bc(m[:, 0], D), ALU.mult))
                            link(tt(R[:], R[:], bc(m[:, 1], D), ALU.add))
                            link(tt(R[:], R[:], rows(vec[:, 1], T), ALU.mult))
                            link(tt(R[:], R[:], rows(vec[:, 2], T), ALU.add))
                        link(tt(X[:], X[:], R[:], ALU.add))

        if stop >= 5:
            free_sems()
            attend(2, A["L2_gnn_W"], A["L2_gnn_attn_l"].rearrange("h d -> (h d)"),
                   A["L2_gnn_attn_r"].rearrange("h d -> (h d)"), False)
        if stop >= 6:
            free_sems()
            attend(3, A["L3_gnn_W"], A["L3_gnn_w_att_src"].rearrange("o h d -> (o h d)"),
                   A["L3_gnn_w_att_dst"].rearrange("o h d -> (o h d)"), True)

        written = sem("written")
        with nc.Block() as block:
            @block.sync
            def _(sp):
                last = N - (T - 1) * P
                sp.dma_start(out[0:(T - 1) * P, :].rearrange("(t p) d -> p t d", p=P), X[:, 0:T - 1, :]).then_inc(written, 16)
                sp.dma_start(out[(T - 1) * P:N, :], X[0:last, T - 1, :]).then_inc(written, 16)
                sp.wait_ge(written, 32)


_INS = ['x', 'src', 'dst', 'edge_attr3_1x1', 'edge_attr_4', 'edge_attr_8', 'L0_gnn_W1', 'L0_gnn_b1', 'L0_gnn_W2',
        'L0_gnn_b2', 'L0_gnn_Wout', 'L0_gnn_bout', 'L1_gnn_w1_s', 'L1_gnn_w1_v', 'L1_gnn_wsc_s', 'L1_gnn_wsc_v',
        'L1_gnn_w2_s', 'L1_gnn_w2_v', 'L1_gnn_fc_w1', 'L1_gnn_fc_w2', 'L1_gnn_fc_w3', 'L1_gnn_g_s', 'L1_gnn_g_v',
        'L2_gnn_W', 'L2_gnn_attn_l', 'L2_gnn_attn_r', 'L2_gnn_bias', 'L2_gnn_gamma', 'L2_gnn_beta', 'L3_gnn_W',
        'L3_gnn_w_att_src', 'L3_gnn_w_att_dst']


def kernel(**inputs):
    import numpy as _np
    import concourse.bacc as _bacc
    from concourse import mybir as _mybir
    from concourse.bass_utils import run_bass_kernel_spmd as _run

    nc = _bacc.Bacc("TRN2", target_bir_lowering=False, num_devices=1)
    arrays, args = {}, {}
    for name in _INS:
        a = _np.ascontiguousarray(inputs[name])
        arrays[f"in_{name}_dram"] = a
        args[name] = nc.dram_tensor(f"in_{name}_dram", a.shape, _mybir.dt.from_np(a.dtype), kind="ExternalInput").ap()
    out = nc.dram_tensor("out_0_dram", (N, D), _mybir.dt.float32, kind="ExternalOutput").ap()
    gnn(nc, args, out)
    r = _run(nc, [arrays], core_ids=[0])
    return r.results[0]["out_0_dram"]
```

```python
from contextlib import ExitStack, contextmanager

import concourse.bass as bass
from concourse import mybir

F32 = mybir.dt.float32
BF16 = mybir.dt.bfloat16
I32 = mybir.dt.int32
U32 = mybir.dt.uint32
ALU = mybir.AluOpType
ACT = mybir.ActivationFunctionType
AX = mybir.AxisListType

P = 128
N = 3125
D = 256
E = 53125
T = -(-N // P)
NP = T * P
C = -(-E // P)
EP = C * P
LASTROW = E - (P - 1) * C
Q = C + T - 1
PAD = NP - 1
QB = 4
QP = Q // QB
CB = 4
CP = C // CB
H = 16
MUL = 64
HEADS = 4
RS = 16
RD = 4
BIG = 1.0e30
FAR = 8192.0
B = 4
EPS = 1e-5


class Steps:

    def __init__(self, sem):
        self.sem, self.n, self.loop = sem, 0, None

    def on(self, eng):
        self.eng = eng
        return self

    def note(self, ins):
        ins.then_inc(self.sem, 1)
        self.n += 1

    def __call__(self, ins):
        self.note(ins)
        self.settle()

    def settle(self):
        if self.loop is None:
            self.eng.wait_ge(self.sem, self.n)
        else:
            i, per = self.loop
            self.eng.wait_ge(self.sem, i * per + self.n)

    def run(self, n, body):
        start = self.n
        body(0)
        per = self.n - start
        with self.eng.Fori(1, n, 1) as i:
            self.n, self.loop = start, (i, per)
            body(i)
        self.n, self.loop = start + per * n, None


class Group:

    def __init__(self, i, ng, c):
        self.i, self.ng, self.off, self.slot = i, ng, c // ng, c % ng

    def at(self, per=1, more=0):
        return self.i * (self.ng * per) + ((self.off * self.ng + self.slot) * per + more)

    def lap(self, per=1, more=0):
        return self.i * per + (self.off * per + more)

    def first(self):
        return isinstance(self.i, int) and self.at() == 0


def need(eng, semaphore, value):
    if not isinstance(value, int) or value > 0:
        eng.wait_ge(semaphore, value)


def groups(eng, n, ng, stages, head=None):
    def turn(i, slots):
        for s in slots:
            if head is not None and s == slots[0]:
                head(i, s)
            for lag, step in stages:
                g = Group(i, ng, s - lag)
                if not isinstance(i, int) or 0 <= g.at() < n:
                    step(g)
    for i in range(2):
        turn(i, range(ng))
    with eng.Fori(2, n // ng, 1) as i:
        turn(i, range(ng))
    most = max(lag for lag, _ in stages) + n % ng
    if most:
        turn(n // ng, range(most))


class Links:

    def __init__(self, eng, semaphore, per):
        self.eng, self.sem, self.per = eng, semaphore, per

    def start(self, g):
        self.g, self.k = g, 0
        return self

    def __call__(self, ins):
        self.k += 1
        assert self.k <= self.per
        ins.then_inc(self.sem, 1)
        self.eng.wait_ge(self.sem, self.g.at(self.per, self.k))


def later(i):
    return not (isinstance(i, int) and i == 0)


def gnn(nc, A, out, stop=99):
    with ExitStack() as ctx:
        def sb(name, shape, dt=F32, scope=ctx):
            return scope.enter_context(nc.sbuf_tensor(name, shape, dt))

        def bank(name, scope, inner=None, dt=F32):
            b = scope.enter_context(nc.psum_tensor(name, [P, 2048 // (4 if dt == F32 else 2)], dt))
            return b[:] if inner is None else b[:].rearrange("p (n m) -> p n m", m=inner)

        def pair_tiles(k, engine, ng, tiles_of):
            def load(i, s):
                start, n = i * (ng * B) - B, ng * B
                if isinstance(i, int):
                    start, n = max(start, 0), min(n if i else n - B, Q - max(start, 0))
                _, ts = nc.values_load_multi_w_load_instructions(
                    toff[k][0:1, bass.ds(start, n)], engines=(engine,), min_val=0, max_val=T - 1,
                    skip_runtime_bounds_check_because="a pair's tile is one of the T tiles")
                first = 0 if isinstance(i, int) and i == 0 else -B
                for r in range(n):
                    tiles_of[(first + r) % (ng * B)] = ts[r]
            return load

        stage_sems = []

        def sem(name):
            stage_sems.append(nc.alloc_semaphore(name=name))
            return stage_sems[-1]

        def free_sems():
            with nc.Block() as block:
                @block.gpsimd
                def _(pool):
                    nc.clear_and_free_semaphores(stage_sems)
            stage_sems.clear()

        def dram(name, shape, dt=F32):
            return nc.dram_tensor(name, shape, dt, kind="Internal").ap()

        rec_s = dram("rec_s", (EP, RS))
        rec_d = dram("rec_d", (EP, RD))
        turned_hots = dram("turned_hots", (P, Q // B, 2 * B * P), BF16)
        tab16 = [dram("tab16a", (NP, H)), dram("tab16b", (NP, H))]
        taby = dram("taby", (NP, D))
        tabf = [dram("tabf2", (NP, D)), dram("tabf3", (NP, D))]

        dve_step, act_step, pe_step = [Steps(ctx.enter_context(nc.semaphore(f"{e}_step"))) for e in ("dve", "act", "pe")]
        parked = ctx.enter_context(nc.semaphore("parked"))

        def hold(eng):
            eng.sem_inc(parked, 1)

        X = sb("X", [P, T, D])
        ident = sb("ident", [P, P])
        identb = sb("identb", [P, P], BF16)
        ones = sb("ones", [P, P])
        icol = sb("icol", [P, Q])
        unsorted = sb("unsorted", [P, 1], I32)
        tri = sb("tri", [P, B, P], BF16)
        lower = sb("lower", [P, P])
        degs = {k: sb(f"deg_{k}", [P, T]) for k in "sd"}
        dinv = sb("dinv", [P, T])
        dn = sb("dn", [P, T])
        toff = {k: sb(f"toff_{k}", [P, Q], I32) for k in "sd"}
        keyl = {k: sb(f"keyl_{k}", [P, Q]) for k in "sd"}
        S_idx = sb("S_idx", [P, Q], U32)
        S_attr = sb("S_attr", [P, Q, 12])
        D_idx = sb("D_idx", [P, Q], U32)
        D_dist = sb("D_dist", [P, Q])
        D_key = sb("D_key", [P, Q])
        edges = ExitStack()
        src_i = sb("src_i", [P, C], I32, edges)
        dst_i = sb("dst_i", [P, C], I32, edges)
        fl = {k: {n: sb(f"{n}_{k}", [P, C], F32, edges) for n in ("key", "lo", "hi")} for k in "sd"}

        ld = sem("ld")
        filled = sem("filled")
        made = sem("made")
        with ExitStack() as scope:
            ti = sb("ti", [P, C], I32, scope)
            ii = sb("ii", [P, Q], I32, scope)
            ip = sb("ip", [P, P], I32, scope)
            ipf = sb("ipf", [P, P], F32, scope)
            with nc.Block() as block:
                @block.sync
                def _(sp):
                    sp.wait_ge(filled, 3)
                    for a, b in ((A["src"], src_i), (A["dst"], dst_i)):
                        sp.dma_start(b[0:P - 1, :], a[0:(P - 1) * C].rearrange("(p c) -> p c", c=C)).then_inc(ld, 16)
                        sp.dma_start(b[P - 1:P, 0:LASTROW], a[(P - 1) * C:E].rearrange("(p c) -> p c", p=1)).then_inc(ld, 16)
                    last = N - (T - 1) * P
                    sp.dma_start(X[:, 0:T - 1, :], A["x"][0:(T - 1) * P, :].rearrange("(t p) d -> p t d", p=P)).then_inc(ld, 16)
                    sp.dma_start(X[0:last, T - 1, :], A["x"][(T - 1) * P:N, :]).then_inc(ld, 16)

                @block.gpsimd
                def _(pool):
                    nc.gpsimd.iota(ii[:], pattern=[[1, Q]], base=0, channel_multiplier=0).then_inc(made, 1)
                    nc.gpsimd.iota(ip[:], pattern=[[0, P]], base=0, channel_multiplier=1).then_inc(made, 1)

                @block.vector
                def _(dve):
                    link = dve_step.on(dve)
                    nc.vector.memset(src_i[:], PAD).then_inc(filled, 1)
                    nc.vector.memset(dst_i[:], PAD).then_inc(filled, 1)
                    nc.vector.memset(X[:, T - 1, :], 0.0).then_inc(filled, 1)
                    nc.vector.memset(ones[:], 1.0)
                    dve.wait_ge(made, 2)
                    link(nc.vector.tensor_copy(icol[:], ii[:]))
                    link(nc.vector.tensor_copy(ipf[:], ip[:]))
                    link(nc.vector.tensor_tensor(ident[:], icol[:, 0:P], ipf[:], ALU.is_equal))
                    link(nc.vector.tensor_copy(identb[:], ident[:]))
                    link(nc.vector.tensor_tensor(lower[:], icol[:, 0:P], ipf[:], ALU.is_gt))
                    for b in range(B):
                        link(nc.vector.tensor_tensor(tri[:, b, :], icol[:, 0:P], ipf[:], ALU.is_ge))
                    link(nc.vector.tensor_scalar(tri[:], tri[:], FAR, None, ALU.mult))
                    dve.wait_ge(ld, 96)
                    for k, a in (("s", src_i), ("d", dst_i)):
                        f = fl[k]
                        link(nc.vector.tensor_copy(f["key"][:], a[:]))
                        link(nc.vector.tensor_scalar(ti[:], a[:], 7, None, ALU.logical_shift_right))
                        link(nc.vector.tensor_copy(f["hi"][:], ti[:]))
                        link(nc.vector.scalar_tensor_tensor(out=f["lo"][:], in0=f["hi"][:], scalar=-float(P),
                                                            in1=f["key"][:], op0=ALU.mult, op1=ALU.add))

        def bc(ap, n):
            return ap.unsqueeze(2).to_broadcast([ap.shape[0], ap.shape[1], n])

        def rows(ap, n):
            return ap.unsqueeze(1).to_broadcast([ap.shape[0], n, ap.shape[1]])

        def one_hots(out, key, q):
            return nc.vector.tensor_tensor(out, rows(icol[:, 0:out.shape[-1]], B), bc(key[:, bass.ds(q, B)], out.shape[-1]),
                                           ALU.is_equal)

        with ExitStack() as scope:
            less = sb("less", [P, C], F32, scope)
            count = sb("count", [P, 2], F32, scope)
            nxt = sb("nxt", [P, 1], F32, scope)
            first, total = bank("first", scope), bank("total", scope)
            shifted, counted, summed = sem("shifted"), sem("counted"), sem("unsorted_summed")
            with nc.Block() as block:
                @block.tensor
                def _(pe):
                    nc.tensor.matmul(first[0:P - 1, 0:1], lhsT=ident[:, 1:P], rhs=fl["d"]["key"][:, 0:1], start=True,
                                     stop=True).then_inc(shifted, 1)
                    pe.wait_ge(counted, 1)
                    nc.tensor.matmul(total[:, 0:2], lhsT=ones[:], rhs=count[:], start=True, stop=True).then_inc(summed, 1)

                @block.vector
                def _(dve):
                    link = dve_step.on(dve)
                    tt = nc.vector.tensor_tensor
                    key = fl["d"]["key"]
                    link(nc.vector.memset(count[:], 0.0))
                    link(nc.vector.memset(less[:], 0.0))
                    link(tt(less[:, 1:C], key[:, 1:C], key[:, 0:C - 1], ALU.is_lt))
                    link(nc.vector.tensor_reduce(count[:, 0:1], less[:], AX.X, ALU.add))
                    dve.wait_ge(shifted, 1)
                    link(tt(count[0:P - 1, 1:2], first[0:P - 1, 0:1], key[0:P - 1, C - 1:C], ALU.is_lt))
                    dve.sem_inc(counted, 1)
                    dve.wait_ge(summed, 1)
                    link(nc.vector.tensor_reduce(nxt[:], total[:, 0:2], AX.X, ALU.add))
                    link(nc.vector.tensor_copy(unsorted[:], nxt[:]))

        def sort(k, scope):
            f = fl[k]
            W, rec = (RS, rec_s) if k == "s" else (RD, rec_d)
            steps = dve_step if k == "s" else Steps(sem("sort_steps"))

            @contextmanager
            def branch(eng, kind):
                if k == "s":
                    yield
                else:
                    n = nc.values_load(unsorted[0:1, 0:1], engines=(kind,), min_val=0, max_val=EP)
                    with eng.If(n != 0):
                        yield

            HH = sb(f"HH{k}", [P, T, C + 1], F32, scope)
            R = sb(f"R{k}", [P, C, W], F32, scope)
            NG = 4
            ohlo = sb(f"ohlo{k}", [P, NG, B, P], BF16, scope)
            ohhi = sb(f"ohhi{k}", [P, NG, B, T], F32, scope)
            ohhb = sb(f"ohhb{k}", [P, 2, B, T], BF16, scope)
            base = sb(f"base{k}", [P, 3, T], F32, scope)
            onesc = sb(f"onesc{k}", [P, C + 1], F32, scope)
            raw = sb(f"raw{k}", [P, C, 8], F32, scope) if k == "s" else None
            raw2 = sb(f"raw2{k}", [P, C, 4 if k == "s" else 1], F32, scope)
            banks = ExitStack()
            hp = [bank(f"hp{k}{h}", banks, 32) for h in range(2)]
            oh_ready = [sem(f"oh_ready{k}{h}") for h in range(2)]
            cnt_ready = [sem(f"cnt_ready{k}{h}") for h in range(2)]
            cnt_kept = [sem(f"cnt_kept{k}{h}") for h in range(2)]
            rl, rf, recorded = sem(f"rec_loaded{k}"), sem(f"rec_filled{k}"), sem(f"recorded{k}")

            with nc.Block() as block:
                @block.sync
                def _(sp):
                    sp.wait_ge(rf, 2 if k == "s" else 1)
                    for a, b in ([(A["edge_attr_8"], raw), (A["edge_attr_4"], raw2)] if k == "s"
                                 else [(A["edge_attr3_1x1"].rearrange("e a b -> e (a b)"), raw2)]):
                        sp.dma_start(b[0:P - 1, :, :], a[0:(P - 1) * C, :].rearrange("(p c) f -> p c f", c=C)).then_inc(rl, 16)
                        sp.dma_start(b[P - 1:P, 0:LASTROW, :], a[(P - 1) * C:E, :].rearrange("(p c) f -> p c f", p=1)).then_inc(rl, 16)

                @block.vector
                def _(dve):
                    link = dve_step.on(dve)
                    link(nc.vector.memset(onesc[:], 1.0))

                    def body(i):
                        for h in range(2):
                            if later(i):
                                dve.wait_ge(cnt_ready[h], i)
                            at = bass.ds(i * (2 * B) + h * B, B)
                            one_hots(ohlo[:, h], f["lo"], i * (2 * B) + h * B).then_inc(oh_ready[h], 1)
                            nc.vector.tensor_tensor(ohhb[:, h], rows(icol[:, 0:T], B), bc(f["hi"][:, at], T),
                                                    ALU.is_equal).then_inc(oh_ready[h], 1)
                    with branch(dve, mybir.EngineType.DVE):
                        steps.on(dve).run(C // (2 * B), body)

                @block.gpsimd
                def _(pool):
                    nc.gpsimd.memset(raw2[:], 0.0).then_inc(rf, 1)
                    if k == "s":
                        nc.gpsimd.memset(raw[:], 0.0).then_inc(rf, 1)
                    nc.gpsimd.memset(R[:, :, (14 if k == "s" else 3):], 0.0).then_inc(rf, 1)
                    pool.wait_ge(rf, 3 if k == "s" else 2)

                @block.tensor
                def _(pe):
                    pe_step.on(pe)

                    def body(i):
                        for h in range(2):
                            pe.wait_ge(oh_ready[h], i * 2 + 2)
                            if later(i):
                                pe.wait_ge(cnt_kept[h], i)
                            for b in range(B):
                                mm = nc.tensor.matmul(hp[h][:, b, 0:T], lhsT=ohlo[:, h, b, :], rhs=ohhb[:, h, b, :],
                                                      start=True, stop=True)
                            mm.then_inc(cnt_ready[h], 1)
                    with branch(pe, mybir.EngineType.PE):
                        pe_step.run(C // (2 * B), body)

                @block.scalar
                def _(act):
                    act_step.on(act)

                    def body(i):
                        for h in range(2):
                            act.wait_ge(cnt_ready[h], i + 1)
                            hold(act)
                            nc.scalar.copy(HH[:, :, bass.ds(i * (2 * B) + h * B + 1, B)],
                                           hp[h][:, 0:B, 0:T].rearrange("p b t -> p t b")).then_inc(cnt_kept[h], 1)
                    with branch(act, mybir.EngineType.Activation):
                        act_step.run(C // (2 * B), body)
                    act.wait_ge(rl, 64 if k == "s" else 32)
                    if k == "s":
                        fields = ((R[:, :, 0:8], raw[:]), (R[:, :, 8:12], raw2[:]), (R[:, :, 12], fl["d"]["key"][:]),
                                  (R[:, :, 13], fl["s"]["key"][:]))
                    else:
                        fields = ((R[:, :, 0], fl["s"]["key"][:]), (R[:, :, 1], fl["d"]["key"][:]), (R[:, :, 2], raw2[:, :, 0]))
                    for out, a in fields:
                        nc.scalar.copy(out, a).then_inc(recorded, 1)
                    act.wait_ge(recorded, len(fields))

            banks.close()
            tot = [bank(f"tot{k}{n}", banks)[:, 0:T] for n in range(2)]
            totals, summed = sem(f"totals{k}"), sem(f"summed{k}")
            with nc.Block() as block:
                @block.vector
                def _(dve):
                    with branch(dve, mybir.EngineType.DVE):
                        link = steps.on(dve)
                        nc.vector.tensor_reduce(degs[k][:], HH[:, :, 1:C + 1], AX.X, ALU.add).then_inc(totals, 1)
                        dve.wait_ge(summed, 2)
                        link(nc.vector.tensor_copy(base[:, 0, :], tot[1]))
                        link(nc.vector.tensor_tensor_scan(base[:, 1, :], onesc[:, 0:T], base[:, 0, :], 0.0, ALU.mult, ALU.add))
                        link(nc.vector.tensor_tensor(base[:, 2, :], base[:, 1, :], base[:, 0, :], ALU.subtract))
                        link(nc.vector.tensor_tensor(HH[:, :, 0], base[:, 2, :], tot[0], ALU.add))

                        for t in range(T):
                            row = HH[:, t, :]
                            link.note(nc.vector.tensor_tensor_scan(row, onesc[:], row, 0.0, ALU.mult, ALU.add))
                        link.settle()

                @block.tensor
                def _(pe):
                    with branch(pe, mybir.EngineType.PE):
                        pe.wait_ge(totals, 1)
                        nc.tensor.matmul(tot[0], lhsT=lower[:], rhs=degs[k][:], start=True, stop=True).then_inc(summed, 1)
                        nc.tensor.matmul(tot[1], lhsT=ones[:], rhs=degs[k][:], start=True, stop=True).then_inc(summed, 1)

            banks.close()
            dk = sb(f"dk{k}", [P, NG, B, P], F32, scope)
            eq = sb(f"eq{k}", [P, 2, B, P], F32, scope)
            ohT = sb(f"ohT{k}", [P, NG, B, P], F32, scope)
            pr = sb(f"pr{k}", [P, 2, B, T], F32, scope)
            rk = sb(f"rk{k}", [P, 2, 2, B], F32, scope)
            pos = sb(f"pos{k}", [P, NG, B], U32, scope)
            rst = sb(f"rst{k}", [P, NG, B, W], F32, scope)
            kr = [bank(f"kr{k}{h}", scope, P) for h in range(2)]
            if k == "s":
                dlo = sb("dlo", [P, NG, B, P], BF16, scope)
                dhi = sb("dhi", [P, NG, B, T], BF16, scope)
                dcount = bank("dcount", scope)[:, 0:T]
                dhot, dcounted = sem("dhot"), sem("dcounted")
            tp = [bank(f"tpb{k}{h}", scope, P, BF16)[:, 0:B] for h in range(2)]
            Rp = [bank(f"Rp{k}{h}", scope, 32) for h in range(2)]
            hot, keyed, keyrow, turned, hotT, found, parts, placed, staged, copied = [
                sem(f"rank_{n}_{k}") for n in ("hot", "keyed", "keyrow", "turned", "hotT", "found", "parts", "placed", "staged", "copied")]
            landed = [sem(f"landed{k}{h}") for h in range(NG)]
            n_g = C // B

            with nc.Block() as block:
                @block.sync
                def _(sp):
                    if k == "d":
                        n = nc.values_load(unsorted[0:1, 0:1], engines=(mybir.EngineType.SP,), min_val=0, max_val=EP)
                        with sp.If(n == 0):
                            sp.dma_start(rec.rearrange("(p c) f -> p c f", c=C), R[:]).then_inc(copied, 16)
                            sp.wait_ge(copied, 16)

                @block.vector
                def _(dve):
                    with branch(dve, mybir.EngineType.DVE):
                        tt = nc.vector.tensor_tensor

                        def hots(g):
                            at = bass.ds(g.at(B), B)
                            need(dve, turned, g.at(1, 1 - NG))
                            one_hots(ohlo[:, g.slot], f["lo"], g.at(B)).then_inc(hot, 1)
                            need(dve, keyrow, g.at(1, 1 - NG))
                            tt(dk[:, g.slot], rows(ident[:], B), bc(f["key"][:, at], P), ALU.mult).then_inc(keyed, 1)
                            need(dve, placed, g.at(1, 1 - NG))
                            one_hots(ohhi[:, g.slot], f["hi"], g.at(B)).then_inc(hot, 1)

                        def places(g):
                            at, h = bass.ds(g.at(B), B), g.slot % 2
                            dve.wait_ge(keyrow, g.at(1, 1))
                            tt(eq[:, h], kr[g.slot % 2], bc(f["key"][:, at], P), ALU.is_equal).then_inc(parts, 1)
                            dve.wait_ge(found, g.at(1, 1))
                            dve.wait_ge(hot, g.at(2, 2))
                            tt(pr[:, h], Rp[h][:, 0:B, 0:T], ohhi[:, g.slot], ALU.mult).then_inc(parts, 1)
                            dve.wait_ge(parts, g.at(4, 1))
                            nc.vector.tensor_reduce(rk[:, h, 0], eq[:, h], AX.X, ALU.add).then_inc(parts, 1)
                            dve.wait_ge(parts, g.at(4, 2))
                            nc.vector.tensor_reduce(rk[:, h, 1], pr[:, h], AX.X, ALU.add).then_inc(parts, 1)
                            need(dve, landed[g.slot], g.lap(16 * B))
                            dve.wait_ge(parts, g.at(4, 4))
                            tt(pos[:, g.slot], rk[:, h, 0], rk[:, h, 1], ALU.add).then_inc(placed, 1)

                        def dst_hots(g):
                            need(dve, dcounted, g.at(1, 1 - NG))
                            one_hots(dlo[:, g.slot], fl["d"]["lo"], g.at(B)).then_inc(dhot, 1)
                            one_hots(dhi[:, g.slot], fl["d"]["hi"], g.at(B)).then_inc(dhot, 1)
                        groups(dve, n_g, NG, [(0, hots), (2, places)] + ([(0, dst_hots)] if k == "s" else []))
                        if k == "s":
                            dve.wait_ge(dcounted, n_g)
                            dve_step.on(dve)(nc.vector.tensor_copy(degs["d"][:], dcount))

                @block.tensor
                def _(pe):
                    with branch(pe, mybir.EngineType.PE):
                        def keys(g):
                            pe.wait_ge(keyed, g.at(1, 1))
                            need(pe, placed, g.at(1, -1))
                            out = kr[g.slot % 2].rearrange("p b m -> p (b m)")
                            nc.tensor.matmul(out, lhsT=ones[:], rhs=dk[:, g.slot].rearrange("p b m -> p (b m)"),
                                             start=True, stop=False)
                            nc.tensor.matmul(out, lhsT=identb[:], rhs=tri[:].rearrange("p b m -> p (b m)"), start=False,
                                             stop=True).then_inc(keyrow, 1)

                        def turn(g):
                            pe.wait_ge(hot, g.at(2, 1))
                            need(pe, hotT, g.at(1, -1))
                            for b in range(B):
                                mm = nc.tensor.transpose(tp[g.slot % 2][:, b, :], ohlo[:, g.slot, b, :], identb[:])
                            mm.then_inc(turned, 1)

                        def look(g):
                            pe.wait_ge(hotT, g.at(1, 1))
                            need(pe, placed, g.at(1, -1))
                            hold(pe)
                            for b in range(B):
                                mm = nc.tensor.matmul(Rp[g.slot % 2][:, b, 0:T], lhsT=ohT[:, g.slot, b, :],
                                                      rhs=HH[:, :, bass.ds(g.at(B, b), 1)].rearrange("p t o -> p (t o)"),
                                                      start=True, stop=True)
                            mm.then_inc(found, 1)

                        def dst_count(g):
                            pe.wait_ge(dhot, g.at(2, 2))
                            for b in range(B):
                                mm = nc.tensor.matmul(dcount, lhsT=dlo[:, g.slot, b, :], rhs=dhi[:, g.slot, b, :],
                                                      start=g.first() and b == 0, stop=False, skip_group_check=True)
                            mm.then_inc(dcounted, 1)
                        groups(pe, n_g, NG, [(0, turn), (1, look), (0, keys)] + ([(1, dst_count)] if k == "s" else []))

                @block.scalar
                def _(act):
                    with branch(act, mybir.EngineType.Activation):
                        def keep(g):
                            act.wait_ge(turned, g.at(1, 1))
                            need(act, found, g.at(1, 1 - NG))
                            nc.scalar.copy(ohT[:, g.slot], tp[g.slot % 2]).then_inc(hotT, 1)

                        def stage(g):
                            need(act, landed[g.slot], g.lap(16 * B))
                            hold(act)
                            nc.scalar.copy(rst[:, g.slot], R[:, bass.ds(g.at(B), B), :]).then_inc(staged, 1)
                        groups(act, n_g, NG, [(0, keep), (1, stage)])

                @block.gpsimd
                def _(pool):
                    with branch(pool, mybir.EngineType.Pool):
                        def scatter(g):
                            pool.wait_ge(placed, g.at(1, 1))
                            pool.wait_ge(staged, g.at(1, 1))
                            hold(pool)
                            for b in range(B):
                                nc.gpsimd.indirect_dma_start(
                                    rec[:, :], bass.IndirectOffsetOnAxis(ap=pos[:, g.slot, b:b + 1], axis=0),
                                    rst[:, g.slot, b, :], None).then_inc(landed[g.slot], 16)
                        groups(pool, n_g, NG, [(0, scatter)])
                        for h in range(NG):
                            pool.wait_ge(landed[h], 16 * B * (n_g // NG))

        for k in "sd":
            if stop >= 1:
                with ExitStack() as scope:
                    sort(k, scope)
        edges.close()

        def pairs(k, scope):
            W, rec, kc = (RS, rec_s, 13) if k == "s" else (RD, rec_d, 1)
            lastk = sb(f"lastk{k}", [CP, CB], F32, scope)
            li = sb(f"li{k}", [CP, CB], I32, scope)
            ci = sb(f"ci{k}", [CP, CB], I32, scope)
            v = sb(f"v{k}", [CP, 3, CB], F32, scope)
            cmp = sb(f"cmp{k}", [CP, CB, Q], F32, scope)
            cq = sb(f"cq{k}", [P, Q], F32, scope)
            cidx = sb(f"cidx{k}", [QP, QB], U32, scope)
            TX = sb(f"TX{k}", [QP, QB, P, W], F32, scope)
            cqp = bank(f"cqp{k}", scope)[:, 0:Q]
            cqi = bank(f"cqi{k}", scope)[0:QP, 0:QB]
            tq = [bank(f"tq{k}{n}", scope)[:, 0:Q] for n in range(2)]
            got, iot, cmpd, cnt, ci_ok, rows_in = [sem(f"{n}{k}") for n in ("got", "iot", "cmpd", "cnt", "ci_ok", "rows_in")]
            fields = ([(c, S_attr[:, :, c]) for c in range(12)] + [(12, S_idx[:]), (13, None)]) if k == "s" \
                else [(0, D_idx[:]), (1, None), (2, D_dist[:])]
            turned, taken = sem(f"fturned{k}"), sem(f"ftaken{k}")
            with nc.Block() as block:
                @block.sync
                def _(sp):
                    last = rec.rearrange("(b p e) f -> p b e f", b=CB, p=CP)
                    for b in range(CB):
                        sp.dma_start(lastk[:, b:b + 1], last[:, b, P - 1, kc:kc + 1],
                                     allow_slow_non_contiguous=True).then_inc(got, 16)

                @block.gpsimd
                def _(pool):
                    nc.gpsimd.iota(ci[:], pattern=[[CP, CB]], base=0, channel_multiplier=1).then_inc(iot, 1)
                    pool.wait_ge(ci_ok, 1)
                    for b in range(QB):
                        nc.gpsimd.indirect_dma_start(
                            TX[:, b].rearrange("p e f -> p (e f)"), None,
                            rec.rearrange("(c e) f -> c (e f)", e=P),
                            bass.IndirectOffsetOnAxis(ap=cidx[:, b:b + 1], axis=0)).then_inc(rows_in, 16)
                    pool.wait_ge(rows_in, 16 * QB)

                @block.vector
                def _(dve):
                    link = dve_step.on(dve)
                    dve.wait_ge(got, 16 * CB)
                    dve.wait_ge(iot, 1)
                    link(nc.vector.tensor_copy(li[:], lastk[:]))
                    link(nc.vector.tensor_scalar(li[:], li[:], 7, None, ALU.logical_shift_right))
                    link(nc.vector.tensor_copy(v[:, 0], li[:]))
                    link(nc.vector.tensor_copy(v[:, 1], ci[:]))
                    link(nc.vector.tensor_tensor(v[:, 2], v[:, 0], v[:, 1], ALU.add))
                    for b in range(CB):
                        nc.vector.tensor_scalar(cmp[:, b], icol[0:CP, :], v[:, 2, b:b + 1], None,
                                                ALU.is_gt).then_inc(cmpd, 1)
                    dve.wait_ge(cnt, 2)
                    nc.vector.tensor_copy(cidx[:], cqi).then_inc(ci_ok, 1)
                    link(nc.vector.tensor_copy(cq[:], cqp))
                    link(nc.vector.tensor_tensor(cq[:], icol[:], cq[:], ALU.subtract))
                    link(nc.vector.tensor_copy(toff[k][:], cq[:]))
                    for n, (c, dest) in enumerate(fields):
                        dve.wait_ge(turned, n + 1)
                        if dest is None:
                            if k == "d":
                                link(nc.vector.tensor_copy(D_key[:], tq[n % 2]))
                            nc.vector.scalar_tensor_tensor(out=keyl[k][:], in0=cq[:], scalar=-float(P),
                                                           in1=tq[n % 2], op0=ALU.mult, op1=ALU.add).then_inc(taken, 1)
                        else:
                            nc.vector.tensor_copy(dest, tq[n % 2]).then_inc(taken, 1)

                @block.tensor
                def _(pe):
                    pe.wait_ge(cmpd, CB)
                    for b in range(CB):
                        mm = nc.tensor.matmul(cqp, lhsT=ones[0:CP, :], rhs=cmp[:, b], start=(b == 0), stop=(b == CB - 1))
                    mm.then_inc(cnt, 1)
                    for j in range(QB):
                        for b in range(CB):
                            mm = nc.tensor.matmul(cqi[:, j:j + 1], lhsT=cmp[:, b, j * QP:(j + 1) * QP],
                                                  rhs=ones[0:CP, 0:1], start=(b == 0), stop=(b == CB - 1))
                    mm.then_inc(cnt, 1)
                    pe.wait_ge(rows_in, 16 * QB)
                    for n, (c, dest) in enumerate(fields):
                        if n >= 2:
                            pe.wait_ge(taken, n - 1)
                        for j in range(QB):
                            mm = nc.tensor.transpose(tq[n % 2][:, j * QP:(j + 1) * QP], TX[:, j, :, c],
                                                     ident[0:QP, 0:QP])
                        mm.then_inc(turned, 1)

        for k in "sd":
            if stop >= 2:
                with ExitStack() as scope:
                    pairs(k, scope)

        TB = 5

        def layernorm_stats(dve, link, st, m, var_ready, rstd_ready, X=X):
            def body(i):
                for k in range(TB):
                    ins = nc.vector.bn_stats(st[:, bass.ds(i * TB + k, 1), :].rearrange("p o s -> p (o s)"),
                                             X[:, bass.ds(i * TB + k, 1), :].rearrange("p o d -> p (o d)"))
                    if k < TB - 1:
                        link.note(ins)
                    else:
                        link(ins)
            dve_step.run(T // TB, body)
            tt = nc.vector.tensor_tensor
            link(tt(m[:, 2], st[:, :, 1], st[:, :, 4], ALU.subtract))
            link(tt(m[:, 2], m[:, 2], m[:, 2], ALU.mult))
            link(tt(m[:, 3], st[:, :, 2], st[:, :, 5], ALU.add))
            link(nc.vector.tensor_scalar(m[:, 3], m[:, 3], 1.0 / D, None, ALU.mult))
            link(nc.vector.scalar_tensor_tensor(out=m[:, 3], in0=m[:, 2], scalar=0.25, in1=m[:, 3],
                                                op0=ALU.mult, op1=ALU.add))
            nc.vector.tensor_scalar(m[:, 3], m[:, 3], EPS, None, ALU.add).then_inc(var_ready, 1)
            link(tt(m[:, 4], st[:, :, 1], st[:, :, 4], ALU.add))
            dve.wait_ge(rstd_ready, 1)
            link(nc.vector.reciprocal(m[:, 0], m[:, 3]))
            link(nc.vector.scalar_tensor_tensor(out=m[:, 1], in0=m[:, 4], scalar=-0.5, in1=m[:, 0],
                                                op0=ALU.mult, op1=ALU.mult))

        def tiles(name, fill, K, turns, project, post, before=None, after=None, loads=None, norm=False, w=D, nt=None, clears=None):
            with ExitStack() as scope:
                nt = nt or (len(turns(X[:, 0, :])) if w == D else 1)
                st = [sb(f"st{name}{k}", [P, w], F32, scope) for k in range(TB)]
                hT = [sb(f"hT{name}{k}", [K, nt, P], F32, scope) for k in range(TB)]
                bst = sb(f"bst{name}", [P, T, 6], F32, scope)
                m = sb(f"m{name}", [P, 5, T], F32, scope)
                tp = [bank(f"tp{name}{k}", scope, P) for k in range(3)]
                op = [bank(f"op{name}{k}", scope) for k in range(3)]
                var_ready, rstd_ready = sem(f"var_ready{name}"), sem(f"rstd_ready{name}")
                loaded, stats, filled, turned, copied, product, taken, stored, cleared = [
                    sem(f"{n}{name}") for n in ("loaded", "stats", "filled", "turned", "copied", "product", "taken", "stored",
                                                "cleared")]
                with nc.Block() as block:
                    @block.sync
                    def _(sp):
                        for a, b in loads or []:
                            sp.dma_start(a, b, allow_slow_non_contiguous=True).then_inc(loaded, 16)
                        if after is not None:
                            sp.wait_ge(taken, T)
                            n = after(sp, stored)
                            sp.wait_ge(stored, 16 * n)

                    @block.gpsimd
                    def _(pool):
                        if clears is not None:
                            nc.gpsimd.memset(clears[:], 0.0).then_inc(cleared, 1)
                            pool.wait_ge(cleared, 1)

                    @block.vector
                    def _(dve):
                        link = dve_step.on(dve)
                        if norm:
                            layernorm_stats(dve, link, bst, m, var_ready, rstd_ready)
                        if loads:
                            dve.wait_ge(loaded, 16 * len(loads))
                        if before is not None:
                            before(dve, link)
                        nc.vector.memset(bst[:, 0, 0:1], 0.0).then_inc(stats, 1)

                        def body(i):
                            for k in range(TB):
                                dve.wait_ge(product, i * TB + (k + 1))
                                post(dve, link, i * TB + k, op[k % 3]).then_inc(taken, 1)
                        dve_step.run(T // TB, body)

                    @block.scalar
                    def _(act):
                        act_step.on(act)
                        if norm:
                            act.wait_ge(var_ready, 1)
                            nc.scalar.sqrt(m[:, 3], m[:, 3]).then_inc(rstd_ready, 1)
                        act.wait_ge(stats, 1)

                        def body(i):
                            for k in range(TB):
                                fill(i * TB + k, st[k], m).then_inc(filled, 1)
                            for k in range(TB):
                                act.wait_ge(turned, i * TB + (k + 1))
                                if later(i):
                                    act.wait_ge(product, i * TB + (k + 1 - TB))
                                nc.scalar.copy(hT[k][:], tp[k % 3][0:K, 0:nt, :]).then_inc(copied, 1)
                        act_step.run(T // TB, body)

                    @block.tensor
                    def _(pe):
                        pe_step.on(pe)
                        if loads:
                            pe.wait_ge(loaded, 16 * len(loads))
                        pe.wait_ge(stats, 1)

                        def turn(i, k):
                            pe.wait_ge(filled, i * TB + (k + 1))
                            if later(i) or k >= 2:
                                pe.wait_ge(copied, i * TB + (k - 1))
                            hold(pe)
                            for j, piece in enumerate(turns(st[k][:])):
                                mm = nc.tensor.transpose(tp[k % 3][0:K, j, :], piece, ident[:])
                            mm.then_inc(turned, 1)

                        def multiply(i, k):
                            pe.wait_ge(copied, i * TB + (k + 1))
                            if later(i) or k >= 2:
                                pe.wait_ge(taken, i * TB + (k - 1))
                            project(hT[k], op[k % 3]).then_inc(product, 1)

                        def body(i):
                            for k in range(TB):
                                turn(i, k)
                                if k:
                                    multiply(i, k - 1)
                            multiply(i, TB - 1)
                        pe_step.run(T // TB, body)

        def tile(a, t):
            return a[:, bass.ds(t, 1), :].rearrange("p o d -> p (o d)")

        def normed(t, st, m):
            return nc.scalar.activation(st[:], tile(X, t), ACT.Relu, bias=m[:, 1, bass.ds(t, 1)],
                                        scale=m[:, 0, bass.ds(t, 1)])

        def two(W):
            def project(hT, o):
                m = W.shape[-1]
                nc.tensor.matmul(o[:, 0:m], lhsT=hT[:, 0, :], rhs=W[:, 0, :], start=True, stop=False)
                return nc.tensor.matmul(o[:, 0:m], lhsT=hT[:, 1, :], rhs=W[:, 1, :], start=False, stop=True)
            return project

        def row(a):
            return a.unsqueeze(0).to_broadcast([P, a.shape[0]])

        def halves(st):
            return [st[:, 0:P], st[:, P:D]]

        def conv(n, table, hout, bias, src, lo, hi):
            with ExitStack() as scope:
                NG = 4
                hot = sb(f"chot{n}", [P, B, P], BF16, scope)
                hotT = sb(f"chotT{n}", [P, B, P], F32, scope)
                idx = sb(f"cidx{n}", [P, NG, B], U32, scope)
                G = sb(f"G{n}", [P, NG, B, H], F32, scope)
                ohlo = sb(f"cohlo{n}", [P, NG, B, P], F32, scope)
                ohhi = sb(f"cohhi{n}", [P, NG, B, T], F32, scope)
                V = sb(f"V{n}", [P, NG, B, T, H], F32, scope)
                acc = bank(f"acc{n}", scope)[:, 0:T * H]
                tp = bank(f"ctp{n}", scope, P, BF16)[:, 0:B]
                gp = bank(f"cgp{n}", scope, H)
                made, turned, kept, fetched, got, mades, spread, summed = [
                    sem(f"c{x}{n}") for x in ("made", "turned", "kept", "fetched", "got", "mades", "spread", "summed")]
                staged, gathered = [[sem(f"c{x}{n}{h}") for h in range(NG)] for x in ("staged", "gathered")]

                def only_pe(step):
                    return lambda g: step(g) if g.slot == 0 else None

                def only_pool(step):
                    return lambda g: step(g) if g.slot else None

                with nc.Block() as block:
                    @block.vector
                    def _(dve):
                        link = dve_step.on(dve)
                        tt = nc.vector.tensor_tensor

                        def src_hots(g):
                            need(dve, turned, g.lap())
                            one_hots(hot[:], keyl["s"], g.at(B)).then_inc(made, 1)

                        def hots(g):
                            need(dve, summed, g.at(1, 1 - NG))
                            one_hots(ohhi[:, g.slot], hi, g.at(B)).then_inc(mades, 1)
                            one_hots(ohlo[:, g.slot], lo, g.at(B)).then_inc(mades, 1)

                        def spreads(g):
                            if g.slot == 0:
                                dve.wait_ge(got, g.lap(1, 1))
                            else:
                                dve.wait_ge(gathered[g.slot], g.lap(16 * B, 16 * B))
                            dve.wait_ge(mades, g.at(2, 1))
                            tt(V[:, g.slot], G[:, g.slot].unsqueeze(2).to_broadcast([P, B, T, H]),
                               ohhi[:, g.slot].unsqueeze(3).to_broadcast([P, B, T, H]), ALU.mult).then_inc(spread, 1)
                        groups(dve, Q // B, NG, [(0, only_pe(src_hots)), (0, hots), (2, spreads)])
                        dve.wait_ge(summed, Q // B)
                        hv = hout[:].rearrange("p t f -> p (t f)")
                        link(tt(hv, acc, table[:].rearrange("p t f -> p (t f)"), ALU.add))
                        link(tt(hout[:], hout[:], bc(dinv[:], H), ALU.mult))
                        link(tt(hout[:], hout[:], rows(bias[:], T), ALU.add))
                        link(nc.vector.tensor_scalar(hout[:], hout[:], 0.0, None, ALU.max))

                    @block.scalar
                    def _(act):
                        def keep(g):
                            act.wait_ge(turned, g.lap(1, 1))
                            need(act, fetched, g.lap())
                            nc.scalar.copy(hotT[:], tp).then_inc(kept, 1)

                        def take(g):
                            act.wait_ge(fetched, g.lap(1, 1))
                            need(act, spread, g.at(1, 1 - NG))
                            nc.scalar.copy(G[:, g.slot], gp[:, 0:B, :]).then_inc(got, 1)

                        def stage(g):
                            need(act, gathered[g.slot], g.lap(16 * B))
                            hold(act)
                            nc.scalar.copy(idx[:, g.slot], src[:, bass.ds(g.at(B), B)]).then_inc(staged[g.slot], 1)
                        groups(act, Q // B, NG, [(0, only_pe(keep)), (0, only_pool(stage)), (1, only_pe(take))])

                    @block.gpsimd
                    def _(pool):
                        def gather(g):
                            pool.wait_ge(staged[g.slot], g.lap(1, 1))
                            need(pool, spread, g.at(1, 1 - NG))
                            hold(pool)
                            for b in range(B):
                                nc.gpsimd.indirect_dma_start(
                                    G[:, g.slot, b, :], None, tab16[n][:, :],
                                    bass.IndirectOffsetOnAxis(ap=idx[:, g.slot, b:b + 1], axis=0)
                                ).then_inc(gathered[g.slot], 16)
                        groups(pool, Q // B, NG, [(0, only_pool(gather))])

                    @block.tensor
                    def _(pe):
                        tiles_of = {}

                        def turn(g):
                            pe.wait_ge(made, g.lap(1, 1))
                            need(pe, kept, g.lap())
                            for b in range(B):
                                mm = nc.tensor.transpose(tp[:, b, :], hot[:, b, :], identb[:])
                            mm.then_inc(turned, 1)

                        def fetch(g):
                            pe.wait_ge(kept, g.lap(1, 1))
                            need(pe, got, g.lap())
                            hold(pe)
                            for b in range(B):
                                mm = nc.tensor.matmul(gp[:, b, :], lhsT=hotT[:, b, :],
                                                      rhs=table[:, bass.ds(tiles_of[g.slot * B + b], 1), :]
                                                      .rearrange("p o f -> p (o f)"), start=True, stop=True)
                            mm.then_inc(fetched, 1)

                        def sums(g):
                            pe.wait_ge(spread, g.at(1, 1))
                            pe.wait_ge(mades, g.at(2, 2))
                            for b in range(B):
                                mm = nc.tensor.matmul(acc, lhsT=ohlo[:, g.slot, b, :],
                                                      rhs=V[:, g.slot, b].rearrange("p t f -> p (t f)"),
                                                      start=g.first() and b == 0, stop=False, skip_group_check=True)
                            mm.then_inc(summed, 1)
                        groups(pe, Q // B, NG, [(3, sums), (0, only_pe(turn)), (1, only_pe(fetch))],
                               pair_tiles("s", mybir.EngineType.PE, NG, tiles_of))

        if stop >= 3:
            free_sems()
            with ExitStack() as scope:
                W1 = sb("W1", [P, 2, H], F32, scope)
                W2 = sb("W2", [H, H], F32, scope)
                WoT = sb("WoT", [H, D], F32, scope)
                b1 = sb("b1", [P, H], F32, scope)
                b2 = sb("b2", [P, H], F32, scope)
                bo = sb("bo", [P, D], F32, scope)
                g = [sb(f"g{n}", [P, T, H], F32, scope) for n in range(2)]
                h16 = [sb(f"h16{n}", [P, T, H], F32, scope) for n in range(2)]
                pre = sb("pre", [P, T, D], F32, scope)

                rooted = sem("rooted")
                dst_lo, dst_hi = sb("dst_lo", [P, Q], F32, scope), sb("dst_hi", [P, Q], F32, scope)
                tile_of_dst = sb("tile_of_dst", [P, Q], U32, scope)
                src_q, src_f, off = sb("src_q", [P, Q], U32, scope), sb("src_f", [P, Q], F32, scope), sb("off", [P, Q], F32, scope)

                with nc.Block() as block:
                    @block.vector
                    def _(dve):
                        link = dve_step.on(dve)
                        link(nc.vector.tensor_scalar(tile_of_dst[:], S_idx[:], 7, None, ALU.logical_shift_right))
                        link(nc.vector.tensor_copy(dst_hi[:], tile_of_dst[:]))
                        link(nc.vector.tensor_copy(dst_lo[:], S_idx[:]))
                        link(nc.vector.scalar_tensor_tensor(out=dst_lo[:], in0=dst_hi[:], scalar=-float(P), in1=dst_lo[:],
                                                            op0=ALU.mult, op1=ALU.add))
                        keys = keyl["s"]
                        for bound, op in ((0.0, ALU.is_lt), (float(P - 1), ALU.is_gt)):
                            link(nc.vector.tensor_scalar(off[:], keys[:], bound, None, op))
                            link(nc.vector.scalar_tensor_tensor(out=dst_lo[:], in0=off[:], scalar=FAR, in1=dst_lo[:],
                                                                op0=ALU.mult, op1=ALU.add))
                        link(nc.vector.tensor_copy(src_f[:], toff["s"][:]))
                        link(nc.vector.scalar_tensor_tensor(out=src_f[:], in0=src_f[:], scalar=float(P), in1=keys[:],
                                                            op0=ALU.mult, op1=ALU.add))
                        link(nc.vector.tensor_copy(src_q[:], src_f[:]))
                        link(nc.vector.tensor_scalar(dinv[:], degs["d"][:], 1.0, None, ALU.add))
                        nc.vector.tensor_scalar(dn[:], degs["s"][:], 1.0, None, ALU.max).then_inc(rooted, 1)
                        dve.wait_ge(rooted, 3)
                        link(nc.vector.reciprocal(dinv[:], dinv[:]))
                        link(nc.vector.reciprocal(dn[:], dn[:]))

                    @block.scalar
                    def _(act):
                        act.wait_ge(rooted, 1)
                        nc.scalar.sqrt(dinv[:], dinv[:]).then_inc(rooted, 1)
                        nc.scalar.sqrt(dn[:], dn[:]).then_inc(rooted, 1)

                def scaled(n):
                    def post(dve, link, t, o):
                        return nc.vector.tensor_scalar(tile(g[n], t), o[:, 0:H], dinv[:, bass.ds(t, 1)], None, ALU.mult)
                    return post

                def store16(n):
                    def after(sp, s):
                        sp.dma_start(tab16[n].rearrange("(t p) f -> p t f", p=P), g[n][:]).then_inc(s, 16)
                        return 1
                    return after

                tiles("a", normed, P, halves, two(W1), scaled(0), after=store16(0), norm=True,
                      loads=[(W1[:], A["L0_gnn_W1"].rearrange("(k p) m -> p k m", p=P)), (W2[:], A["L0_gnn_W2"]),
                             (WoT[:], A["L0_gnn_Wout"].rearrange("d h -> h d")), (b1[:], row(A["L0_gnn_b1"])),
                             (b2[:], row(A["L0_gnn_b2"])), (bo[:], row(A["L0_gnn_bout"]))])
                conv(0, g[0], h16[0], b1, src_q, dst_lo, dst_hi)
                tiles("b", lambda t, st, m: nc.scalar.copy(st[:], tile(h16[0], t)), H, lambda st: [st],
                      lambda hT, o: nc.tensor.matmul(o[:, 0:H], lhsT=hT[:, 0, :], rhs=W2[:], start=True, stop=True),
                      scaled(1), after=store16(1), w=H)
                conv(1, g[1], h16[1], b2, src_q, dst_lo, dst_hi)
                tiles("c", lambda t, st, m: nc.scalar.copy(st[:], tile(h16[1], t)), H, lambda st: [st],
                      lambda hT, o: nc.tensor.matmul(o[:, 0:D], lhsT=hT[:, 0, :], rhs=WoT[:], start=True, stop=True),
                      lambda dve, link, t, o: nc.vector.tensor_tensor(tile(pre, t), o[:, 0:D], bo[:], ALU.add), w=H)
                gate = sem("gate")
                with nc.Block() as block:
                    @block.scalar
                    def _(act):
                        nc.scalar.activation(pre[:], pre[:], ACT.Sigmoid).then_inc(gate, 1)

                    @block.vector
                    def _(dve):
                        dve.wait_ge(gate, 1)
                        dve_step.on(dve)(nc.vector.tensor_tensor(X[:], X[:], pre[:], ALU.add))

        def rsqrt_block(v, name, pre=None):
            made, rooted = sem(f"made{name}"), sem(f"rooted{name}")
            with nc.Block() as block:
                @block.vector
                def _(dve):
                    link = dve_step.on(dve)
                    pre(link)
                    dve.sem_inc(made, 1)
                    dve.wait_ge(rooted, 1)
                    link(nc.vector.reciprocal(v, v))

                @block.scalar
                def _(act):
                    act.wait_ge(made, 1)
                    nc.scalar.sqrt(v, v).then_inc(rooted, 1)

        def messages(SUM, fc1, fc2, fc3):
            with ExitStack() as scope:
                NG = 4
                G = sb("Gy", [P, NG, B, D], F32, scope)
                idx = sb("idxy", [P, NG, B], U32, scope)
                at = sb("at", [P, NG, B * 8], F32, scope)
                aT = sb("aT", [B * 8, 2, P], F32, scope)
                s1 = sb("s1", [P, 2, 2 * P], F32, scope)
                s2 = sb("s2", [P, 2, 2 * P], F32, scope)
                oh = sb("oh1", [P, 2, B, P], F32, scope)
                M = sb("M1", [P, 2, B, 8, MUL], F32, scope)
                w = sb("w", [P, 2, B, 4, MUL], F32, scope)
                tb = sb("tb", [P, B, MUL], F32, scope)
                evs = sb("evs", [P, 2, B, 3, MUL], F32, scope)
                sh = sb("sh", [P, NG, B, 4], F32, scope)
                wb = [[bank(f"w{h}{n}", scope) for n in range(2)] for h in range(2)]
                sm = [bank(f"sm{n}", scope) for n in range(2)]
                a0, a1 = bank("a0", scope), bank("a1", scope)
                gathered = [sem(f"gathered_y{h}") for h in range(NG)]
                pool_idx = sem("pool_idx")
                (attr_st, attr_tp, attr_T, h1_done, s1_done, h2_done, s2_done, w_done, w_kept, sh_st, ev_scaled, parts, msg,
                 summed, added) = [
                    sem(f"{x}_y") for x in ("attr_st", "attr_tp", "attr_T", "h1_done", "s1_done", "h2_done", "s2_done",
                                            "w_done", "w_kept", "sh_st", "ev_scaled", "parts", "msg", "summed", "added")]
                n_g = Q // B
                with nc.Block() as block:
                    @block.gpsimd
                    def _(pool):
                        link = Links(pool, pool_idx, 1)

                        def gather(g):
                            need(pool, gathered[g.slot], g.lap(16 * B))
                            link.start(g)(nc.gpsimd.tensor_copy(idx[:, g.slot], S_idx[:, bass.ds(g.at(B), B)]))
                            need(pool, msg, g.at(5, 5 - NG * 5))
                            hold(pool)
                            for b in range(B):
                                nc.gpsimd.indirect_dma_start(
                                    G[:, g.slot, b, :], None, taby[:, :],
                                    bass.IndirectOffsetOnAxis(ap=idx[:, g.slot, b:b + 1], axis=0)
                                ).then_inc(gathered[g.slot], 16)
                        groups(pool, n_g, NG, [(0, gather)])

                    @block.scalar
                    def _(act):
                        copy = nc.scalar.copy

                        def stage(g):
                            need(act, attr_tp, g.at(1, 1 - NG))
                            hold(act)
                            copy(at[:, g.slot].rearrange("p (b f) -> p b f", b=B),
                                 S_attr[:, bass.ds(g.at(B), B), 0:8]).then_inc(attr_st, 1)

                        def keep_turned(g):
                            act.wait_ge(attr_tp, g.at(1, 1))
                            need(act, h1_done, g.at(1, -1))
                            copy(aT[:, g.slot % 2], a0[0:B * 8, 0:P]).then_inc(attr_T, 1)

                        def stage_sh(g):
                            copy(sh[:, g.slot], S_attr[:, bass.ds(g.at(B), B), 8:12]).then_inc(sh_st, 1)

                        def scale_ev(bs):
                            def step(g):
                                act.wait_ge(gathered[g.slot], g.lap(16 * B, 16 * B))
                                for b in bs:
                                    for d in range(3):
                                        ins = nc.scalar.activation(
                                            evs[:, g.slot % 2, b, d], G[:, g.slot, b, (d + 1) * MUL:(d + 2) * MUL],
                                            ACT.Copy, scale=sh[:, g.slot, b, d + 1:d + 2])
                                ins.then_inc(ev_scaled, 1)
                            return step

                        def keep_weights(g):
                            act.wait_ge(sh_st, g.at(1, 1))
                            need(act, msg, g.at(5, 5 - 2 * 5))
                            for n in range(2):
                                act.wait_ge(w_done, g.at(2, n + 1))
                                w4 = wb[g.slot % 2][n].rearrange("p (b k u) -> p b k u", k=4, u=MUL)
                                copy(w[:, g.slot % 2, 2 * n:2 * n + 2, 1:4:2, :], w4[:, :, 1:4:2, :]).then_inc(w_kept, 1)
                                hold(act)
                                for b in range(2):
                                    nc.scalar.activation(w[:, g.slot % 2, 2 * n + b, 0:4:2, :], w4[:, b, 0:4:2, :], ACT.Copy,
                                                         scale=sh[:, g.slot, 2 * n + b, 0:1]).then_inc(w_kept, 1)

                        def silu1(g):
                            act.wait_ge(h1_done, g.at(1, 1))
                            need(act, h2_done, g.at(1, -1))
                            nc.scalar.activation(s1[:, g.slot % 2], a0[:, 0:2 * P], ACT.Silu, scale=8.0 ** -0.5).then_inc(s1_done, 1)

                        def silu2(g):
                            act.wait_ge(h2_done, g.at(1, 1))
                            need(act, w_done, g.at(2, -2))
                            nc.scalar.activation(s2[:, g.slot % 2], a1[:, 0:2 * P], ACT.Silu, scale=0.125).then_inc(s2_done, 1)
                        groups(act, n_g, NG, [(0, stage), (4, keep_weights), (1, keep_turned), (4, scale_ev((0, 1))), (1, silu1),
                                          (4, scale_ev((2, 3))), (3, stage_sh), (2, silu2)])

                    @block.tensor
                    def _(pe):
                        def turn(g):
                            pe.wait_ge(attr_st, g.at(1, 1))
                            need(pe, s1_done, g.at(1))
                            hold(pe)
                            nc.tensor.transpose(a0[0:B * 8, 0:P], at[:, g.slot], ident[:]).then_inc(attr_tp, 1)

                        def layer1(g):
                            pe.wait_ge(attr_T, g.at(1, 1))
                            hold(pe)
                            for j in range(2):
                                mm = nc.tensor.matmul(a0[:, j * P:(j + 1) * P], lhsT=fc1[:, j], rhs=aT[:, g.slot % 2],
                                                      start=True, stop=True)
                            mm.then_inc(h1_done, 1)

                        def layer2(g):
                            pe.wait_ge(s1_done, g.at(1, 1))
                            need(pe, s2_done, g.at(1))
                            hold(pe)
                            nc.tensor.matmul(a1[:, 0:2 * P], lhsT=fc2[:], rhs=s1[:, g.slot % 2], start=True,
                                             stop=True).then_inc(h2_done, 1)

                        def weights(g):
                            pe.wait_ge(s2_done, g.at(1, 1))
                            need(pe, w_kept, g.at(6, 6 - 2 * 6))
                            for n in range(2):
                                nc.tensor.matmul(wb[g.slot % 2][n], lhsT=s2[:, g.slot % 2, n * P:(n + 1) * P],
                                                 rhs=fc3[:], start=True, stop=True).then_inc(w_done, 1)

                        def sums(bs):
                            def step(g):
                                need(pe, msg, g.at(5, 5))
                                for b in bs:
                                    need(pe, added, g.at(B, b - 1))
                                    nc.tensor.matmul(sm[b % 2], lhsT=oh[:, g.slot % 2, b, :],
                                                     rhs=M[:, g.slot % 2, b].rearrange("p k u -> p (k u)"), start=True,
                                                     stop=True).then_inc(summed, 1)
                            return step
                        groups(pe, n_g, NG, [(0, turn), (4, sums((0,))), (0, layer1), (4, sums((1, 2))), (1, layer2),
                                             (4, sums((3,))), (2, weights)])

                    @block.vector
                    def _(dve):
                        mul = ALU.mult
                        tt = nc.vector.tensor_tensor
                        tiles_of = {}

                        def add(g, b):
                            r = g.slot * B + b
                            acc = SUM[:, bass.ds(tiles_of[r], 1), :].rearrange("p o f -> p (o f)")
                            need(dve, added, g.at(B, b))
                            dve.wait_ge(summed, g.at(B, b + 1))
                            tt(acc, acc, sm[b % 2], ALU.add).then_inc(added, 1)

                        def messages_of(g):
                            h = g.slot % 2
                            at_q = bass.ds(g.at(B), B)
                            sh1 = S_attr[:, at_q, 9:12].unsqueeze(3).to_broadcast([P, B, 3, MUL])
                            es = G[:, g.slot, :, 0:MUL]
                            ev = G[:, g.slot, :, MUL:D].rearrange("p b (d u) -> p b d u", u=MUL)
                            old = None if g.first() else Group(g.i, NG, g.off * NG + g.slot - 1)

                            def add_old(b):
                                if old is not None:
                                    add(old, b)
                            need(dve, summed, g.at(B, B - 2 * B))
                            one_hots(oh[:, h], keyl["s"], g.at(B)).then_inc(msg, 1)
                            dve.wait_ge(gathered[g.slot], g.lap(16 * B, 16 * B))
                            dve.wait_ge(w_kept, g.at(6, 6))
                            tt(M[:, h, :, 0:2, :], w[:, h, :, 0:2, :], es.unsqueeze(2).to_broadcast([P, B, 2, MUL]),
                               mul).then_inc(msg, 1)
                            add_old(0)
                            dve.wait_ge(msg, g.at(5, 2))
                            tt(M[:, h, :, 2:8:2, :], M[:, h, :, 1:2, :].to_broadcast([P, B, 3, MUL]), sh1, mul).then_inc(msg, 1)
                            add_old(1)
                            dve.wait_ge(ev_scaled, g.at(2, 2))
                            tt(tb[:], evs[:, h, :, 0], evs[:, h, :, 1], ALU.add).then_inc(parts, 1)
                            add_old(2)
                            dve.wait_ge(parts, g.at(2, 1))
                            tt(tb[:], tb[:], evs[:, h, :, 2], ALU.add).then_inc(parts, 1)
                            tt(M[:, h, :, 3:8:2, :], w[:, h, :, 2:3, :].to_broadcast([P, B, 3, MUL]), ev, mul).then_inc(msg, 1)
                            dve.wait_ge(parts, g.at(2, 2))
                            tt(M[:, h, :, 1, :], w[:, h, :, 3, :], tb[:], mul).then_inc(msg, 1)
                            add_old(3)
                        groups(dve, n_g, NG, [(0, messages_of)], pair_tiles("s", mybir.EngineType.DVE, NG, tiles_of))
                        for b in range(B):
                            add(Group(n_g // NG, NG, n_g % NG - 1), b)
                        dve.wait_ge(added, Q)

        if stop >= 4:
            free_sems()
            with ExitStack() as scope:
                w1 = [sb(f"w1{n}", [MUL, 2 * MUL], F32, scope) for n in "sv"]
                w2 = [sb(f"w2{n}", [2 * MUL, MUL], F32, scope) for n in "sv"]
                fc1 = sb("fc1", [B * 8, 2, P], F32, scope)
                fc2 = sb("fc2", [P, P], F32, scope)
                fc3 = sb("fc3", [P, 2 * 4 * MUL], F32, scope)
                cleared = sem("fc_cleared")
                with nc.Block() as block:
                    @block.vector
                    def _(dve):
                        for a in (fc1, fc2, fc3):
                            nc.vector.memset(a[:], 0.0).then_inc(cleared, 1)
                        dve.wait_ge(cleared, 3)
                gsv = sb("gsv", [P, 2, MUL], F32, scope)
                SC = sb("SC", [P, T, D], F32, scope)
                SUM = sb("SUM", [P, T, 8 * MUL], F32, scope)
                with ExitStack() as inner:
                    Y = sb("Y", [P, T, D], F32, inner)

                    def y_project(hT, o):
                        for j in range(4):
                            mm = nc.tensor.matmul(o[:, j * 2 * MUL:(j + 1) * 2 * MUL], lhsT=hT[:, j, :],
                                                  rhs=w1[min(j, 1)][:], start=True, stop=True)
                        return mm

                    def y_post(dve, link, t, o):
                        o4 = o.rearrange("p (j k u) -> p j k u", k=2, u=MUL)
                        link(nc.vector.tensor_copy(tile(Y, t).rearrange("p (j u) -> p j u", u=MUL), o4[:, :, 0, :]))
                        return nc.vector.tensor_scalar(tile(SC, t).rearrange("p (j u) -> p j u", u=MUL), o4[:, :, 1, :],
                                                       MUL ** -0.5, None, ALU.mult)

                    def y_store(sp, s):
                        sp.dma_start(taby.rearrange("(t p) f -> p t f", p=P), Y[:]).then_inc(s, 16)
                        return 1

                    pre = "L1_gnn_"
                    tiles("d", normed, MUL, lambda st: [st[:, 0:MUL]] + [st[:, MUL + d:D:3] for d in range(3)],
                          y_project, y_post, after=y_store, norm=True, clears=SUM,
                          loads=[(w1[0][:, 0:MUL], A[pre + "w1_s"]), (w1[0][:, MUL:], A[pre + "wsc_s"]),
                                 (w1[1][:, 0:MUL], A[pre + "w1_v"]), (w1[1][:, MUL:], A[pre + "wsc_v"]),
                                 (w2[0][:], A[pre + "w2_s"]), (w2[1][:], A[pre + "w2_v"]),
                                 *[(fc1[b * 8:(b + 1) * 8, b // 2, b % 2 * MUL:(b % 2 + 1) * MUL], A[pre + "fc_w1"])
                                   for b in range(B)],
                                 *[(fc2[h * MUL:(h + 1) * MUL, h * MUL:(h + 1) * MUL], A[pre + "fc_w2"]) for h in range(2)],
                                 *[(fc3[h * MUL:(h + 1) * MUL, h * 4 * MUL:(h + 1) * 4 * MUL], A[pre + "fc_w3"]) for h in range(2)],
                                 (gsv[:, 0], row(A[pre + "g_s"])), (gsv[:, 1], row(A[pre + "g_v"]))])
                messages(SUM, fc1, fc2, fc3)
                O = sb("O", [P, T, D], F32, scope)
                ms = sb("ms", [P, 2, T], F32, scope)
                dns = sb("dns", [P, T], F32, scope)

                def before(dve, link):
                    link(nc.vector.tensor_scalar(dns[:], dn[:], MUL ** -0.5 * MUL ** -0.5 * (2 * MUL) ** -0.5, None, ALU.mult))
                    link(nc.vector.tensor_scalar(w2[0][MUL:, :], w2[0][MUL:, :], 0.5773502691896258, None, ALU.mult))

                def o_project(hT, o):
                    for j in range(4):
                        mm = nc.tensor.matmul(o[:, j * MUL:(j + 1) * MUL], lhsT=hT[:, j, :], rhs=w2[min(j, 1)][:],
                                              start=True, stop=True)
                    return mm

                tiles("e", lambda t, st, m: nc.scalar.copy(st[:], tile(SUM, t)), P,
                      lambda st: [st[:, j * P:(j + 1) * P] for j in range(4)], o_project,
                      lambda dve, link, t, o: nc.vector.scalar_tensor_tensor(
                          out=tile(O, t), in0=o[:, 0:D], scalar=dns[:, bass.ds(t, 1)], in1=tile(SC, t),
                          op0=ALU.mult, op1=ALU.add), before=before, w=8 * MUL, nt=4)

                def mean_squares(link):
                    sq = SUM[:, :, 0:D]
                    link(nc.vector.tensor_tensor(sq, O[:], O[:], ALU.mult))
                    for n, (a, b) in enumerate(((0, MUL), (MUL, D))):
                        link(nc.vector.tensor_reduce(ms[:, n], sq[:, :, a:b], AX.X, ALU.add))
                        link(nc.vector.tensor_scalar(ms[:, n], ms[:, n], 1.0 / (b - a), EPS, ALU.mult, ALU.add))

                rsqrt_block(ms[:], "rms", mean_squares)
                with nc.Block() as block:
                    @block.vector
                    def _(dve):
                        link = dve_step.on(dve)
                        for n, (a, b) in enumerate(((0, MUL), (MUL, D))):
                            link(nc.vector.tensor_tensor(O[:, :, a:b], O[:, :, a:b], bc(ms[:, n], b - a), ALU.mult))
                            for j in range(a // MUL, b // MUL):
                                o = O[:, :, j * MUL:(j + 1) * MUL]
                                x = X[:, :, 0:MUL] if j == 0 else X[:, :, MUL + j - 1:D:3]
                                link(nc.vector.tensor_tensor(o, o, rows(gsv[:, n], T), ALU.mult))
                                link(nc.vector.tensor_tensor(x, x, o, ALU.add))

        def attend(l, W, al, ar, dist):
            outer = ExitStack()
            with outer:
                EX = sb(f"EX{l}", [P, Q, HEADS], F32, outer)
                EA = sb(f"EA{l}", [P, Q, HEADS], F32, outer) if dist else EX
                with ExitStack() as scope:
                    wt = sb(f"wt{l}", [P, 2, D + 2 * HEADS], F32, scope)
                    attn = sb(f"attn{l}", [P, 2, D], F32, scope)
                    el = sb(f"el{l}", [P, T, 2, HEADS], F32, scope)
                    elt = sb(f"elt{l}", [P, T, HEADS], F32, scope)
                    ert = sb(f"ert{l}", [P, T, HEADS], F32, scope)
                    EL = sb(f"EL{l}", [P, Q, HEADS], F32, scope)
                    ER = sb(f"ER{l}", [P, Q, HEADS], F32, scope)
                    with ExitStack() as inner:
                        F = sb(f"F{l}", [P, T, D], F32, inner)
                        fa = sb(f"fa{l}", [P, 2, D], F32, inner)

                        def before(dve, link):
                            for k in range(2):
                                link(nc.vector.tensor_tensor(fa[:], wt[:, k, 0:D].unsqueeze(1).to_broadcast([P, 2, D]),
                                                             attn[:], ALU.mult))
                                link(nc.vector.tensor_reduce(wt[:, k, D:], fa[:].rearrange("p k (h d) -> p (k h) d", h=HEADS),
                                                             AX.X, ALU.add))

                        def post(dve, link, t, o):
                            link.note(nc.vector.tensor_copy(tile(F, t), o[:, 0:D]))
                            return nc.vector.tensor_copy(el[:, bass.ds(t, 1)].rearrange("p o k h -> p (o k h)"),
                                                         o[:, D:D + 2 * HEADS])

                        def store(sp, s):
                            sp.dma_start(tabf[l - 2].rearrange("(t p) f -> p t f", p=P), F[:]).then_inc(s, 16)
                            return 1

                        tiles(f"f{l}", normed, P, halves, two(wt), post, before=before, after=store, norm=True,
                              loads=[(wt[:, :, 0:D], W.rearrange("(k p) m -> p k m", p=P)), (attn[:, 0], row(al)), (attn[:, 1], row(ar))])
                    logits(l, el, elt, ert, EL, ER)
                    weights_of_edges(l, EL, ER, EX, EA, dist)
                SUM = sb(f"SUM{l}", [P, T, D + HEADS], F32, outer)
                with ExitStack() as scope:
                    NG = 5
                    SUM2 = sb(f"SUM2{l}", [P, T, D + HEADS], F32, scope)
                    G = sb(f"G{l}", [P, NG, B, D], F32, scope)
                    idx = sb(f"idx{l}", [P, NG, B], U32, scope)
                    oh = sb(f"oh{l}", [P, NG, B, P], F32, scope)
                    M = sb(f"M{l}", [P, NG, B, D + HEADS], F32, scope)
                    sm = [bank(f"sm{l}{n}", scope)[:, 0:D + HEADS] for n in range(NG)]
                    gathered = [sem(f"gathered{l}{h}") for h in range(NG)]
                    staged, msg, summed, added, cleared = [
                        sem(f"{x}{l}") for x in ("staged", "msg", "summed", "added", "cleared")]
                    with nc.Block() as block:
                        @block.scalar
                        def _(act):
                            def stage(g):
                                need(act, msg, g.at(3, 3 - 3 * NG))
                                hold(act)
                                nc.scalar.copy(idx[:, g.slot], D_idx[:, bass.ds(g.at(B), B)]).then_inc(staged, 1)
                            groups(act, Q // B, NG, [(0, stage)])

                        @block.gpsimd
                        def _(pool):
                            def gather(g):
                                need(pool, staged, g.at(1, 1))
                                hold(pool)
                                for b in range(B):
                                    nc.gpsimd.indirect_dma_start(
                                        G[:, g.slot, b, :], None, tabf[l - 2][:, :],
                                        bass.IndirectOffsetOnAxis(ap=idx[:, g.slot, b:b + 1], axis=0)
                                    ).then_inc(gathered[g.slot], 16)
                            groups(pool, Q // B, NG, [(0, gather)])

                        @block.tensor
                        def _(pe):
                            def sums(g):
                                need(pe, msg, g.at(3, 3))
                                for b in range(B):
                                    need(pe, added, g.at(B, b + 1 - NG))
                                    nc.tensor.matmul(sm[(g.slot * B + b) % NG], lhsT=oh[:, g.slot, b, :], rhs=M[:, g.slot, b],
                                                     start=True, stop=True).then_inc(summed, 1)
                            groups(pe, Q // B, NG, [(0, sums)])

                        @block.vector
                        def _(dve):
                            tt = nc.vector.tensor_tensor
                            nc.vector.memset(SUM[:], 0.0).then_inc(cleared, 1)
                            nc.vector.memset(SUM2[:], 0.0).then_inc(cleared, 1)
                            dve.wait_ge(cleared, 2)
                            tiles_of = {}

                            def message(g):
                                at_q = bass.ds(g.at(B), B)
                                need(dve, summed, g.at(B, B - B * NG))
                                one_hots(oh[:, g.slot], keyl["d"], g.at(B)).then_inc(msg, 1)
                                nc.vector.tensor_copy(M[:, g.slot, :, D:], EX[:, at_q, :]).then_inc(msg, 1)
                                dve.wait_ge(gathered[g.slot], g.lap(16 * B, 16 * B))
                                tt(M[:, g.slot, :, 0:D].rearrange("p b (k d) -> p b k d", k=HEADS),
                                   G[:, g.slot].rearrange("p b (k d) -> p b k d", k=HEADS),
                                   EA[:, at_q, :].unsqueeze(3).to_broadcast([P, B, HEADS, D // HEADS]),
                                   ALU.mult).then_inc(msg, 1)

                            def add(g):
                                for b in range(B):
                                    r = g.slot * B + b
                                    acc = (SUM, SUM2)[b % 2][:, bass.ds(tiles_of[r], 1), :].rearrange("p o f -> p (o f)")
                                    need(dve, added, g.at(B, b - 1))
                                    dve.wait_ge(summed, g.at(B, b + 1))
                                    tt(acc, acc, sm[r % NG], ALU.add).then_inc(added, 1)
                            groups(dve, Q // B, NG, [(0, message), (1, add)],
                                   pair_tiles("d", mybir.EngineType.DVE, NG, tiles_of))
                            dve.wait_ge(added, Q)
                            dve_step.on(dve)(tt(SUM[:], SUM[:], SUM2[:], ALU.add))
                gat_end(l, SUM)

        def logits(l, el, elt, ert, EL, ER):
            keeps = l == 2
            with ExitStack() as scope:
                lo = sb(f"llo{l}", [P, Q], F32, scope)
                hi = sb(f"lhi{l}", [P, Q], F32, scope)
                hii = sb(f"lhii{l}", [P, Q], U32, scope)
                NG, ahead = 4, 3
                el3 = sb(f"el3{l}", [P, 3, T, HEADS], BF16, scope)
                er3 = sb(f"er3{l}", [P, T, 3, HEADS], BF16, scope)
                hot_s = sb(f"hot_s{l}", [P, NG, B, P], BF16, scope)
                hot_d = sb(f"hot_d{l}", [P, NG, B, P], BF16, scope)
                ohhi = sb(f"lohhi{l}", [P, NG, B, T], F32, scope)
                hotT = sb(f"hotT{l}", [P, NG, 2 * B, P], BF16, scope)
                pr = sb(f"lpr{l}", [P, NG, B, T * HEADS], F32, scope)
                tp = [bank(f"ltp{l}{h}", scope, P, BF16) for h in range(NG)]
                lp = [bank(f"llp{l}{h}", scope) for h in range(NG)]
                stored, fetched = [[sem(f"{x}{l}{h}") for h in range(NG)] for x in ("lstored", "lfetched")]
                made_s, made_d, made_hi, turned, copied, looked, picked, taken, split = [
                    sem(f"{x}{l}") for x in ("made_s", "made_d", "made_hi", "lturned", "lcopied", "looked", "picked", "ltaken", "lsplit")]
                NL = B * T * HEADS
                with nc.Block() as block:
                    @block.sync
                    def _(sp):
                        def put(g):
                            sp.wait_ge(copied, g.at(1, 1))
                            hold(sp)
                            sp.dma_start(turned_hots[:, bass.ds(g.at(), 1), :],
                                         hotT[:, g.slot:g.slot + 1].rearrange("p o b m -> p o (b m)")).then_inc(stored[g.slot], 16)

                        def get(g):
                            need(sp, looked, g.at(1, 1 - NG))
                            hold(sp)
                            sp.dma_start(hotT[:, g.slot:g.slot + 1].rearrange("p o b m -> p o (b m)"),
                                         turned_hots[:, bass.ds(g.at(), 1), :]).then_inc(fetched[g.slot], 16)
                        groups(sp, Q // B, NG, [(0, put if keeps else get)])
                        for h in range(NG):
                            sp.wait_ge((stored if keeps else fetched)[h], 16 * len(range(h, Q // B, NG)))

                    @block.vector
                    def _(dve):
                        link = dve_step.on(dve)
                        tt = nc.vector.tensor_tensor
                        link(nc.vector.tensor_scalar(hii[:], D_idx[:], 7, None, ALU.logical_shift_right))
                        link(nc.vector.tensor_copy(hi[:], hii[:]))
                        link(nc.vector.tensor_copy(lo[:], D_idx[:]))
                        link(nc.vector.scalar_tensor_tensor(out=lo[:], in0=hi[:], scalar=-float(P), in1=lo[:],
                                                            op0=ALU.mult, op1=ALU.add))
                        link(nc.vector.tensor_copy(elt[:], el[:, :, 0, :]))
                        link(nc.vector.tensor_copy(ert[:], el[:, :, 1, :]))
                        for n in range(3):
                            link(nc.vector.tensor_copy(el3[:, n], elt[:]))
                            link(nc.vector.tensor_copy(er3[:, :, n, :], ert[:]))
                            link(tt(elt[:], elt[:], el3[:, n], ALU.subtract))
                            link(tt(ert[:], ert[:], er3[:, :, n, :], ALU.subtract))
                        dve.sem_inc(split, 1)

                        def pick(g):
                            dve.wait_ge(looked, g.at(1, 1))
                            dve.wait_ge(made_hi, g.at(1, 1))
                            tt(pr[:, g.slot].rearrange("p b (t k) -> p b t k", k=HEADS),
                               lp[g.slot][:, 0:NL].rearrange("p (b t k) -> p b t k", b=B, k=HEADS),
                               ohhi[:, g.slot].unsqueeze(3).to_broadcast([P, B, T, HEADS]), ALU.mult).then_inc(picked, 1)

                        def hots(g):
                            if keeps:
                                need(dve, turned, g.at(1, 1 - NG))
                                one_hots(hot_s[:, g.slot], lo, g.at(B)).then_inc(made_s, 1)
                                one_hots(hot_d[:, g.slot], keyl["d"], g.at(B)).then_inc(made_d, 1)
                            need(dve, picked, g.at(1, 1 - NG))
                            one_hots(ohhi[:, g.slot], hi, g.at(B)).then_inc(made_hi, 1)

                        def take(g):
                            at_q = bass.ds(g.at(B), B)
                            nc.vector.tensor_reduce(
                                ER[:, at_q, :], lp[g.slot][:, NL:NL + 3 * B * HEADS].rearrange("p (b n k) -> p b k n", b=B, k=HEADS),
                                AX.X, ALU.add).then_inc(taken, 1)
                            dve.wait_ge(picked, g.at(1, 1))
                            nc.vector.tensor_reduce(EL[:, at_q, :], pr[:, g.slot].rearrange("p b (t k) -> p b k t", k=HEADS),
                                                    AX.X, ALU.add).then_inc(taken, 1)
                        groups(dve, Q // B, NG, [(ahead, pick), (0, hots), (ahead, take)])

                    @block.scalar
                    def _(act):
                        def copy(g):
                            act.wait_ge(turned, g.at(1, 1))
                            need(act, looked, g.at(1, 1 - NG))
                            need(act, stored[g.slot], g.lap(16))
                            nc.scalar.copy(hotT[:, g.slot], tp[g.slot]).then_inc(copied, 1)
                        if keeps:
                            groups(act, Q // B, NG, [(0, copy)])

                    @block.tensor
                    def _(pe):
                        pe.wait_ge(split, 1)
                        tiles_of = {}

                        def turn(g):
                            pe.wait_ge(made_s, g.at(1, 1))
                            pe.wait_ge(made_d, g.at(1, 1))
                            need(pe, copied, g.at(1, 1 - NG))
                            for b in range(B):
                                nc.tensor.transpose(tp[g.slot][:, b, :], hot_s[:, g.slot, b, :], identb[:])
                            for b in range(B):
                                mm = nc.tensor.transpose(tp[g.slot][:, B + b, :], hot_d[:, g.slot, b, :], identb[:])
                            mm.then_inc(turned, 1)

                        def look(g):
                            need(pe, taken, g.at(2, 2 - 2 * NG))
                            if keeps:
                                pe.wait_ge(copied, g.at(1, 1))
                            else:
                                pe.wait_ge(fetched[g.slot], g.lap(16, 16))
                            hold(pe)
                            o = lp[g.slot]
                            for b in range(B):
                                for n in range(3):
                                    nc.tensor.matmul(o[:, b * T * HEADS:(b + 1) * T * HEADS], lhsT=hotT[:, g.slot, b, :],
                                                     rhs=el3[:, n].rearrange("p t k -> p (t k)"), start=(n == 0), stop=(n == 2))
                            for b in range(B):
                                at = NL + b * 3 * HEADS
                                mm = nc.tensor.matmul(o[:, at:at + 3 * HEADS], lhsT=hotT[:, g.slot, B + b, :],
                                                      rhs=er3[:, bass.ds(tiles_of[g.slot * B + b], 1)]
                                                      .rearrange("p o n k -> p (o n k)"), start=True, stop=True)
                            mm.then_inc(looked, 1)
                        groups(pe, Q // B, NG, ([(0, turn)] if keeps else []) + [(1, look)],
                               pair_tiles("d", mybir.EngineType.PE, NG, tiles_of))

        def weights_of_edges(l, EL, ER, EX, EA, dist):
            with ExitStack() as scope:
                TE = sb(f"TE{l}", [QP, QB, HEADS, P], F32, scope)
                TK = sb(f"TK{l}", [QP, QB, P], F32, scope)
                pen = sb(f"pen{l}", [QP, QB, P + 1], F32, scope)
                S = sb(f"S{l}", [QP, QB, HEADS, P], F32, scope)
                ends = sb(f"ends{l}", [QP, QB, HEADS], F32, scope)
                LR = sb(f"LR{l}", [HEADS, Q], F32, scope)
                KF = sb(f"KF{l}", [HEADS, Q], F32, scope)
                KL = sb(f"KL{l}", [HEADS, Q], F32, scope)
                pl = sb(f"pl{l}", [HEADS, Q + 1], F32, scope)
                pls = sb(f"pls{l}", [HEADS, Q], F32, scope)
                plb = sb(f"plb{l}", [HEADS, Q], F32, scope)
                GR = sb(f"GR{l}", [HEADS, Q + 2], F32, scope)
                CR = sb(f"CR{l}", [HEADS, Q], F32, scope)
                cin = sb(f"cin{l}", [QP, QB, HEADS], F32, scope)
                MX = sb(f"MX{l}", [P, HEADS, Q], F32, scope)
                ts = sb(f"ts{l}", [P, HEADS, Q], F32, scope)
                z = sb(f"z{l}", [P, Q, HEADS], F32, scope)
                bk = [bank(f"wb{l}{n}", scope) for n in range(2)]
                r_up, r_down = sem(f"r_up{l}"), sem(f"r_down{l}")

                plan = []
                for b in range(QB):
                    plan.append([("T", (b, h), EL) for h in range(HEADS)])
                plan.append([("K", b, None) for b in range(QB)])
                plan.append([("F", b, None) for b in range(QB)])
                plan.append([("L", b, None) for b in range(QB)])
                for way in range(2):
                    plan.append([("E", b, None) for b in range(QB)])
                    plan.append([("C", b, None) for b in range(QB)])
                for h in range(HEADS):
                    plan.append([("M", (b, h), None) for b in range(QB)])

                with nc.Block() as block:
                    @block.tensor
                    def _(pe):
                        for n, work in enumerate(plan):
                            pe.wait_ge(r_down, n + 1)
                            o = bk[n % 2]
                            for what, k, _ in work:
                                if what == "T":
                                    mm = nc.tensor.transpose(o[0:QP, k[1] * P:(k[1] + 1) * P],
                                                             EL[:, k[0] * QP:(k[0] + 1) * QP, k[1]], ident[:])
                                elif what == "K":
                                    mm = nc.tensor.transpose(o[0:QP, k * P:(k + 1) * P], D_key[:, k * QP:(k + 1) * QP], ident[:])
                                elif what in "FL":
                                    e = 0 if what == "F" else P - 1
                                    mm = nc.tensor.matmul(o[0:HEADS, k * QP:(k + 1) * QP],
                                                          lhsT=TK[:, k, e:e + 1].to_broadcast([QP, HEADS]),
                                                          rhs=ident[0:QP, 0:QP], start=True, stop=True)
                                elif what == "E":
                                    mm = nc.tensor.transpose(o[0:HEADS, k * QP:(k + 1) * QP], ends[:, k, :], ident[0:QP, 0:QP])
                                elif what == "C":
                                    mm = nc.tensor.transpose(o[0:QP, k * HEADS:(k + 1) * HEADS], CR[:, k * QP:(k + 1) * QP],
                                                             ident[0:HEADS, 0:HEADS])
                                else:
                                    mm = nc.tensor.transpose(o[:, k[0] * QP:(k[0] + 1) * QP], TE[:, k[0], k[1], :],
                                                             ident[0:QP, 0:QP])
                            mm.then_inc(r_up, 1)

                    @block.vector
                    def _(dve):
                        link = dve_step.on(dve)
                        v = nc.vector
                        tt = v.tensor_tensor
                        done = [0]

                        def go():
                            dve.sem_inc(r_down, 1)

                        def got():
                            done[0] += 1
                            dve.wait_ge(r_up, done[0])
                            return bk[(done[0] - 1) % 2]

                        go()
                        go()
                        for b in range(QB):
                            o = got()
                            link(v.tensor_copy(TE[:, b].rearrange("p h e -> p (h e)"), o[0:QP, :]))
                            if b < QB - 1:
                                go()
                        link(v.tensor_copy(TK[:].rearrange("p b e -> p (b e)"), got()[0:QP, :]))
                        go()
                        link(v.tensor_copy(KF[:], got()[0:HEADS, 0:Q]))
                        go()
                        link(v.tensor_copy(KL[:], got()[0:HEADS, 0:Q]))
                        link(v.memset(pen[:], 0.0))
                        link(tt(pen[:, :, 1:P], TK[:, :, 1:P], TK[:, :, 0:P - 1], ALU.not_equal))
                        link(v.tensor_scalar(pen[:], pen[:], -BIG, None, ALU.mult))
                        link(v.memset(pl[:], 1.0))
                        link(tt(pl[:, 1:Q], KF[:, 1:Q], KL[:, 0:Q - 1], ALU.not_equal))
                        link(v.tensor_scalar(pl[:], pl[:], -BIG, None, ALU.mult))
                        link(tt(CR[:], KF[:], KL[:], ALU.not_equal))
                        link(v.tensor_scalar(CR[:], CR[:], -BIG, None, ALU.mult))
                        link(tt(pls[:], pl[:, 0:Q], CR[:], ALU.add))
                        link(tt(plb[:], pl[:, 1:Q + 1], CR[:], ALU.add))
                        link(v.memset(GR[:], -BIG))
                        for way in range(2):
                            for b in range(QB):
                                for h in range(HEADS):
                                    if way == 0:
                                        link.note(v.tensor_tensor_scan(S[:, b, h], pen[:, b, 0:P], TE[:, b, h], -BIG, ALU.add, ALU.max))
                                    else:
                                        link.note(v.tensor_tensor_scan(S[:, b, h, ::-1], pen[:, b, P:0:-1], TE[:, b, h, ::-1], -BIG,
                                                                       ALU.add, ALU.max))
                            link.settle()
                            link(v.tensor_copy(ends[:], S[:, :, :, P - 1 if way == 0 else 0]))
                            go()
                            link(v.tensor_copy(LR[:], got()[0:HEADS, 0:Q]))
                            if way == 0:
                                link(v.tensor_tensor_scan(GR[:, 1:Q + 1], pls[:], LR[:], -BIG, ALU.add, ALU.max))
                                link(tt(CR[:], GR[:, 0:Q], pl[:, 0:Q], ALU.add))
                            else:
                                link(v.tensor_tensor_scan(GR[:, Q:0:-1], plb[:, ::-1], LR[:, ::-1], -BIG, ALU.add, ALU.max))
                                link(tt(CR[:], GR[:, 2:Q + 2], pl[:, 1:Q + 1], ALU.add))
                            go()
                            link(v.tensor_copy(cin[:], got()[0:QP, 0:QB * HEADS].rearrange("p (b h) -> p b h", h=HEADS)))
                            for b in range(QB):
                                for h in range(HEADS):
                                    c = cin[:, b, h:h + 1]
                                    if way == 0:
                                        link.note(v.tensor_tensor_scan(TE[:, b, h], pen[:, b, 0:P], TE[:, b, h], c, ALU.add, ALU.max))
                                    else:
                                        link.note(v.tensor_tensor_scan(TE[:, b, h, ::-1], pen[:, b, P:0:-1], TE[:, b, h, ::-1], c,
                                                                       ALU.add, ALU.max))
                            link.settle()
                        go()
                        go()
                        for h in range(HEADS):
                            link(v.tensor_copy(MX[:, h], got()[:, 0:Q]))
                            if h < HEADS - 2:
                                go()
                        er = ER[:].rearrange("p q h -> p h q")
                        link(tt(MX[:], MX[:], er, ALU.add))
                        link(v.scalar_tensor_tensor(out=ts[:], in0=MX[:], scalar=0.2, in1=MX[:], op0=ALU.mult, op1=ALU.max))
                        link(tt(z[:], EL[:], ER[:], ALU.add))
                        link(v.scalar_tensor_tensor(out=z[:], in0=z[:], scalar=0.2, in1=z[:], op0=ALU.mult, op1=ALU.max))
                        link(tt(z[:], z[:], ts[:].rearrange("p h q -> p q h"), ALU.subtract))
                        dve.sem_inc(r_down, 1)
                        if dist:
                            dve.wait_ge(r_up, len(plan) + 1)
                            link(tt(EA[:], EX[:], bc(D_dist[:], HEADS), ALU.mult))

                    @block.scalar
                    def _(act):
                        act.wait_ge(r_down, len(plan) + 1)
                        nc.scalar.activation(EX[:], z[:], ACT.Exp).then_inc(r_up, 1)

        def gat_end(l, SUM):
            with ExitStack() as scope:
                den = sb(f"den{l}", [P, T, HEADS], F32, scope)
                st = sb(f"gst{l}", [P, T, 6], F32, scope)
                m = sb(f"gm{l}", [P, 5, T], F32, scope)
                R = sb(f"GR2{l}", [P, T, D], F32, scope)
                vec = sb(f"vec{l}", [P, 3, D], F32, scope)
                var_ready, rstd_ready, loaded, stats_ready, scaled = [
                    sem(f"{x}{l}") for x in ("gvar", "grstd", "gld", "gstats", "gscaled")]
                with nc.Block() as block:
                    @block.sync
                    def _(sp):
                        if l == 2:
                            for n, a in enumerate(("bias", "gamma", "beta")):
                                sp.dma_start(vec[:, n], row(A["L2_gnn_" + a])).then_inc(loaded, 16)

                    @block.scalar
                    def _(act):
                        if l == 2:
                            act.wait_ge(var_ready, 1)
                            nc.scalar.sqrt(m[:, 3], m[:, 3]).then_inc(rstd_ready, 1)
                            act.wait_ge(stats_ready, 1)
                            for t in range(T):
                                nc.scalar.activation(R[:, t], R[:, t], ACT.Identity, bias=m[:, 1, t:t + 1],
                                                     scale=m[:, 0, t:t + 1]).then_inc(scaled, 1)

                    @block.vector
                    def _(dve):
                        link = dve_step.on(dve)
                        tt = nc.vector.tensor_tensor
                        link(nc.vector.tensor_scalar(den[:], SUM[:, :, D:], 1e-9, None, ALU.max))
                        link(nc.vector.reciprocal(den[:], den[:]))
                        link(tt(R[:].rearrange("p t (h d) -> p t h d", h=HEADS),
                                SUM[:, :, 0:D].rearrange("p t (h d) -> p t h d", h=HEADS),
                                den[:].unsqueeze(3).to_broadcast([P, T, HEADS, D // HEADS]), ALU.mult))
                        if l == 2:
                            dve.wait_ge(loaded, 48)
                            link(tt(R[:], R[:], rows(vec[:, 0], T), ALU.add))
                            link(nc.vector.tensor_scalar(R[:], R[:], 0.0, None, ALU.max))
                            layernorm_stats(dve, link, st, m, var_ready, rstd_ready, R)
                            dve.sem_inc(stats_ready, 1)
                            for t in range(0, T, TB):
                                some = slice(t, t + TB)
                                dve.wait_ge(scaled, t + TB)
                                link(tt(R[:, some], R[:, some], rows(vec[:, 1], TB), ALU.mult))
                                link(tt(R[:, some], R[:, some], rows(vec[:, 2], TB), ALU.add))
                                link(tt(X[:, some], X[:, some], R[:, some], ALU.add))
                        else:
                            link(tt(X[:], X[:], R[:], ALU.add))

        if stop >= 5:
            free_sems()
            attend(2, A["L2_gnn_W"], A["L2_gnn_attn_l"].rearrange("h d -> (h d)"),
                   A["L2_gnn_attn_r"].rearrange("h d -> (h d)"), False)
        if stop >= 6:
            free_sems()
            attend(3, A["L3_gnn_W"], A["L3_gnn_w_att_src"].rearrange("o h d -> (o h d)"),
                   A["L3_gnn_w_att_dst"].rearrange("o h d -> (o h d)"), True)

        written = sem("written")
        with nc.Block() as block:
            @block.sync
            def _(sp):
                last = N - (T - 1) * P
                sp.dma_start(out[0:(T - 1) * P, :].rearrange("(t p) d -> p t d", p=P), X[:, 0:T - 1, :]).then_inc(written, 16)
                sp.dma_start(out[(T - 1) * P:N, :], X[0:last, T - 1, :]).then_inc(written, 16)
                sp.wait_ge(written, 32)


_INS = ['x', 'src', 'dst', 'edge_attr3_1x1', 'edge_attr_4', 'edge_attr_8', 'L0_gnn_W1', 'L0_gnn_b1', 'L0_gnn_W2',
        'L0_gnn_b2', 'L0_gnn_Wout', 'L0_gnn_bout', 'L1_gnn_w1_s', 'L1_gnn_w1_v', 'L1_gnn_wsc_s', 'L1_gnn_wsc_v',
        'L1_gnn_w2_s', 'L1_gnn_w2_v', 'L1_gnn_fc_w1', 'L1_gnn_fc_w2', 'L1_gnn_fc_w3', 'L1_gnn_g_s', 'L1_gnn_g_v',
        'L2_gnn_W', 'L2_gnn_attn_l', 'L2_gnn_attn_r', 'L2_gnn_bias', 'L2_gnn_gamma', 'L2_gnn_beta', 'L3_gnn_W',
        'L3_gnn_w_att_src', 'L3_gnn_w_att_dst']


def kernel(**inputs):
    import numpy as _np
    import concourse.bacc as _bacc
    from concourse import mybir as _mybir
    from concourse.bass_utils import run_bass_kernel_spmd as _run

    nc = _bacc.Bacc("TRN2", target_bir_lowering=False, num_devices=1)
    arrays, args = {}, {}
    for name in _INS:
        a = _np.ascontiguousarray(inputs[name])
        arrays[f"in_{name}_dram"] = a
        args[name] = nc.dram_tensor(f"in_{name}_dram", a.shape, _mybir.dt.from_np(a.dtype), kind="ExternalInput").ap()
    out = nc.dram_tensor("out_0_dram", (N, D), _mybir.dt.float32, kind="ExternalOutput").ap()
    gnn(nc, args, out)
    r = _run(nc, [arrays], core_ids=[0])
    return r.results[0]["out_0_dram"]
```
